# Optimizing a Trainium2 kernel written in Bass

```python
import numpy as np
import jax
import jax.numpy as jnp

def _softmax(x, axis=-1):
    return jax.nn.softmax(x, axis=axis)

def _gelu(x):
    return jax.nn.gelu(x, approximate=True)

def _silu(x):
    return jax.nn.silu(x)

def _sigmoid(x):
    return jax.nn.sigmoid(x)

def _layernorm(x, axis=-1, eps=1e-05):
    m = jnp.mean(x, axis=axis, keepdims=True)
    v = jnp.var(x, axis=axis, keepdims=True)
    return (x - m) / jnp.sqrt(v + eps)

def _scatter_add(tgt, idx, src, axis=0):
    return tgt.at[idx].add(src)

def _segment_sum(src, seg, n):
    return jax.ops.segment_sum(src, seg, n)
kernel_name = 'mk_sandwich_d4_jaxref_r8_a0a37c'

def setup_inputs(seed: int=0):
    np.random.seed(seed)
    _w = jnp.asarray

    def _L0_attn_setup():
        import jax, jax.numpy as jnp
        import numpy as np
        D_MODEL = 256
        N_HEADS = 16
        HEAD_DIM = D_MODEL // N_HEADS
        SCALE = HEAD_DIM ** (-0.5)
        key = jax.random.key(seed)
        ks = jax.random.split(key, 9)
        B, L, D = (4, 512, D_MODEL)
        s = 1.0 / np.sqrt(D)
        inp = {'x': jax.random.normal(ks[0], (B, L, D), dtype=jnp.float32)}
        inp['Wq'] = jax.random.normal(ks[1], (D, D), dtype=jnp.float32) * s
        inp['bq'] = jnp.zeros((D,), dtype=jnp.float32)
        inp['Wk'] = jax.random.normal(ks[2], (D, D), dtype=jnp.float32) * s
        inp['bk'] = jnp.zeros((D,), dtype=jnp.float32)
        inp['Wv'] = jax.random.normal(ks[3], (D, D), dtype=jnp.float32) * s
        inp['bv'] = jnp.zeros((D,), dtype=jnp.float32)
        inp['Wo'] = jax.random.normal(ks[4], (D, D), dtype=jnp.float32) * s
        inp['bo'] = jnp.zeros((D,), dtype=jnp.float32)
        return inp
    _L0_attn_in = _L0_attn_setup()

    def _L0_ffn_setup():
        import jax, jax.numpy as jnp
        import numpy as np
        BLOCK_SIZE = 32
        HIDDEN_SIZE = 256
        MLP_DIM = 2048
        NVFP4_LUT = jnp.array([0.0, 0.5, 1.0, 1.5, 2.0, 3.0, 4.0, 6.0, 0.0, -0.5, -1.0, -1.5, -2.0, -3.0, -4.0, -6.0], dtype=jnp.float32)

        def dequant_nvfp4(W_packed, scales, block=BLOCK_SIZE):
            N = W_packed.shape[0]
            low = W_packed & 15
            high = W_packed >> 4 & 15
            idx = jnp.stack([low, high], axis=-1).reshape(N, -1)
            vals = NVFP4_LUT[idx]
            K = vals.shape[1]
            vals = vals.reshape(N, K // block, block) * scales[:, :, None]
            return vals.reshape(N, K)
        key = jax.random.key(seed)
        ks = jax.random.split(key, 7)
        x = jax.random.normal(ks[0], (4, 32, HIDDEN_SIZE), dtype=jnp.float32)
        gate_W_packed = jax.random.randint(ks[1], (MLP_DIM, HIDDEN_SIZE // 2), 0, 32, dtype=jnp.int32)
        gate_scales = jax.random.uniform(ks[2], (MLP_DIM, HIDDEN_SIZE // BLOCK_SIZE), dtype=jnp.float32) * 0.1 + 0.001
        up_W_packed = jax.random.randint(ks[3], (MLP_DIM, HIDDEN_SIZE // 2), 0, 32, dtype=jnp.int32)
        up_scales = jax.random.uniform(ks[4], (MLP_DIM, HIDDEN_SIZE // BLOCK_SIZE), dtype=jnp.float32) * 0.1 + 0.001
        down_W_packed = jax.random.randint(ks[5], (HIDDEN_SIZE, MLP_DIM // 2), 0, 32, dtype=jnp.int32)
        down_scales = jax.random.uniform(ks[6], (HIDDEN_SIZE, MLP_DIM // BLOCK_SIZE), dtype=jnp.float32) * 0.1 + 0.001
        return {'x': x, 'gate_W_packed': gate_W_packed, 'gate_scales': gate_scales, 'up_W_packed': up_W_packed, 'up_scales': up_scales, 'down_W_packed': down_W_packed, 'down_scales': down_scales}
    _L0_ffn_in = _L0_ffn_setup()

    def _L1_attn_setup():
        import jax, jax.numpy as jnp
        import numpy as np
        B_, S_, E_ = (1, 256, 256)
        NH, P_, N_, G_, K_, CS = (64, 64, 128, 1, 4, 32)
        INTER = NH * P_
        CONV_DIM = INTER + 2 * G_ * N_
        PROJ = INTER + CONV_DIM + NH
        EPS = 1e-05

        def segsum(x):
            L = x.shape[-1]
            i = jnp.arange(L)
            strict = i[:, None] > i[None, :]
            X = jnp.where(strict, x[..., :, None], 0.0)
            S = jnp.cumsum(X, axis=-2)
            return jnp.where(i[:, None] >= i[None, :], S, -jnp.inf)
        key = jax.random.key(seed)
        ks = jax.random.split(key, 6)
        return {'input_states': jax.random.normal(ks[0], (B_, S_, E_), dtype=jnp.float32), 'mask': jnp.ones((B_, 1, S_), dtype=jnp.int32), 'W_in': jax.random.normal(ks[1], (PROJ, E_), dtype=jnp.float32) * 0.02, 'conv_w': jax.random.normal(ks[2], (CONV_DIM, K_), dtype=jnp.float32) * 0.2, 'conv_b': jnp.zeros((CONV_DIM,), dtype=jnp.float32), 'dt_bias': jnp.ones((NH,), dtype=jnp.float32), 'A_log': jnp.log(jnp.arange(1, NH + 1, dtype=jnp.float32)), 'D': jnp.ones((NH,), dtype=jnp.float32), 'norm_w': jnp.ones((INTER,), dtype=jnp.float32), 'W_out': jax.random.normal(ks[3], (E_, INTER), dtype=jnp.float32) * 0.02}
    _L1_attn_in = _L1_attn_setup()

    def _L1_ffn_setup():
        import jax, jax.numpy as jnp
        import numpy as np
        HIDDEN = 256
        INTER = 704
        B, S = (2, 256)

        def _ternary(key, shape):
            return jax.random.randint(key, shape, -1, 2).astype(jnp.float32)
        key = jax.random.key(seed)
        ks = jax.random.split(key, 7)
        x = jax.random.normal(ks[0], (B, S, HIDDEN), dtype=jnp.float32)
        gate_w = _ternary(ks[1], (INTER, HIDDEN))
        up_w = _ternary(ks[2], (INTER, HIDDEN))
        down_w = _ternary(ks[3], (HIDDEN, INTER))
        gate_s = jax.random.uniform(ks[4], (INTER,), minval=0.01, maxval=0.1, dtype=jnp.float32)
        up_s = jax.random.uniform(ks[5], (INTER,), minval=0.01, maxval=0.1, dtype=jnp.float32)
        down_s = jax.random.uniform(ks[6], (HIDDEN,), minval=0.01, maxval=0.1, dtype=jnp.float32)
        return {'x': x, 'gate_w': gate_w, 'up_w': up_w, 'down_w': down_w, 'gate_s': gate_s, 'up_s': up_s, 'down_s': down_s}
    _L1_ffn_in = _L1_ffn_setup()

    def _L2_attn_setup():
        import jax, jax.numpy as jnp
        import numpy as np
        B, S, DM = (2, 128, 256)
        H, HD, RD = (16, 128, 64)
        DQL, DKVL = (48, 64)
        THETA = 10000.0
        EPS = 1e-06

        def _rope_tables(seq, dim, theta):
            freqs = 1.0 / theta ** (jnp.arange(0, dim, 2, dtype=jnp.float32) / dim)
            t = jnp.arange(seq, dtype=jnp.float32)
            ang = jnp.outer(t, freqs)
            return (jnp.cos(ang), jnp.sin(ang))

        def _apply_rope(x, cos, sin):
            xr = x.reshape(x.shape[:-1] + (-1, 2))
            xe, xo = (xr[..., 0], xr[..., 1])
            c = cos[None, :, None, :]
            s = sin[None, :, None, :]
            return jnp.stack([xe * c - xo * s, xe * s + xo * c], axis=-1).reshape(x.shape)

        def _rmsnorm(x, w):
            return x * jax.lax.rsqrt(jnp.mean(x * x, axis=-1, keepdims=True) + EPS) * w

        def _reference_tuple_inner(x, Wq_down, q_norm_w, Wq_up, Wq_rope, Wkv_down, kv_norm_w, Wk_up, Wv_up, Wk_rope, Wout):
            b, s, _ = x.shape
            cos, sin = _rope_tables(s, RD, THETA)
            c_q = _rmsnorm(x @ Wq_down, q_norm_w)
            q = (c_q @ Wq_up).reshape(b, s, H, HD).transpose(0, 2, 1, 3)
            q_rope = _apply_rope((x @ Wq_rope).reshape(b, s, H, RD), cos, sin)
            q_rope = q_rope.transpose(0, 2, 1, 3)
            c_kv = _rmsnorm(x @ Wkv_down, kv_norm_w)
            k = (c_kv @ Wk_up).reshape(b, s, H, HD).transpose(0, 2, 1, 3)
            v = (c_kv @ Wv_up).reshape(b, s, H, HD).transpose(0, 2, 1, 3)
            k_rope = _apply_rope((x @ Wk_rope).reshape(b, s, H, RD), cos, sin)
            k_rope = k_rope.transpose(0, 2, 1, 3)
            scale = (HD + RD) ** (-0.5)
            scores = (jnp.einsum('bhqd,bhkd->bhqk', q, k) + jnp.einsum('bhqd,bhkd->bhqk', q_rope, k_rope)) * scale
            attn = jax.nn.softmax(scores, axis=-1)
            out = jnp.einsum('bhqk,bhkd->bhqd', attn, v)
            out = out.transpose(0, 2, 1, 3).reshape(b, s, H * HD) @ Wout
            return (out, attn)
        key = jax.random.key(seed)
        ks = jax.random.split(key, 9)
        sc = 0.02
        return {'x': jax.random.normal(ks[0], (B, S, DM), dtype=jnp.float32), 'Wq_down': jax.random.normal(ks[1], (DM, DQL), dtype=jnp.float32) * sc, 'q_norm_w': jnp.ones((DQL,), dtype=jnp.float32), 'Wq_up': jax.random.normal(ks[2], (DQL, H * HD), dtype=jnp.float32) * sc, 'Wq_rope': jax.random.normal(ks[3], (DM, H * RD), dtype=jnp.float32) * sc, 'Wkv_down': jax.random.normal(ks[4], (DM, DKVL), dtype=jnp.float32) * sc, 'kv_norm_w': jnp.ones((DKVL,), dtype=jnp.float32), 'Wk_up': jax.random.normal(ks[5], (DKVL, H * HD), dtype=jnp.float32) * sc, 'Wv_up': jax.random.normal(ks[6], (DKVL, H * HD), dtype=jnp.float32) * sc, 'Wk_rope': jax.random.normal(ks[7], (DM, H * RD), dtype=jnp.float32) * sc, 'Wout': jax.random.normal(ks[8], (H * HD, DM), dtype=jnp.float32) * sc}
    _L2_attn_in = _L2_attn_setup()

    def _L2_ffn_setup():
        import jax, jax.numpy as jnp
        import numpy as np
        key = jax.random.key(seed)
        k1, k2, k3, k4 = jax.random.split(key, 4)
        B, S, D_IN, D_OUT = (4, 512, 256, 256)
        x = jax.random.normal(k1, (B, S, D_IN), dtype=jnp.float32)
        weight = jax.random.normal(k2, (D_OUT, D_IN), dtype=jnp.float32) * 0.02
        scale_weight = jax.random.uniform(k3, (D_OUT,), dtype=jnp.float32, minval=0.5, maxval=1.5)
        bias = jax.random.normal(k4, (D_OUT,), dtype=jnp.float32) * 0.02
        return {'x': x, 'weight': weight, 'scale_weight': scale_weight, 'bias': bias}
    _L2_ffn_in = _L2_ffn_setup()

    def _L3_attn_setup():
        import jax, jax.numpy as jnp
        import numpy as np
        B, S, HID = (2, 256, 256)
        NK, NV, DK, DV = (16, 32, 128, 128)
        KCONV, CHUNK, EPS = (4, 64, 1e-06)
        KEY_DIM = NK * DK
        VAL_DIM = NV * DV
        CONV_DIM = 2 * KEY_DIM + VAL_DIM

        def _forward(x, W_qkv, W_z, W_b, W_a, W_out, conv_w, dt_bias, A_log, norm_w):
            Bs, Ss, _ = x.shape
            mixed = jnp.einsum('bsh,ch->bsc', x, W_qkv)
            z = jnp.einsum('bsh,vh->bsv', x, W_z)
            b = jnp.einsum('bsh,nh->bsn', x, W_b)
            a = jnp.einsum('bsh,nh->bsn', x, W_a)
            xp = jnp.pad(mixed, ((0, 0), (KCONV - 1, 0), (0, 0)))
            conv = sum((xp[:, k:k + Ss, :] * conv_w[:, k] for k in range(KCONV)))
            mixed = jax.nn.silu(conv)
            q, k, v = jnp.split(mixed, [KEY_DIM, 2 * KEY_DIM], axis=-1)
            q = q.reshape(Bs, Ss, NK, DK)
            k = k.reshape(Bs, Ss, NK, DK)
            v = v.reshape(Bs, Ss, NV, DV)
            rep = NV // NK
            q = jnp.repeat(q, rep, axis=2)
            k = jnp.repeat(k, rep, axis=2)
            beta = jax.nn.sigmoid(b)
            g = -jnp.exp(A_log) * jax.nn.softplus(a + dt_bias)
            l2n = lambda t: t / jnp.maximum(jnp.linalg.norm(t, axis=-1, keepdims=True), 1e-12)
            q, k = (l2n(q), l2n(k))
            qT = jnp.swapaxes(q, 1, 2) * DK ** (-0.5)
            kT = jnp.swapaxes(k, 1, 2)
            vT = jnp.swapaxes(v, 1, 2)
            bT = jnp.swapaxes(beta, 1, 2)
            gT = jnp.swapaxes(g, 1, 2)
            N = Ss // CHUNK
            qc = qT.reshape(Bs, NV, N, CHUNK, DK)
            kc = kT.reshape(Bs, NV, N, CHUNK, DK)
            vc = vT.reshape(Bs, NV, N, CHUNK, DV)
            bc = bT.reshape(Bs, NV, N, CHUNK)
            gc = jnp.cumsum(gT.reshape(Bs, NV, N, CHUNK), axis=-1)
            v_beta = vc * bc[..., None]
            k_beta = kc * bc[..., None]
            tril = jnp.tril(jnp.ones((CHUNK, CHUNK), bool))
            strict = jnp.tril(jnp.ones((CHUNK, CHUNK), bool), -1)
            diff = gc[..., :, None] - gc[..., None, :]
            decay = jnp.exp(jnp.where(tril, diff, 0.0)) * tril
            A = -(jnp.einsum('bhnid,bhnjd->bhnij', k_beta, kc) * decay) * strict
            eye = jnp.eye(CHUNK, dtype=A.dtype)
            Tm = jax.scipy.linalg.solve_triangular(eye - A, jnp.broadcast_to(eye, A.shape), lower=True, unit_diagonal=True)
            u = jnp.einsum('bhnij,bhnjv->bhniv', Tm, v_beta)
            kcd = jnp.einsum('bhnij,bhnjd->bhnid', Tm, k_beta * jnp.exp(gc)[..., None])
            front = lambda t: jnp.moveaxis(t, 2, 0)
            xs = (front(qc), front(kc), front(u), front(kcd), front(decay), front(gc))
            S0 = jnp.zeros((Bs, NV, DK, DV), jnp.float32)

            def step(St, inp):
                q_i, k_i, u_i, kcd_i, dec_i, g_i = inp
                attn = jnp.einsum('bhid,bhjd->bhij', q_i, k_i) * dec_i
                v_new = u_i - jnp.einsum('bhid,bhdv->bhiv', kcd_i, St)
                inter = jnp.einsum('bhid,bhdv->bhiv', q_i * jnp.exp(g_i)[..., None], St)
                out_i = inter + jnp.einsum('bhij,bhjv->bhiv', attn, v_new)
                g_last = g_i[..., -1]
                St_new = St * jnp.exp(g_last)[..., None, None] + jnp.einsum('bhid,bhiv->bhdv', k_i * jnp.exp(g_last[..., None] - g_i)[..., None], v_new)
                return (St_new, out_i)
            _, outs = jax.lax.scan(step, S0, xs)
            core = jnp.moveaxis(outs, 0, 2).reshape(Bs, NV, Ss, DV)
            core = jnp.swapaxes(core, 1, 2)
            zr = z.reshape(Bs, Ss, NV, DV)
            var = jnp.mean(core * core, axis=-1, keepdims=True)
            normed = core * jax.lax.rsqrt(var + EPS) * norm_w * jax.nn.silu(zr)
            return jnp.einsum('bsv,hv->bsh', normed.reshape(Bs, Ss, VAL_DIM), W_out)
        key = jax.random.key(seed)
        ks = jax.random.split(key, 10)
        n = lambda k, shape, s: jax.random.normal(k, shape, jnp.float32) * s
        return {'x': n(ks[0], (B, S, HID), 1.0), 'W_qkv': n(ks[1], (CONV_DIM, HID), HID ** (-0.5)), 'W_z': n(ks[2], (VAL_DIM, HID), HID ** (-0.5)), 'W_b': n(ks[3], (NV, HID), HID ** (-0.5)), 'W_a': n(ks[4], (NV, HID), HID ** (-0.5)), 'W_out': n(ks[5], (HID, VAL_DIM), VAL_DIM ** (-0.5)), 'conv_w': n(ks[6], (CONV_DIM, KCONV), 0.5), 'dt_bias': n(ks[7], (NV,), 0.5), 'A_log': n(ks[8], (NV,), 0.5), 'norm_w': jnp.ones((DV,), jnp.float32)}
    _L3_attn_in = _L3_attn_setup()

    def _L3_ffn_setup():
        import jax, jax.numpy as jnp
        import numpy as np
        TOP_K = 2
        NUM_EXPERTS = 8
        ROUTE_SCALE = 1.0
        key = jax.random.key(seed)
        ks = jax.random.split(key, 8)
        bs, slen, dim, hidden, E = (4, 128, 256, 128, NUM_EXPERTS)
        s = 0.02
        return {'x': jax.random.normal(ks[0], (bs, slen, dim), jnp.float32), 'gate_w': jax.random.normal(ks[1], (E, dim), jnp.float32) * s, 'w1': jax.random.normal(ks[2], (E, hidden, dim), jnp.float32) * s, 'w2': jax.random.normal(ks[3], (E, dim, hidden), jnp.float32) * s, 'w3': jax.random.normal(ks[4], (E, hidden, dim), jnp.float32) * s, 'ws1': jax.random.normal(ks[5], (hidden, dim), jnp.float32) * s, 'ws2': jax.random.normal(ks[6], (dim, hidden), jnp.float32) * s, 'ws3': jax.random.normal(ks[7], (hidden, dim), jnp.float32) * s}
    _L3_ffn_in = _L3_ffn_setup()
    _d = {'L0_attn_x': _L0_attn_in['x'], 'L0_attn_Wq': _L0_attn_in['Wq'], 'L0_attn_bq': _L0_attn_in['bq'], 'L0_attn_Wk': _L0_attn_in['Wk'], 'L0_attn_bk': _L0_attn_in['bk'], 'L0_attn_Wv': _L0_attn_in['Wv'], 'L0_attn_bv': _L0_attn_in['bv'], 'L0_attn_Wo': _L0_attn_in['Wo'], 'L0_attn_bo': _L0_attn_in['bo'], 'L0_ffn_gate_W_packed': _L0_ffn_in['gate_W_packed'], 'L0_ffn_gate_scales': _L0_ffn_in['gate_scales'], 'L0_ffn_up_W_packed': _L0_ffn_in['up_W_packed'], 'L0_ffn_up_scales': _L0_ffn_in['up_scales'], 'L0_ffn_down_W_packed': _L0_ffn_in['down_W_packed'], 'L0_ffn_down_scales': _L0_ffn_in['down_scales'], 'L1_attn_mask': _L1_attn_in['mask'], 'L1_attn_W_in': _L1_attn_in['W_in'], 'L1_attn_conv_w': _L1_attn_in['conv_w'], 'L1_attn_conv_b': _L1_attn_in['conv_b'], 'L1_attn_dt_bias': _L1_attn_in['dt_bias'], 'L1_attn_A_log': _L1_attn_in['A_log'], 'L1_attn_D': _L1_attn_in['D'], 'L1_attn_norm_w': _L1_attn_in['norm_w'], 'L1_attn_W_out': _L1_attn_in['W_out'], 'L1_ffn_gate_w': _L1_ffn_in['gate_w'], 'L1_ffn_up_w': _L1_ffn_in['up_w'], 'L1_ffn_down_w': _L1_ffn_in['down_w'], 'L1_ffn_gate_s': _L1_ffn_in['gate_s'], 'L1_ffn_up_s': _L1_ffn_in['up_s'], 'L1_ffn_down_s': _L1_ffn_in['down_s'], 'L2_attn_Wq_down': _L2_attn_in['Wq_down'], 'L2_attn_q_norm_w': _L2_attn_in['q_norm_w'], 'L2_attn_Wq_up': _L2_attn_in['Wq_up'], 'L2_attn_Wq_rope': _L2_attn_in['Wq_rope'], 'L2_attn_Wkv_down': _L2_attn_in['Wkv_down'], 'L2_attn_kv_norm_w': _L2_attn_in['kv_norm_w'], 'L2_attn_Wk_up': _L2_attn_in['Wk_up'], 'L2_attn_Wv_up': _L2_attn_in['Wv_up'], 'L2_attn_Wk_rope': _L2_attn_in['Wk_rope'], 'L2_attn_Wout': _L2_attn_in['Wout'], 'L2_ffn_weight': _L2_ffn_in['weight'], 'L2_ffn_scale_weight': _L2_ffn_in['scale_weight'], 'L2_ffn_bias': _L2_ffn_in['bias'], 'L3_attn_W_qkv': _L3_attn_in['W_qkv'], 'L3_attn_W_z': _L3_attn_in['W_z'], 'L3_attn_W_b': _L3_attn_in['W_b'], 'L3_attn_W_a': _L3_attn_in['W_a'], 'L3_attn_W_out': _L3_attn_in['W_out'], 'L3_attn_conv_w': _L3_attn_in['conv_w'], 'L3_attn_dt_bias': _L3_attn_in['dt_bias'], 'L3_attn_A_log': _L3_attn_in['A_log'], 'L3_attn_norm_w': _L3_attn_in['norm_w'], 'L3_ffn_gate_w': _L3_ffn_in['gate_w'], 'L3_ffn_w1': _L3_ffn_in['w1'], 'L3_ffn_w2': _L3_ffn_in['w2'], 'L3_ffn_w3': _L3_ffn_in['w3'], 'L3_ffn_ws1': _L3_ffn_in['ws1'], 'L3_ffn_ws2': _L3_ffn_in['ws2'], 'L3_ffn_ws3': _L3_ffn_in['ws3']}
    _x0 = _d['L0_attn_x']
    _d['L0_attn_x'] = jax.random.normal(jax.random.fold_in(jax.random.key(seed), 1), (1, 1024, 256), dtype=_x0.dtype)
    del _x0
    return _d

def reference(L0_attn_x, L0_attn_Wq, L0_attn_bq, L0_attn_Wk, L0_attn_bk, L0_attn_Wv, L0_attn_bv, L0_attn_Wo, L0_attn_bo, L0_ffn_gate_W_packed, L0_ffn_gate_scales, L0_ffn_up_W_packed, L0_ffn_up_scales, L0_ffn_down_W_packed, L0_ffn_down_scales, L1_attn_mask, L1_attn_W_in, L1_attn_conv_w, L1_attn_conv_b, L1_attn_dt_bias, L1_attn_A_log, L1_attn_D, L1_attn_norm_w, L1_attn_W_out, L1_ffn_gate_w, L1_ffn_up_w, L1_ffn_down_w, L1_ffn_gate_s, L1_ffn_up_s, L1_ffn_down_s, L2_attn_Wq_down, L2_attn_q_norm_w, L2_attn_Wq_up, L2_attn_Wq_rope, L2_attn_Wkv_down, L2_attn_kv_norm_w, L2_attn_Wk_up, L2_attn_Wv_up, L2_attn_Wk_rope, L2_attn_Wout, L2_ffn_weight, L2_ffn_scale_weight, L2_ffn_bias, L3_attn_W_qkv, L3_attn_W_z, L3_attn_W_b, L3_attn_W_a, L3_attn_W_out, L3_attn_conv_w, L3_attn_dt_bias, L3_attn_A_log, L3_attn_norm_w, L3_ffn_gate_w, L3_ffn_w1, L3_ffn_w2, L3_ffn_w3, L3_ffn_ws1, L3_ffn_ws2, L3_ffn_ws3):

    def _L0_attn_ref(x, Wq, bq, Wk, bk, Wv, bv, Wo, bo):
        import jax, jax.numpy as jnp
        import numpy as np
        D_MODEL = 256
        N_HEADS = 16
        HEAD_DIM = D_MODEL // N_HEADS
        SCALE = HEAD_DIM ** (-0.5)
        B, L, D = x.shape
        H, Hd = (N_HEADS, HEAD_DIM)
        q = jnp.einsum('bld,ed->ble', x, Wq) + bq
        k = jnp.einsum('bld,ed->ble', x, Wk) + bk
        v = jnp.einsum('bld,ed->ble', x, Wv) + bv
        phi_q = jax.nn.elu(q) + 1.0
        phi_k = jax.nn.elu(k) + 1.0
        phi_q = phi_q.reshape(B, L, H, Hd)
        phi_k = phi_k.reshape(B, L, H, Hd)
        v = v.reshape(B, L, H, Hd)
        kv_sum = jnp.cumsum(phi_k * v, axis=1)
        context = (phi_q * kv_sum).reshape(B, L, D) * SCALE
        return jnp.einsum('bld,ed->ble', context, Wo) + bo

    def _L0_ffn_ref(x, gate_W_packed, gate_scales, up_W_packed, up_scales, down_W_packed, down_scales):
        import jax, jax.numpy as jnp
        import numpy as np
        BLOCK_SIZE = 32
        HIDDEN_SIZE = 256
        MLP_DIM = 2048
        NVFP4_LUT = jnp.array([0.0, 0.5, 1.0, 1.5, 2.0, 3.0, 4.0, 6.0, 0.0, -0.5, -1.0, -1.5, -2.0, -3.0, -4.0, -6.0], dtype=jnp.float32)

        def dequant_nvfp4(W_packed, scales, block=BLOCK_SIZE):
            N = W_packed.shape[0]
            low = W_packed & 15
            high = W_packed >> 4 & 15
            idx = jnp.stack([low, high], axis=-1).reshape(N, -1)
            vals = NVFP4_LUT[idx]
            K = vals.shape[1]
            vals = vals.reshape(N, K // block, block) * scales[:, :, None]
            return vals.reshape(N, K)
        B, S, H = x.shape
        xt = x.reshape(B * S, H)
        Wg = dequant_nvfp4(gate_W_packed, gate_scales)
        Wu = dequant_nvfp4(up_W_packed, up_scales)
        Wd = dequant_nvfp4(down_W_packed, down_scales)
        gate = jnp.einsum('th,nh->tn', xt, Wg)
        up = jnp.einsum('th,nh->tn', xt, Wu)
        gelu = jnp.tanh(0.7978845608028654 * (gate + 0.044715 * gate ** 3)) * gate * 0.5 + gate * 0.5
        inter = gelu * up
        out = jnp.einsum('tn,hn->th', inter, Wd)
        return out.reshape(B, S, H)

    def _L1_attn_ref(input_states, mask, W_in, conv_w, conv_b, dt_bias, A_log, D, norm_w, W_out):
        import jax, jax.numpy as jnp
        import numpy as np
        B_, S_, E_ = (1, 256, 256)
        NH, P_, N_, G_, K_, CS = (64, 64, 128, 1, 4, 32)
        INTER = NH * P_
        CONV_DIM = INTER + 2 * G_ * N_
        PROJ = INTER + CONV_DIM + NH
        EPS = 1e-05

        def segsum(x):
            L = x.shape[-1]
            i = jnp.arange(L)
            strict = i[:, None] > i[None, :]
            X = jnp.where(strict, x[..., :, None], 0.0)
            S = jnp.cumsum(X, axis=-2)
            return jnp.where(i[:, None] >= i[None, :], S, -jnp.inf)
        B, S, E = input_states.shape
        proj = input_states @ W_in.T
        gate = proj[..., :INTER]
        h_BC = proj[..., INTER:INTER + CONV_DIM]
        dt = proj[..., INTER + CONV_DIM:]
        xpad = jnp.pad(h_BC, ((0, 0), (K_ - 1, 0), (0, 0)))
        conv = conv_b
        for i in range(K_):
            conv = conv + xpad[:, i:i + S, :] * conv_w[:, i]
        h_BC = jax.nn.silu(conv)
        hidden = h_BC[..., :INTER]
        Bm = h_BC[..., INTER:INTER + G_ * N_]
        Cm = h_BC[..., INTER + G_ * N_:]
        A = -jnp.exp(A_log)
        dt = jnp.clip(jax.nn.softplus(dt + dt_bias), 0.0)
        Hs = hidden.reshape(B, S, NH, P_).astype(jnp.float32)
        Bm = jnp.tile(Bm.reshape(B, S, G_, N_).astype(jnp.float32), (1, 1, NH // G_, 1))
        Cm = jnp.tile(Cm.reshape(B, S, G_, N_).astype(jnp.float32), (1, 1, NH // G_, 1))
        D_resid = D[None, None, :, None] * Hs
        Hdt = Hs * dt[..., None]
        At = A * dt
        C_ = S // CS
        Hc = Hdt.reshape(B, C_, CS, NH, P_)
        Ac = At.reshape(B, C_, CS, NH)
        Bc = Bm.reshape(B, C_, CS, NH, N_)
        Cc = Cm.reshape(B, C_, CS, NH, N_)
        Ap = jnp.transpose(Ac, (0, 3, 1, 2))
        A_cum = jnp.cumsum(Ap, axis=-1)
        L_tri = jnp.exp(segsum(Ap))
        Gm = jnp.einsum('bclhn,bcshn->bclsh', Cc, Bc)
        M = Gm * jnp.transpose(L_tri, (0, 2, 3, 4, 1))
        Yd = jnp.einsum('bclsh,bcshp->bclhp', M, Hc)
        decay = jnp.exp(A_cum[..., -1:] - A_cum)
        Bd = Bc * jnp.transpose(decay, (0, 2, 3, 1))[..., None]
        states = jnp.einsum('bclhn,bclhp->bchpn', Bd, Hc)
        Sd = jnp.transpose(jnp.exp(A_cum), (0, 2, 3, 1))
        Yoff = jnp.einsum('bclhn,bchpn->bclhp', Cc, states) * Sd[..., None]
        y = (Yd + Yoff).reshape(B, S, NH, P_) + D_resid
        y = y.reshape(B, S, INTER)
        yf = y.astype(jnp.float32) * jax.nn.silu(gate.astype(jnp.float32))
        var = jnp.mean(yf * yf, axis=-1, keepdims=True)
        yn = norm_w * (yf * jax.lax.rsqrt(var + EPS))
        return yn @ W_out.T

    def _L1_ffn_ref(x, gate_w, up_w, down_w, gate_s, up_s, down_s):
        import jax, jax.numpy as jnp
        import numpy as np
        HIDDEN = 256
        INTER = 704
        B, S = (2, 256)

        def _ternary(key, shape):
            return jax.random.randint(key, shape, -1, 2).astype(jnp.float32)
        b, s, h = x.shape
        xf = x.reshape(b * s, h)
        g = jnp.einsum('th,ih->ti', xf, gate_w) * gate_s
        u = jnp.einsum('th,ih->ti', xf, up_w) * up_s
        hdn = jax.nn.silu(g) * u
        out = jnp.einsum('ti,hi->th', hdn, down_w) * down_s
        return out.reshape(b, s, -1)

    def _L2_attn_ref(x, Wq_down, q_norm_w, Wq_up, Wq_rope, Wkv_down, kv_norm_w, Wk_up, Wv_up, Wk_rope, Wout):
        import jax, jax.numpy as jnp
        import numpy as np
        B, S, DM = (2, 128, 256)
        H, HD, RD = (16, 128, 64)
        DQL, DKVL = (48, 64)
        THETA = 10000.0
        EPS = 1e-06

        def _rope_tables(seq, dim, theta):
            freqs = 1.0 / theta ** (jnp.arange(0, dim, 2, dtype=jnp.float32) / dim)
            t = jnp.arange(seq, dtype=jnp.float32)
            ang = jnp.outer(t, freqs)
            return (jnp.cos(ang), jnp.sin(ang))

        def _apply_rope(x, cos, sin):
            xr = x.reshape(x.shape[:-1] + (-1, 2))
            xe, xo = (xr[..., 0], xr[..., 1])
            c = cos[None, :, None, :]
            s = sin[None, :, None, :]
            return jnp.stack([xe * c - xo * s, xe * s + xo * c], axis=-1).reshape(x.shape)

        def _rmsnorm(x, w):
            return x * jax.lax.rsqrt(jnp.mean(x * x, axis=-1, keepdims=True) + EPS) * w

        def _reference_tuple_inner(x, Wq_down, q_norm_w, Wq_up, Wq_rope, Wkv_down, kv_norm_w, Wk_up, Wv_up, Wk_rope, Wout):
            b, s, _ = x.shape
            cos, sin = _rope_tables(s, RD, THETA)
            c_q = _rmsnorm(x @ Wq_down, q_norm_w)
            q = (c_q @ Wq_up).reshape(b, s, H, HD).transpose(0, 2, 1, 3)
            q_rope = _apply_rope((x @ Wq_rope).reshape(b, s, H, RD), cos, sin)
            q_rope = q_rope.transpose(0, 2, 1, 3)
            c_kv = _rmsnorm(x @ Wkv_down, kv_norm_w)
            k = (c_kv @ Wk_up).reshape(b, s, H, HD).transpose(0, 2, 1, 3)
            v = (c_kv @ Wv_up).reshape(b, s, H, HD).transpose(0, 2, 1, 3)
            k_rope = _apply_rope((x @ Wk_rope).reshape(b, s, H, RD), cos, sin)
            k_rope = k_rope.transpose(0, 2, 1, 3)
            scale = (HD + RD) ** (-0.5)
            scores = (jnp.einsum('bhqd,bhkd->bhqk', q, k) + jnp.einsum('bhqd,bhkd->bhqk', q_rope, k_rope)) * scale
            attn = jax.nn.softmax(scores, axis=-1)
            out = jnp.einsum('bhqk,bhkd->bhqd', attn, v)
            out = out.transpose(0, 2, 1, 3).reshape(b, s, H * HD) @ Wout
            return (out, attn)
        return _reference_tuple_inner(x, Wq_down, q_norm_w, Wq_up, Wq_rope, Wkv_down, kv_norm_w, Wk_up, Wv_up, Wk_rope, Wout)[0]

    def _L2_ffn_ref(x, weight, scale_weight, bias):
        import jax, jax.numpy as jnp
        import numpy as np
        w = weight * scale_weight[:, None]
        out = jnp.einsum('bsi,oi->bso', x, w) + bias
        return out

    def _L3_attn_ref(x, W_qkv, W_z, W_b, W_a, W_out, conv_w, dt_bias, A_log, norm_w):
        import jax, jax.numpy as jnp
        import numpy as np
        B, S, HID = (2, 256, 256)
        NK, NV, DK, DV = (16, 32, 128, 128)
        KCONV, CHUNK, EPS = (4, 64, 1e-06)
        KEY_DIM = NK * DK
        VAL_DIM = NV * DV
        CONV_DIM = 2 * KEY_DIM + VAL_DIM

        def _forward(x, W_qkv, W_z, W_b, W_a, W_out, conv_w, dt_bias, A_log, norm_w):
            Bs, Ss, _ = x.shape
            mixed = jnp.einsum('bsh,ch->bsc', x, W_qkv)
            z = jnp.einsum('bsh,vh->bsv', x, W_z)
            b = jnp.einsum('bsh,nh->bsn', x, W_b)
            a = jnp.einsum('bsh,nh->bsn', x, W_a)
            xp = jnp.pad(mixed, ((0, 0), (KCONV - 1, 0), (0, 0)))
            conv = sum((xp[:, k:k + Ss, :] * conv_w[:, k] for k in range(KCONV)))
            mixed = jax.nn.silu(conv)
            q, k, v = jnp.split(mixed, [KEY_DIM, 2 * KEY_DIM], axis=-1)
            q = q.reshape(Bs, Ss, NK, DK)
            k = k.reshape(Bs, Ss, NK, DK)
            v = v.reshape(Bs, Ss, NV, DV)
            rep = NV // NK
            q = jnp.repeat(q, rep, axis=2)
            k = jnp.repeat(k, rep, axis=2)
            beta = jax.nn.sigmoid(b)
            g = -jnp.exp(A_log) * jax.nn.softplus(a + dt_bias)
            l2n = lambda t: t / jnp.maximum(jnp.linalg.norm(t, axis=-1, keepdims=True), 1e-12)
            q, k = (l2n(q), l2n(k))
            qT = jnp.swapaxes(q, 1, 2) * DK ** (-0.5)
            kT = jnp.swapaxes(k, 1, 2)
            vT = jnp.swapaxes(v, 1, 2)
            bT = jnp.swapaxes(beta, 1, 2)
            gT = jnp.swapaxes(g, 1, 2)
            N = Ss // CHUNK
            qc = qT.reshape(Bs, NV, N, CHUNK, DK)
            kc = kT.reshape(Bs, NV, N, CHUNK, DK)
            vc = vT.reshape(Bs, NV, N, CHUNK, DV)
            bc = bT.reshape(Bs, NV, N, CHUNK)
            gc = jnp.cumsum(gT.reshape(Bs, NV, N, CHUNK), axis=-1)
            v_beta = vc * bc[..., None]
            k_beta = kc * bc[..., None]
            tril = jnp.tril(jnp.ones((CHUNK, CHUNK), bool))
            strict = jnp.tril(jnp.ones((CHUNK, CHUNK), bool), -1)
            diff = gc[..., :, None] - gc[..., None, :]
            decay = jnp.exp(jnp.where(tril, diff, 0.0)) * tril
            A = -(jnp.einsum('bhnid,bhnjd->bhnij', k_beta, kc) * decay) * strict
            eye = jnp.eye(CHUNK, dtype=A.dtype)
            Tm = jax.scipy.linalg.solve_triangular(eye - A, jnp.broadcast_to(eye, A.shape), lower=True, unit_diagonal=True)
            u = jnp.einsum('bhnij,bhnjv->bhniv', Tm, v_beta)
            kcd = jnp.einsum('bhnij,bhnjd->bhnid', Tm, k_beta * jnp.exp(gc)[..., None])
            front = lambda t: jnp.moveaxis(t, 2, 0)
            xs = (front(qc), front(kc), front(u), front(kcd), front(decay), front(gc))
            S0 = jnp.zeros((Bs, NV, DK, DV), jnp.float32)

            def step(St, inp):
                q_i, k_i, u_i, kcd_i, dec_i, g_i = inp
                attn = jnp.einsum('bhid,bhjd->bhij', q_i, k_i) * dec_i
                v_new = u_i - jnp.einsum('bhid,bhdv->bhiv', kcd_i, St)
                inter = jnp.einsum('bhid,bhdv->bhiv', q_i * jnp.exp(g_i)[..., None], St)
                out_i = inter + jnp.einsum('bhij,bhjv->bhiv', attn, v_new)
                g_last = g_i[..., -1]
                St_new = St * jnp.exp(g_last)[..., None, None] + jnp.einsum('bhid,bhiv->bhdv', k_i * jnp.exp(g_last[..., None] - g_i)[..., None], v_new)
                return (St_new, out_i)
            _, outs = jax.lax.scan(step, S0, xs)
            core = jnp.moveaxis(outs, 0, 2).reshape(Bs, NV, Ss, DV)
            core = jnp.swapaxes(core, 1, 2)
            zr = z.reshape(Bs, Ss, NV, DV)
            var = jnp.mean(core * core, axis=-1, keepdims=True)
            normed = core * jax.lax.rsqrt(var + EPS) * norm_w * jax.nn.silu(zr)
            return jnp.einsum('bsv,hv->bsh', normed.reshape(Bs, Ss, VAL_DIM), W_out)
        return _forward(x, W_qkv, W_z, W_b, W_a, W_out, conv_w, dt_bias, A_log, norm_w)

    def _L3_ffn_ref(x, gate_w, w1, w2, w3, ws1, ws2, ws3):
        import jax, jax.numpy as jnp
        import numpy as np
        TOP_K = 2
        NUM_EXPERTS = 8
        ROUTE_SCALE = 1.0
        bs, slen, dim = x.shape
        xf = x.reshape(-1, dim)
        logits = (xf @ gate_w.T).astype(jnp.float32)
        scores = jax.nn.sigmoid(logits)
        top_scores, sel_idx = jax.lax.top_k(scores, TOP_K)
        top_scores = top_scores * ROUTE_SCALE
        routed = jnp.zeros_like(xf)
        for k in range(TOP_K):
            xs = xf * top_scores[:, k][:, None]
            h1 = jnp.einsum('td,ehd->teh', xs, w1)
            h3 = jnp.einsum('td,ehd->teh', xs, w3)
            h = jax.nn.silu(h1) * h3
            onehot = jax.nn.one_hot(sel_idx[:, k], NUM_EXPERTS, dtype=h.dtype)
            routed = routed + jnp.einsum('teh,te,edh->td', h, onehot, w2)
        shared = jax.nn.silu(xf @ ws1.T) * (xf @ ws3.T) @ ws2.T
        out = (shared + routed).reshape(bs, slen, dim)
        return out
    x = L0_attn_x
    x = x + _layernorm(_L0_attn_ref(_layernorm(x, axis=-1), L0_attn_Wq, L0_attn_bq, L0_attn_Wk, L0_attn_bk, L0_attn_Wv, L0_attn_bv, L0_attn_Wo, L0_attn_bo), axis=-1)
    x = x + _layernorm(_L0_ffn_ref(_layernorm(x, axis=-1), L0_ffn_gate_W_packed, L0_ffn_gate_scales, L0_ffn_up_W_packed, L0_ffn_up_scales, L0_ffn_down_W_packed, L0_ffn_down_scales), axis=-1)
    x = x + _layernorm(_L1_attn_ref(_layernorm(x, axis=-1), L1_attn_mask, L1_attn_W_in, L1_attn_conv_w, L1_attn_conv_b, L1_attn_dt_bias, L1_attn_A_log, L1_attn_D, L1_attn_norm_w, L1_attn_W_out), axis=-1)
    x = x + _layernorm(_L1_ffn_ref(_layernorm(x, axis=-1), L1_ffn_gate_w, L1_ffn_up_w, L1_ffn_down_w, L1_ffn_gate_s, L1_ffn_up_s, L1_ffn_down_s), axis=-1)
    x = x + _layernorm(_L2_attn_ref(_layernorm(x, axis=-1), L2_attn_Wq_down, L2_attn_q_norm_w, L2_attn_Wq_up, L2_attn_Wq_rope, L2_attn_Wkv_down, L2_attn_kv_norm_w, L2_attn_Wk_up, L2_attn_Wv_up, L2_attn_Wk_rope, L2_attn_Wout), axis=-1)
    x = x + _layernorm(_L2_ffn_ref(_layernorm(x, axis=-1), L2_ffn_weight, L2_ffn_scale_weight, L2_ffn_bias), axis=-1)
    x = x + _layernorm(_L3_attn_ref(_layernorm(x, axis=-1), L3_attn_W_qkv, L3_attn_W_z, L3_attn_W_b, L3_attn_W_a, L3_attn_W_out, L3_attn_conv_w, L3_attn_dt_bias, L3_attn_A_log, L3_attn_norm_w), axis=-1)
    x = x + _layernorm(_L3_ffn_ref(_layernorm(x, axis=-1), L3_ffn_gate_w, L3_ffn_w1, L3_ffn_w2, L3_ffn_w3, L3_ffn_ws1, L3_ffn_ws2, L3_ffn_ws3), axis=-1)
    return x

_drawn_inputs = setup_inputs


def setup_inputs(seed=0):
    import zlib

    import numpy as np

    out = dict(_drawn_inputs(seed))
    spreads = {'L0_attn_bq': (0.0, 0.1),
     'L0_attn_bk': (0.0, 0.1),
     'L0_attn_bv': (0.0, 0.1),
     'L0_attn_bo': (0.0, 0.438),
     'L1_attn_conv_b': (0.0, 0.1),
     'L1_attn_dt_bias': (1.0, 0.6),
     'L1_attn_D': (1.0, 0.2),
     'L1_attn_norm_w': (1.0, 0.2),
     'L2_attn_q_norm_w': (1.0, 0.6),
     'L2_attn_kv_norm_w': (1.0, 0.2),
     'L3_attn_norm_w': (1.0, 0.2)}
    factors = {'L1_attn_A_log': 8.0,
     'L2_attn_Wq_down': 8.0,
     'L2_attn_Wq_up': 8.0,
     'L2_attn_Wq_rope': 8.0,
     'L2_attn_Wk_up': 8.0,
     'L2_attn_Wk_rope': 8.0}
    for name, (base, spread) in spreads.items():
        noise = np.random.default_rng([zlib.crc32(name.encode()), seed]).standard_normal(out[name].shape)
        drawn = base * np.exp(spread * noise) if base else spread * noise
        out[name] = jnp.asarray(drawn.astype(out[name].dtype))
    for name, factor in factors.items():
        out[name] = (out[name] * factor).astype(out[name].dtype)
    return out
```

```python
from contextlib import ExitStack

import numpy as np
import concourse.bass as bass
from concourse import mybir

F32 = mybir.dt.float32
BF16 = mybir.dt.bfloat16
I32 = mybir.dt.int32
ALU = mybir.AluOpType
ACT = mybir.ActivationFunctionType
AX = mybir.AxisListType

P = 128
S = 1024
D = 256
TT = S // P
KC = D // P
HALF = 512
NH2 = S // HALF
LN_EPS = 1e-5


def half(h):
    return slice(h * HALF, (h + 1) * HALF)


def tile(t):
    return slice(t * P, (t + 1) * P)


class Shared:
    pass


class Scope:

    def __init__(self, nc, ctx, tag):
        self.nc, self.ctx, self.tag, self.sems = nc, ctx, tag, []
        ctx.callback(self.clear)

    def clear(self):
        if self.sems:
            self.nc.clear_and_free_semaphores(self.sems)
            self.nc.all_engine_barrier()

    def sb(self, name, shape, dt=F32):
        return self.ctx.enter_context(self.nc.sbuf_tensor(f"{self.tag}_{name}", shape, dt))

    def ps(self, name, shape, dt=F32):
        return self.ctx.enter_context(self.nc.psum_tensor(f"{self.tag}_{name}", shape, dt))

    def sem(self, name):
        self.sems.append(self.nc.alloc_semaphore(f"{self.tag}_{name}"))
        return self.sems[-1]


def start_block(nc, g, x_dram):
    with ExitStack() as ctx:
        m = Scope(nc, ctx, "start")
        x_in, blank, made = m.sem("x_in"), m.sem("blank"), m.sem("made")
        block = ctx.enter_context(nc.Block())

        @block.sync
        def _(sp):
            sp.dma_start(g.x[:], x_dram[0].rearrange("(t p) d -> p t d", p=P)).then_inc(x_in, 16)
            sp.wait_ge(x_in, 16)

        @block.gpsimd
        def _(pool):
            nc.gpsimd.memset(g.ident[:], 0.0).then_inc(blank, 1)
            pool.wait_ge(blank, 1)
            nc.gpsimd.affine_select(out=g.ident[:], in_=g.ident[:], compare_op=ALU.not_equal, fill=1.0,
                                    base=0, pattern=[[-1, P]], channel_multiplier=1).then_inc(made, 1)

        @block.vector
        def _(dve):
            nc.vector.memset(g.zero[:], 0.0)
            nc.vector.memset(g.ones[:], 1.0)


def residual_block(nc, g, tag, post=True, pre=True, token_scale=None, out=None):
    with ExitStack() as ctx:
        m = Scope(nc, ctx, tag)
        y_ps = m.ps("y_ps", [P, TT, D])
        xn_ps = m.ps("xn_ps", [P, KC, S])
        stats = m.sb("stats", [P, 2, TT, 6])
        mv = m.sb("mv", [P, 2, TT, 2])
        var = m.sb("var", [P, 2, TT])
        sd = m.sb("sd", [P, 2, TT])
        rstd = m.sb("rstd", [P, 2, TT])
        shift = m.sb("shift", [P, 2, TT])
        eps = m.sb("eps", [P, 1])
        z = m.sb("z", [P, TT, D])
        xn = m.sb("xn", [P, TT, D])
        y_turned, z_ready, x_added = m.sem("y_turned"), m.sem("z_ready"), m.sem("x_added")
        small = [m.sem("small_post"), m.sem("small_pre")]
        got_sd, scaled = m.sem("got_sd"), m.sem("scaled")
        xn_ready, xn_turned, stored = m.sem("xn_ready"), m.sem("xn_turned"), m.sem("stored")
        eps_set = m.sem("eps_set")
        block = ctx.enter_context(nc.Block())

        @block.tensor
        def _(pe):
            if post:
                for t in range(TT):
                    for c in range(KC):
                        last = nc.tensor.transpose(y_ps[:, t, c * P:(c + 1) * P], g.yT[:, c, tile(t)], g.ident[:])
                    last.then_inc(y_turned, 1)
            if pre:
                for t in range(TT):
                    pe.wait_ge(xn_ready, t + 1)
                    for c in range(KC):
                        last = nc.tensor.transpose(xn_ps[:, c, tile(t)], xn[:, t, c:D:KC], g.ident[:])
                    last.then_inc(xn_turned, 1)

        def normalise(dve, n, source, source_ready):
            for t in range(TT):
                if source_ready is not None:
                    dve.wait_ge(source_ready, t + 2 - t % 2)
                nc.vector.bn_stats(stats[:, n, t, :], source[:, t, :]).then_inc(small[n], 1)
            dve.wait_ge(small[n], TT)
            for t in range(TT):
                nc.vector.bn_aggr(mv[:, n, t, :], stats[:, n, t, :]).then_inc(small[n], 1)
            dve.wait_ge(small[n], 2 * TT)
            base = 2 * TT
            if n == 0 and token_scale is not None:
                nc.vector.tensor_tensor(var[:, n, :], mv[:, n, :, 1], token_scale[:], ALU.mult).then_inc(small[n], 1)
                dve.wait_ge(small[n], base + 1)
                nc.vector.tensor_tensor(var[:, n, :], var[:, n, :], token_scale[:], ALU.mult).then_inc(small[n], 1)
            else:
                nc.vector.tensor_copy(var[:, n, :], mv[:, n, :, 1]).then_inc(small[n], 2)
            dve.wait_ge(got_sd, n + (1 if post or n == 0 else 0))
            nc.vector.reciprocal(rstd[:, n, :], sd[:, n, :]).then_inc(small[n], 1)
            dve.wait_ge(small[n], base + 3)
            if n == 0 and token_scale is not None:
                nc.vector.tensor_tensor(rstd[:, n, :], rstd[:, n, :], token_scale[:], ALU.mult).then_inc(small[n], 1)
                dve.wait_ge(small[n], base + 4)
            nc.vector.scalar_tensor_tensor(out=shift[:, n, :], in0=mv[:, n, :, 0], scalar=-1.0,
                                           in1=rstd[:, n, :], op0=ALU.mult, op1=ALU.mult).then_inc(scaled, 1)

        @block.vector
        def _(dve):
            nc.vector.memset(eps[:], LN_EPS).then_inc(eps_set, 1)
            if post:
                normalise(dve, 0, y_ps, y_turned)
                for t in range(TT):
                    dve.wait_ge(z_ready, t + 1)
                    nc.vector.tensor_tensor(g.x[:, t, :], g.x[:, t, :], z[:, t, :], ALU.add).then_inc(x_added, 1)
            if pre:
                normalise(dve, 1, g.x, x_added if post else None)
                dve.wait_ge(scaled, 1 + post)
                for t in range(TT):
                    nc.vector.tensor_scalar(xn[:, t, :], g.x[:, t, :], rstd[:, 1, t:t + 1], shift[:, 1, t:t + 1],
                                            ALU.mult, ALU.add).then_inc(xn_ready, 1)
                dve.wait_ge(xn_turned, TT)
                nc.vector.tensor_copy(g.xnT[:, 1, :], xn_ps[:, 1, :])

        @block.scalar
        def _(act):
            act.wait_ge(eps_set, 1)
            for n, wanted in ((0, post), (1, pre)):
                if not wanted:
                    continue
                act.wait_ge(small[n], 2 * TT + 2)
                nc.scalar.activation(sd[:, n, :], var[:, n, :], ACT.Sqrt, bias=eps[:, 0:1]).then_inc(got_sd, 1)
                if n == 0:
                    act.wait_ge(scaled, 1)
                    for t in range(TT):
                        nc.scalar.activation(z[:, t, :], y_ps[:, t, :], ACT.Identity, bias=shift[:, 0, t:t + 1],
                                             scale=rstd[:, 0, t:t + 1]).then_inc(z_ready, 1)
            if pre:
                act.wait_ge(xn_turned, TT)
                nc.scalar.activation(g.xnT[:, 0, :], xn_ps[:, 0, :], ACT.Copy)

        @block.sync
        def _(sp):
            if out is not None:
                sp.wait_ge(x_added, TT)
                sp.dma_start(out[0].rearrange("(t p) d -> p t d", p=P), g.x[:]).then_inc(stored, 16)
                sp.wait_ge(stored, 16)


def open_sums(nc, g, bank):
    return nc.tensor.matmul(bank, g.zero[:, 0:P], g.zero[:], start=True, stop=True, skip_group_check=True)


def linear_attention_block(nc, g, tag, w_dram, b_dram, head_dim):
    scale = float(head_dim) ** -0.5
    with ExitStack() as ctx:
        m = Scope(nc, ctx, tag)
        w = m.sb("w", [P, 4, KC, D])
        b = m.sb("b", [P, 4, KC])
        qkv_ps = m.ps("qkv_ps", [P, 3, S])
        y_ps = m.ps("y_ps", [P, S])
        low, ex, high, phi = (m.sb(n, [P, 2, S]) for n in ("low", "ex", "high", "phi"))
        kv, total = m.sb("kv", [P, S]), m.sb("total", [P, S])
        ones = m.sb("ones", [P, S])
        context = m.sb("context", [P, KC, S])
        w_in, b_in = m.sem("w_in"), m.sem("b_in")
        projected, low_ready, ex_ready, step = m.sem("projected"), m.sem("low_ready"), m.sem("ex_ready"), m.sem("step")
        ctx_ready, y_ready, y_used = m.sem("ctx_ready"), m.sem("y_ready"), m.sem("y_used")
        block = ctx.enter_context(nc.Block())
        STEPS = 7

        @block.sync
        def _(sp):
            sp.dma_start(b[:], b_dram).then_inc(b_in, 16)
            sp.dma_start(w[:], w_dram).then_inc(w_in, 16)

        @block.tensor
        def _(pe):
            pe.wait_ge(w_in, 16)
            for f in range(KC):
                if f:
                    pe.wait_ge(ctx_ready, f)
                for n in range(3):
                    for h in range(NH2):
                        for c in range(KC):
                            last = nc.tensor.matmul(qkv_ps[:, n, half(h)], w[:, n, c, tile(f)], g.xnT[:, c, half(h)],
                                                    start=(c == 0), stop=(c == KC - 1))
                    last.then_inc(projected, 1)
            pe.wait_ge(ctx_ready, KC)
            for o in range(KC):
                out = y_ps if o == 0 else qkv_ps[:, 0, :]
                for h in range(NH2):
                    for c in range(KC):
                        last = nc.tensor.matmul(out[:, half(h)], w[:, 3, c, tile(o)], context[:, c, half(h)],
                                                start=(c == 0), stop=(c == KC - 1))
                last.then_inc(y_ready, 1)

        @block.vector
        def _(dve):
            nc.vector.memset(ones[:], 1.0).then_inc(step, 1)
            dve.wait_ge(b_in, 16)
            for f in range(KC):
                for n in range(2):
                    dve.wait_ge(projected, 3 * f + n + 1)
                    if f:
                        dve.wait_ge(ex_ready, 2 * f)
                    nc.vector.tensor_scalar(low[:, n, :], qkv_ps[:, n, :], b[:, n, f:f + 1], 0.0,
                                            ALU.add, ALU.min).then_inc(low_ready, 1)
                    nc.vector.tensor_scalar(high[:, n, :], qkv_ps[:, n, :], b[:, n, f:f + 1], 0.0,
                                            ALU.add, ALU.max).then_inc(step, 1)
                done = 1 + STEPS * f + 2
                for n in range(2):
                    dve.wait_ge(ex_ready, 2 * f + n + 1)
                    dve.wait_ge(step, done)
                    nc.vector.tensor_tensor(phi[:, n, :], high[:, n, :], ex[:, n, :], ALU.add).then_inc(step, 1)
                dve.wait_ge(projected, 3 * f + 3)
                dve.wait_ge(step, done + 2)
                nc.vector.scalar_tensor_tensor(out=kv[:], in0=qkv_ps[:, 2, :], scalar=b[:, 2, f:f + 1],
                                               in1=phi[:, 1, :], op0=ALU.add, op1=ALU.mult).then_inc(step, 1)
                dve.wait_ge(step, done + 3)
                nc.vector.tensor_tensor_scan(total[:], ones[:], kv[:], 0.0, ALU.mult, ALU.add).then_inc(step, 1)
                dve.wait_ge(step, done + 4)
                nc.vector.scalar_tensor_tensor(out=context[:, f, :], in0=total[:], scalar=scale, in1=phi[:, 0, :],
                                               op0=ALU.mult, op1=ALU.mult).then_inc(ctx_ready, 1)
                dve.wait_ge(ctx_ready, f + 1)
                dve.sem_inc(step, 1)

        @block.scalar
        def _(act):
            for f in range(KC):
                for n in range(2):
                    act.wait_ge(low_ready, 2 * f + n + 1)
                    if f:
                        act.wait_ge(step, 1 + STEPS * (f - 1) + 4)
                    nc.scalar.activation(ex[:, n, :], low[:, n, :], ACT.Exp).then_inc(ex_ready, 1)
            act.wait_ge(b_in, 16)
            for o in range(KC):
                act.wait_ge(y_ready, o + 1)
                out = y_ps if o == 0 else qkv_ps[:, 0, :]
                nc.scalar.activation(g.yT[:, o, :], out[:, :], ACT.Identity, bias=b[:, 3, o:o + 1])


def linear_block(nc, g, tag, w_dram, sb_dram):
    with ExitStack() as ctx:
        m = Scope(nc, ctx, tag)
        w = m.sb("w", [P, KC, D])
        sb_ = m.sb("sb", [P, 2, KC])
        y_ps = m.ps("y_ps", [P, KC, S])
        w_in, s_in, y_ready = m.sem("w_in"), m.sem("s_in"), m.sem("y_ready")
        block = ctx.enter_context(nc.Block())

        @block.sync
        def _(sp):
            sp.dma_start(w[:], w_dram).then_inc(w_in, 16)
            sp.dma_start(sb_[:], sb_dram).then_inc(s_in, 16)

        @block.tensor
        def _(pe):
            pe.wait_ge(w_in, 16)
            for o in range(KC):
                for h in range(NH2):
                    for c in range(KC):
                        last = nc.tensor.matmul(y_ps[:, o, half(h)], w[:, c, tile(o)], g.xnT[:, c, half(h)],
                                                start=(c == 0), stop=(c == KC - 1))
                last.then_inc(y_ready, 1)

        @block.scalar
        def _(act):
            act.wait_ge(s_in, 16)
            for o in range(KC):
                act.wait_ge(y_ready, o + 1)
                nc.scalar.activation(g.yT[:, o, :], y_ps[:, o, :], ACT.Identity, bias=sb_[:, 1, o:o + 1],
                                     scale=sb_[:, 0, o:o + 1])


FP4, TERNARY, EXPERTS = "fp4", "ternary", "experts"


def gated_ffn_block(nc, g, tag, kind, loops, ring, w_dram, extra_dram):
    U = NH2 * ring
    NV = 6 * P
    pairs = ring // 2
    with ExitStack() as ctx:
        m = Scope(nc, ctx, tag)
        y_ps = m.ps("y_ps", [P, KC, NH2, HALF])
        gate_ps = m.ps("gate_ps", [P, NH2, HALF])
        up_ps = m.ps("up_ps", [P, NH2, HALF])
        acted = m.sb("acted", [P, 2, HALF])
        inner = m.sb("inner", [P, 2, HALF])
        w_in = [m.sem(f"w_in{s}") for s in range(pairs if kind == FP4 else ring)]
        gu_ready, acted_ready, inner_ready = m.sem("gu_ready"), m.sem("acted_ready"), m.sem("inner_ready")
        down_done = m.sem("down_done")
        if kind == FP4:
            packed = m.sb("packed", [P, pairs, NV], I32)
            scales = m.sb("scales", [P, pairs, NV])
            mag = m.sb("mag", [P, 2, NV], I32)
            sign = m.sb("sign", [P, 2, NV], I32)
            t_low, t_high, t_sign = (m.sb(n, [P, 2, NV]) for n in ("t_low", "t_high", "t_sign"))
            wf = m.sb("wf", [P, pairs, 2, NV])
            s_in = [m.sem(f"s_in{s}") for s in range(pairs)]
            unpacked, w_made, w_used = m.sem("unpacked"), m.sem("w_made"), m.sem("w_used")

            def weight(s, what, c):
                if what == 2:
                    return wf[:, s // 2, s % 2, 4 * P + c * P:4 * P + (c + 1) * P]
                return wf[:, s // 2, c, (2 * what + s % 2) * P:(2 * what + s % 2 + 1) * P]
        else:
            wf = m.sb("wf", [P, ring, NV + 2])

            def weight(s, what, c):
                return wf[:, s, (2 * what + c) * P:(2 * what + c + 1) * P]
        if kind == TERNARY:
            out_scale = m.sb("out_scale", [P, KC])
            out_in = m.sem("out_in")
        if kind == EXPERTS:
            score = m.sb("score", [P, ring, S])
            scored = m.sb("scored", [P, 2, HALF])
            up_sb = m.sb("up_sb", [P, 2, HALF])
            e_in = [m.sem(f"e_in{s}") for s in range(ring)]
            scored_ready, up_ready = m.sem("scored_ready"), m.sem("up_ready")
        ps_freed = up_ready if kind == EXPERTS else inner_ready
        block = ctx.enter_context(nc.Block())

        @block.sync
        def _(sp):
            def load(i, s):
                if kind == FP4:
                    at = i * pairs + s
                    sp.dma_start(packed[:, s, :], w_dram[bass.ds(at, 1)].rearrange("a p n -> p (a n)")
                                 ).then_inc(w_in[s], 16)
                    src = extra_dram[bass.ds(at, 1)].rearrange("a b n -> (a b) n")
                    sp.dma_start(scales[:, s, :], src.unsqueeze(1).to_broadcast((8, 16, NV))).then_inc(s_in[s], 16)
                else:
                    at = i * ring + s
                    sp.dma_start(wf[:, s, :], w_dram[bass.ds(at, 1)].rearrange("a p n -> p (a n)")
                                 ).then_inc(w_in[s], 16)
                    if kind == EXPERTS:
                        sp.dma_start(score[:, s, :], extra_dram[bass.ds(at, 1), :].to_broadcast((P, S))
                                     ).then_inc(e_in[s], 16)

            for s in range(len(w_in)):
                load(0, s)
            if kind == TERNARY:
                sp.dma_start(out_scale[:], extra_dram).then_inc(out_in, 16)
            with sp.Fori(1, loops) as i:
                for s in range(len(w_in)):
                    if kind == FP4:
                        sp.wait_ge(w_made, i * pairs + (s + 1 - pairs))
                    else:
                        sp.wait_ge(down_done, i * U + (2 * s + 4 - U))
                    load(i, s)

        @block.tensor
        def _(pe):
            pe.sem_inc(down_done, 2)
            if kind == FP4:
                pe.sem_inc(w_used, pairs)
            for c in range(KC):
                for h in range(NH2):
                    open_sums(nc, g, y_ps[:, c, h, :])

            def gate_up(i, u):
                s, h = (u // NH2) % ring, u % NH2
                if h == 0:
                    if kind == FP4:
                        if s % 2 == 0:
                            pe.wait_ge(w_made, i * pairs + (u // 4 + 1))
                    else:
                        pe.wait_ge(w_in[s], i * 16 + 16 * (1 + u // U))
                pe.wait_ge(ps_freed, i * U + (u + 1))
                for what, ps in ((0, gate_ps), (1, up_ps)):
                    for c in range(KC):
                        last = nc.tensor.matmul(ps[:, h, :], weight(s, what, c), g.xnT[:, c, half(h)],
                                                start=(c == 0), stop=(c == KC - 1))
                last.then_inc(gu_ready, 1)

            def down(i, u):
                s, h = u // NH2, u % NH2
                pe.wait_ge(inner_ready, i * U + (u + (1 if kind == EXPERTS else 3)))
                for c in range(KC):
                    last = nc.tensor.matmul(y_ps[:, c, h, :], weight(s, 2, c), inner[:, u % 2, :],
                                            start=False, stop=True, skip_group_check=True)
                last.then_inc(down_done, 1)
                if kind == FP4 and u % 4 == 3:
                    pe.wait_ge(down_done, i * U + (u + 3))
                    pe.sem_inc(w_used, 1)

            gate_up(0, 0)
            with pe.Fori(0, loops - 1) as i:
                for u in range(U):
                    gate_up(i, u + 1)
                    down(i, u)
            for u in range(U):
                if u + 1 < U:
                    gate_up(loops - 1, u + 1)
                down(loops - 1, u)

        @block.scalar
        def _(act):
            if kind == TERNARY:
                act.wait_ge(out_in, 16)
            with act.Fori(0, loops) as i:
                for u in range(U):
                    s, h = u // NH2, u % NH2
                    if kind == EXPERTS:
                        act.wait_ge(scored_ready, i * U + (u + 1))
                        nc.scalar.activation(acted[:, u % 2, :], scored[:, u % 2, :], ACT.Silu).then_inc(acted_ready, 1)
                        continue
                    act.wait_ge(gu_ready, i * U + (u + 1))
                    if kind == FP4:
                        nc.scalar.activation(acted[:, u % 2, :], gate_ps[:, h, :], ACT.Gelu_apprx_tanh
                                             ).then_inc(acted_ready, 1)
                    else:
                        nc.scalar.activation(acted[:, u % 2, :], gate_ps[:, h, :], ACT.Silu,
                                             scale=wf[:, s, NV:NV + 1]).then_inc(acted_ready, 1)
            act.wait_ge(down_done, loops * U + 2)
            for c in range(KC):
                y = y_ps[:, c].rearrange("p h n -> p (h n)")
                if kind == TERNARY:
                    nc.scalar.activation(g.yT[:, c, :], y, ACT.Identity, scale=out_scale[:, c:c + 1])
                else:
                    nc.scalar.activation(g.yT[:, c, :], y, ACT.Copy)

        @block.vector
        def _(dve):
            dve.sem_inc(ps_freed, 2)

            def unpack(i, s, part):
                at = i * (pairs * 9) + s * 9
                if part == 0:
                    dve.wait_ge(w_in[s], i * 16 + 16)
                    for nib in range(2):
                        nc.vector.tensor_scalar(mag[:, nib, :], packed[:, s, :], 4 * nib, 7,
                                                ALU.logical_shift_right, ALU.bitwise_and).then_inc(unpacked, 1)
                        nc.vector.tensor_scalar(sign[:, nib, :], packed[:, s, :], 4 * nib, 8,
                                                ALU.logical_shift_right, ALU.bitwise_and).then_inc(unpacked, 1)
                if part == 1:
                    dve.wait_ge(unpacked, at + 4)
                    nc.vector.scalar_tensor_tensor(out=t_low[:], in0=mag[:], scalar=4.0, in1=mag[:],
                                                   op0=ALU.max, op1=ALU.add).then_inc(unpacked, 1)
                    nc.vector.tensor_scalar(t_high[:], mag[:], 6.0, 2.0, ALU.max, ALU.mult).then_inc(unpacked, 1)
                    nc.vector.tensor_scalar(t_sign[:], sign[:], -0.125, 0.5, ALU.mult, ALU.add).then_inc(unpacked, 1)
                if part == 2:
                    dve.wait_ge(unpacked, at + 7)
                    nc.vector.scalar_tensor_tensor(out=t_low[:], in0=t_low[:], scalar=-16.0, in1=t_high[:],
                                                   op0=ALU.add, op1=ALU.add).then_inc(unpacked, 1)
                    dve.wait_ge(unpacked, at + 8)
                    nc.vector.tensor_tensor(t_sign[:], t_sign[:], t_low[:], ALU.mult).then_inc(unpacked, 1)
                if part == 3:
                    dve.wait_ge(unpacked, at + 9)
                    dve.wait_ge(s_in[s], i * 16 + 16)
                    dve.wait_ge(w_used, i * pairs + (s + 1))
                    nc.vector.tensor_tensor(wf[:, s], t_sign[:], scales[:, s, :].unsqueeze(1).to_broadcast((P, 2, NV)),
                                            ALU.mult).then_inc(w_made, 1)

            def multiply(i, u):
                s, h = u // NH2, u % NH2
                at = i * U + (u + 1)
                if kind == EXPERTS:
                    dve.wait_ge(gu_ready, at)
                    if h == 0:
                        dve.wait_ge(e_in[s], i * 16 + 16)
                    nc.vector.tensor_tensor(scored[:, u % 2, :], gate_ps[:, h, :], score[:, s, half(h)],
                                            ALU.mult).then_inc(scored_ready, 1)
                    nc.vector.tensor_tensor(up_sb[:, u % 2, :], up_ps[:, h, :], score[:, s, half(h)],
                                            ALU.mult).then_inc(up_ready, 1)
                    dve.wait_ge(up_ready, i * U + (u + 3))
                dve.wait_ge(acted_ready, at)
                dve.wait_ge(down_done, at)
                if kind == TERNARY:
                    nc.vector.scalar_tensor_tensor(out=inner[:, u % 2, :], in0=up_ps[:, h, :],
                                                   scalar=wf[:, s, NV + 1:NV + 2], in1=acted[:, u % 2, :],
                                                   op0=ALU.mult, op1=ALU.mult).then_inc(inner_ready, 1)
                else:
                    up = up_sb[:, u % 2, :] if kind == EXPERTS else up_ps[:, h, :]
                    nc.vector.tensor_tensor(inner[:, u % 2, :], acted[:, u % 2, :], up, ALU.mult
                                            ).then_inc(inner_ready, 1)

            if kind == FP4:
                for part in range(4):
                    unpack(0, 0, part)
                with dve.Fori(0, loops - 1) as i:
                    for u in range(U):
                        multiply(i, u)
                        nxt = u // 4 + 1
                        unpack(i + nxt // pairs, nxt % pairs, u % 4)
                for u in range(U):
                    multiply(loops - 1, u)
                    if u // 4 + 1 < pairs:
                        unpack(loops - 1, u // 4 + 1, u % 4)
            else:
                with dve.Fori(0, loops) as i:
                    for u in range(U):
                        multiply(i, u)


EXP = 8
TOP = 2


def router_block(nc, g, tag, w_dram, score_dram):
    NE = EXP + 1
    with ExitStack() as ctx:
        m = Scope(nc, ctx, tag)
        w = m.sb("w", [P, KC, EXP])
        logit_ps = m.ps("logit_ps", [P, TT, EXP])
        turned_ps = m.ps("turned_ps", [NE, TT, P])
        score = m.sb("score", [P, TT, EXP])
        above = m.sb("above", [P, TT, EXP, EXP])
        tie = m.sb("tie", [P, TT, EXP, EXP])
        lower = m.sb("lower", [P, EXP, EXP])
        rank = m.sb("rank", [P, TT, EXP])
        chosen = m.sb("chosen", [P, TT, NE])
        rows = m.sb("rows", [NE, S])
        w_in, products, sig, low0, low1, step, turned, copied, stored = (
            m.sem(n) for n in ("w_in", "products", "sig", "low0", "low1", "step", "turned", "copied", "stored"))
        block = ctx.enter_context(nc.Block())

        @block.sync
        def _(sp):
            sp.dma_start(w[:], w_dram).then_inc(w_in, 16)
            sp.wait_ge(copied, 1)
            sp.dma_start(score_dram, rows[:]).then_inc(stored, 16)
            sp.wait_ge(stored, 16)

        @block.gpsimd
        def _(pool):
            nc.gpsimd.memset(lower[:], 1.0).then_inc(low0, 1)
            pool.wait_ge(low0, 1)
            nc.gpsimd.affine_select(out=lower[:], in_=lower[:], compare_op=ALU.is_gt, fill=0.0, base=0,
                                    pattern=[[1, EXP], [-1, EXP]], channel_multiplier=0).then_inc(low1, 1)

        @block.tensor
        def _(pe):
            pe.wait_ge(w_in, 16)
            for t in range(TT):
                for c in range(KC):
                    last = nc.tensor.matmul(logit_ps[:, t, :], g.xnT[:, c, tile(t)], w[:, c, :],
                                            start=(c == 0), stop=(c == KC - 1))
            last.then_inc(products, 1)
            pe.wait_ge(step, 7)
            for t in range(TT):
                last = nc.tensor.transpose(turned_ps[:, t, :], chosen[:, t, :], g.ident[:])
            last.then_inc(turned, 1)

        @block.scalar
        def _(act):
            act.wait_ge(products, 1)
            nc.scalar.activation(score[:], logit_ps[:], ACT.Sigmoid).then_inc(sig, 1)

        @block.vector
        def _(dve):
            nc.vector.memset(chosen[:], 1.0).then_inc(step, 1)
            dve.wait_ge(sig, 1)
            other = score[:].unsqueeze(2).to_broadcast((P, TT, EXP, EXP))
            own = score[:].unsqueeze(3).to_broadcast((P, TT, EXP, EXP))
            nc.vector.tensor_tensor(above[:], other, own, ALU.is_gt).then_inc(step, 1)
            nc.vector.tensor_tensor(tie[:], other, own, ALU.is_equal).then_inc(step, 1)
            dve.wait_ge(low1, 1)
            dve.wait_ge(step, 3)
            nc.vector.tensor_tensor(tie[:], tie[:], lower[:].unsqueeze(1).to_broadcast((P, TT, EXP, EXP)),
                                    ALU.mult).then_inc(step, 1)
            dve.wait_ge(step, 4)
            nc.vector.tensor_tensor(above[:], above[:], tie[:], ALU.add).then_inc(step, 1)
            dve.wait_ge(step, 5)
            nc.vector.tensor_reduce(rank[:], above[:], AX.X, ALU.add).then_inc(step, 1)
            dve.wait_ge(step, 6)
            nc.vector.scalar_tensor_tensor(out=chosen[:, :, 0:EXP], in0=rank[:], scalar=TOP - 0.5, in1=score[:],
                                           op0=ALU.is_lt, op1=ALU.mult).then_inc(step, 1)
            dve.wait_ge(turned, 1)
            nc.vector.tensor_copy(rows[:], turned_ps[:].rearrange("e t p -> e (t p)")).then_inc(copied, 1)


def project_out_block(nc, g, tag, hidden, blocks, w_dram):
    RING = 4
    with ExitStack() as ctx:
        m = Scope(nc, ctx, tag)
        w = m.sb("w", [P, RING, D])
        y_ps = m.ps("y_ps", [P, KC, NH2, HALF])
        w_in = [m.sem(f"w_in{s}") for s in range(RING)]
        block_done = m.sem("block_done")
        block = ctx.enter_context(nc.Block())

        @block.sync
        def _(sp):
            def load(i, s):
                sp.dma_start(w[:, s, :], w_dram[bass.ds(i * RING + s, 1)].rearrange("a p n -> p (a n)")
                             ).then_inc(w_in[s], 16)

            for s in range(RING):
                load(0, s)
            with sp.Fori(1, blocks // RING) as i:
                for s in range(RING):
                    sp.wait_ge(block_done, i * RING + (s + 1 - RING))
                    load(i, s)

        @block.tensor
        def _(pe):
            for c in range(KC):
                for h in range(NH2):
                    open_sums(nc, g, y_ps[:, c, h, :])
            with pe.Fori(0, blocks // RING) as i:
                for s in range(RING):
                    pe.wait_ge(w_in[s], i * 16 + 16)
                    for c in range(KC):
                        for h in range(NH2):
                            src = hidden[:, bass.ds(i * RING + s, 1), half(h)].rearrange("p a n -> p (a n)")
                            last = nc.tensor.matmul(y_ps[:, c, h, :], w[:, s, tile(c)], src, start=False, stop=True,
                                                    skip_group_check=True)
                    last.then_inc(block_done, 1)

        @block.scalar
        def _(act):
            act.wait_ge(block_done, blocks)
            nc.scalar.activation(g.yT[:], y_ps[:].rearrange("p c h n -> p c (h n)"), ACT.Copy)


HEADS, HEAD, ROPE = 16, 128, 64
QL, KVL = 48, 64
LAT_EPS = 1e-6
KV0 = 64


def latent_block(nc, g, tag, latT, lat, stack, w_dram, nw_dram):
    parts = ((0, QL), (KV0, KVL))
    with ExitStack() as ctx:
        m = Scope(nc, ctx, tag)
        w = m.sb("w", [P, KC, P])
        nw = m.sb("nw", [P, 2])
        lat_ps = m.ps("lat_ps", [P, TT, P])
        turned_ps = m.ps("turned_ps", [P, S])
        low_ps = m.ps("low_ps", [KVL, S])
        squares = m.sb("squares", [P, P])
        ssq, sd, rstd = (m.sb(n, [P, 2, TT]) for n in ("ssq", "sd", "rstd"))
        eps = m.sb("eps", [P, 1])
        w_in, nw_in, products, summed, rooted, step, scaled, turned = (
            m.sem(n) for n in ("w_in", "nw_in", "products", "summed", "rooted", "step", "scaled", "turned"))
        block = ctx.enter_context(nc.Block())

        @block.sync
        def _(sp):
            sp.dma_start(w[:], w_dram).then_inc(w_in, 16)
            sp.dma_start(nw[:], nw_dram).then_inc(nw_in, 16)

        @block.tensor
        def _(pe):
            pe.wait_ge(w_in, 16)
            for t in range(TT):
                for c in range(KC):
                    last = nc.tensor.matmul(lat_ps[:, t, :], g.xnT[:, c, tile(t)], w[:, c, :],
                                            start=(c == 0), stop=(c == KC - 1))
            last.then_inc(products, 1)
            for t in range(TT):
                pe.wait_ge(scaled, 2 * t + 2)
                last = nc.tensor.transpose(turned_ps[:, tile(t)], lat[:, t, :], g.ident[:])
            last.then_inc(turned, 1)
            for t in range(TT):
                last = nc.tensor.transpose(low_ps[:, tile(t)], lat[:, t, KV0:P], g.ident[:])
            last.then_inc(turned, 1)

        @block.scalar
        def _(act):
            act.wait_ge(products, 1)
            act.wait_ge(step, 1)
            n = 0
            for t in range(TT):
                for k, (at, width) in enumerate(parts):
                    if n:
                        act.wait_ge(summed, n)
                    nc.scalar.activation(squares[:, 0:width], lat_ps[:, t, at:at + width], ACT.Square,
                                         accum_out=ssq[:, k, t:t + 1]).then_inc(summed, 1)
                    n += 1
            act.wait_ge(summed, n)
            for k, (at, width) in enumerate(parts):
                nc.scalar.activation(sd[:, k, :], ssq[:, k, :], ACT.Sqrt, bias=eps[:, 0:1], scale=1.0 / width
                                     ).then_inc(rooted, 1)
            act.wait_ge(turned, 1)
            act.wait_ge(nw_in, 16)
            nc.scalar.activation(latT[:], turned_ps[:], ACT.Copy, scale=nw[:, 0:1])
            for odd in range(2):
                nc.scalar.activation(stack[KV0:P, odd, 0, 1, :], turned_ps[KV0:P, :], ACT.Copy, scale=nw[KV0:P, 1:2])
            act.wait_ge(turned, 2)
            for odd in range(2):
                nc.scalar.activation(stack[0:KVL, odd, 1, 1, :], low_ps[:], ACT.Copy, scale=nw[0:KVL, 1:2])

        @block.vector
        def _(dve):
            nc.vector.memset(eps[:], LAT_EPS).then_inc(step, 1)
            dve.wait_ge(rooted, 2)
            nc.vector.reciprocal(rstd[:], sd[:]).then_inc(step, 1)
            nc.vector.memset(lat[:], 0.0).then_inc(step, 1)
            dve.wait_ge(step, 3)
            for t in range(TT):
                for k, (at, width) in enumerate(parts):
                    nc.vector.tensor_scalar(lat[:, t, at:at + width], lat_ps[:, t, at:at + width],
                                            rstd[:, k, t:t + 1], None, ALU.mult).then_inc(scaled, 1)


def attention_block(nc, g, tag, latT, lat, stack, wqk_dram, wvo_dram, nw_dram, rope_dram, table_dram):
    SCALE = float(HEAD + ROPE) ** -0.5
    PAIRS = HEADS // 2
    NT = 2 * TT
    UA, UR = 4, 8
    UNITS = UA + UR
    with ExitStack() as ctx:
        m = Scope(nc, ctx, tag)
        wqk = m.sb("wqk", [P, 2, QL + KVL])
        wvo = m.sb("wvo", [P, 2 * KVL + 2 * D])
        wr = m.sb("wr", [P, KC, 4, P])
        nw = m.sb("nw", [P, 2])
        table = m.sb("table", [P, 2, S])
        absorb = m.sb("absorb", [QL, 2 * KVL])
        wout = m.sb("wout", [P, PAIRS, D])
        part = m.sb("part", [P, 2, 2, HALF])
        prob = m.sb("prob", [P, 2, S])
        probT = m.sb("probT", [P, 2, TT, P])
        total, inv, top, bias = (m.sb(n, [P, NT]) for n in ("total", "inv", "top", "bias"))
        ctx_tok = m.sb("ctx_tok", [P, 2 * KVL])
        mixed = m.sb("mixed", [P, PAIRS, S])
        score_ps = m.ps("score_ps", [P, 2, NH2, HALF])
        turned_ps = m.ps("turned_ps", [P, TT, P])
        unit_ps = m.ps("unit_ps", [P, HALF])
        ctx_ps = m.ps("ctx_ps", [P, HALF])
        wqk_in, wvo_in, wr_in, table_in, nw_in = (m.sem(n) for n in ("wqk_in", "wvo_in", "wr_in", "table_in", "nw_in"))
        projected, act_used, rope_used, rotated = (m.sem(n) for n in ("projected", "act_used", "rope_used", "rotated"))
        scored, maxed, biased, powered, turned, kept = (
            m.sem(n) for n in ("scored", "maxed", "biased", "powered", "turned", "kept"))
        valued, inverted, ctx_scaled, ctx_turned, ctx_stored, y_done = (
            m.sem(n) for n in ("valued", "inverted", "ctx_scaled", "ctx_turned", "ctx_stored", "y_done"))
        block = ctx.enter_context(nc.Block())
        TURN = 2 * KVL

        def at(j, odd, per_pair, n):
            return j * (2 * per_pair) + (odd * per_pair + n)

        def pairs(eng, steps):
            with eng.Fori(0, PAIRS // 2 - 1) as j:
                for odd in range(2):
                    steps(j, odd, True)
            steps(PAIRS // 2 - 1, 0, True)
            steps(PAIRS // 2 - 1, 1, False)

        @block.sync
        def _(sp):
            def load(i):
                sp.dma_start(wqk[:], wqk_dram[bass.ds(i, 1)].rearrange("a p h n -> p (a h) n")).then_inc(wqk_in, 16)
                sp.dma_start(wvo[:], wvo_dram[bass.ds(i, 1)].rearrange("a p n -> p (a n)")).then_inc(wvo_in, 16)

            def load_rope(i):
                sp.dma_start(wr[:], rope_dram[bass.ds(i, 1)].rearrange("a p c k n -> p (a c) k n")).then_inc(wr_in, 16)

            load(0)
            sp.dma_start(nw[:], nw_dram).then_inc(nw_in, 16)
            load_rope(0)
            sp.dma_start(table[:], table_dram).then_inc(table_in, 16)
            with sp.Fori(1, PAIRS) as i:
                sp.wait_ge(projected, i * UNITS + (2 - UNITS))
                load(i)
                sp.wait_ge(projected, i * UNITS)
                load_rope(i)

        @block.tensor
        def _(pe):
            pe.sem_inc(rope_used, UR)
            pe.sem_inc(valued, 2)
            pe.sem_inc(kept, 1)
            pe.sem_inc(ctx_stored, 1)

            def unit(j, odd, u):
                if u == 0:
                    pe.wait_ge(rope_used, at(j, odd, UR, UR))
                    pe.wait_ge(wqk_in, at(j, odd, 16, 16))
                    for hd in (1, 0):
                        cols = slice((1 - hd) * KVL, (2 - hd) * KVL)
                        last = nc.tensor.matmul(unit_ps[0:QL, cols], wqk[:, hd, 0:QL], wqk[:, hd, QL:], start=True,
                                                stop=True)
                elif u == 1:
                    pe.wait_ge(act_used, at(j, odd, UA, u))
                    pe.wait_ge(wvo_in, at(j, odd, 16, 16))
                    last = nc.tensor.matmul(unit_ps[:], wvo[:, 0:2 * KVL], wvo[:, 2 * KVL:], start=True, stop=True)
                elif u < UA:
                    pe.wait_ge(act_used, at(j, odd, UA, u))
                    last = nc.tensor.matmul(unit_ps[:], absorb[:], latT[0:QL, half(u - 2)], start=True, stop=True)
                else:
                    r = u - UA
                    if r == 0:
                        pe.wait_ge(act_used, at(j, odd, UA, UA))
                        pe.wait_ge(wr_in, at(j, odd, 16, 16))
                    else:
                        pe.wait_ge(rope_used, at(j, odd, UR, UR + r))
                    qk, h, swap = r // 4, r // 2 % 2, r % 2
                    for c in range(KC):
                        last = nc.tensor.matmul(unit_ps[:], wr[:, c, 2 * qk + swap, :], g.xnT[:, c, half(h)],
                                                start=(c == 0), stop=(c == KC - 1))
                last.then_inc(projected, 1)

            def scores(j, odd, n):
                if n == 0:
                    pe.wait_ge(rotated, at(j, odd, 8, 14))
                    pe.wait_ge(act_used, at(j, odd, UA, UA))
                hd, t = n % 2, n // 2
                for h in range(NH2):
                    last = nc.tensor.matmul(score_ps[:, n % 2, h, :], stack[:, odd, hd, 0, tile(t)],
                                            stack[:, odd, hd, 1, half(h)], start=True, stop=True)
                last.then_inc(scored, 1)

            def turn(j, odd, n):
                pe.wait_ge(powered, at(j, odd, NT, n + 1))
                pe.wait_ge(kept, at(j, odd, NT, n + 1))
                for k in range(TT):
                    last = nc.tensor.transpose(turned_ps[:, k, :], prob[:, n % 2, tile(k)], g.ident[:])
                last.then_inc(turned, 1)

            def values(j, odd, n):
                pe.wait_ge(kept, at(j, odd, NT, n + 2))
                if n % 2 == 0:
                    pe.wait_ge(ctx_stored, at(j, odd, TT, n // 2 + 1))
                for k in range(TT):
                    last = nc.tensor.matmul(ctx_ps[:, (n % 2) * KVL:(n % 2 + 1) * KVL], probT[:, n % 2, k, :],
                                            lat[:, k, KV0:P], start=(k == 0), stop=(k == TT - 1))
                last.then_inc(valued, 1)

            def turn_output(j, odd, t):
                pe.wait_ge(ctx_scaled, at(j, odd, NT, 2 * t + 2))
                nc.tensor.transpose(ctx_ps[:, TURN:TURN + P], ctx_tok[:], g.ident[:]).then_inc(ctx_turned, 1)

            def steps(j, odd, more):
                nj, nodd = (j, 1) if odd == 0 else (j + 1, 0)
                for n in range(NT):
                    if n + 1 < NT:
                        scores(j, odd, n + 1)
                    if n:
                        values(j, odd, n - 1)
                    if more and n < UNITS:
                        unit(nj, nodd, n)
                    turn(j, odd, n)
                    if n and n % 2 == 0:
                        turn_output(j, odd, n // 2 - 1)
                if more:
                    scores(nj, nodd, 0)
                values(j, odd, NT - 1)
                turn_output(j, odd, TT - 1)

            for u in range(UNITS):
                unit(0, 0, u)
            scores(0, 0, 0)
            pairs(pe, steps)
            pe.wait_ge(ctx_stored, PAIRS * TT + 1)
            for c in range(KC):
                for h in range(NH2):
                    for p in range(PAIRS):
                        last = nc.tensor.matmul(score_ps[:, c, h, :], wout[:, p, tile(c)], mixed[:, p, half(h)],
                                                start=(p == 0), stop=(p == PAIRS - 1))
                    last.then_inc(y_done, 1)

        @block.vector
        def _(dve):
            dve.wait_ge(table_in, 16)

            def unit(j, odd, u):
                r = u - UA
                h, swap = r // 2 % 2, r % 2
                dve.wait_ge(projected, at(j, odd, UNITS, u + 1))
                dve.wait_ge(rotated, at(j, odd, 8, 4 * (r // 4) + 2 * h + 4))
                nc.vector.tensor_tensor(part[:, h, swap, :], unit_ps[:], table[:, swap, half(h)],
                                        ALU.mult).then_inc(rope_used, 1)

            def largest(j, odd, n):
                dve.wait_ge(scored, at(j, odd, NT, n + 1))
                nc.vector.tensor_reduce(top[:, n:n + 1], score_ps[:, n % 2].rearrange("p h n -> p (h n)"), AX.X, ALU.max
                                        ).then_inc(maxed, 1)
                dve.wait_ge(maxed, at(j, odd, NT, n + 1))
                nc.vector.tensor_scalar(bias[:, n:n + 1], top[:, n:n + 1], -SCALE, None, ALU.mult
                                        ).then_inc(biased, 1)

            def scale_output(j, odd, t):
                dve.wait_ge(powered, at(j, odd, NT, 2 * t + 2))
                nc.vector.reciprocal(inv[:, 2 * t:2 * t + 2], total[:, 2 * t:2 * t + 2]).then_inc(inverted, 1)
                dve.wait_ge(inverted, at(j, odd, TT, t + 1))
                dve.wait_ge(valued, at(j, odd, NT, 2 * t + 4))
                for hd in range(2):
                    own = slice(hd * KVL, (hd + 1) * KVL)
                    nc.vector.tensor_scalar(ctx_tok[:, own], ctx_ps[:, own], inv[:, 2 * t + hd:2 * t + hd + 1], None,
                                            ALU.mult).then_inc(ctx_scaled, 1)

            def steps(j, odd, more):
                nj, nodd = (j, 1) if odd == 0 else (j + 1, 0)
                for n in range(NT):
                    if n + 1 < NT:
                        largest(j, odd, n + 1)
                    if n and n % 2 == 0:
                        scale_output(j, odd, n // 2 - 1)
                    if more and UA <= n < UNITS:
                        unit(nj, nodd, n)
                if more:
                    largest(nj, nodd, 0)
                scale_output(j, odd, TT - 1)

            for u in range(UA, UNITS):
                unit(0, 0, u)
            largest(0, 0, 0)
            pairs(dve, steps)

        @block.gpsimd
        def _(pool):
            pool.sem_inc(rotated, 6)
            with pool.Fori(0, PAIRS // 2) as j:
                for odd in range(2):
                    for r in range(4):
                        qk, h = r // 2, r % 2
                        pool.wait_ge(rope_used, at(j, odd, UR, UR + 2 * r + 2))
                        for hd in range(2):
                            own = slice(ROPE * hd, ROPE * hd + ROPE)
                            nc.gpsimd.tensor_tensor(stack[own, odd, hd, qk, half(h)], part[own, h, 0, :],
                                                    part[own, h, 1, :], ALU.add).then_inc(rotated, 1)

        @block.scalar
        def _(act):
            act.wait_ge(nw_in, 16)

            def unit(j, odd, u):
                act.wait_ge(projected, at(j, odd, UNITS, u + 1))
                if u == 0:
                    nc.scalar.activation(absorb[:], unit_ps[0:QL, 0:2 * KVL], ACT.Copy).then_inc(act_used, 1)
                elif u == 1:
                    for hd in range(2):
                        own = slice(hd * KVL, (hd + 1) * KVL)
                        last = nc.scalar.activation(wout[own, bass.ds(j * 2 + odd, 1), :],
                                                    unit_ps[own, hd * D:(hd + 1) * D].unsqueeze(1), ACT.Copy,
                                                    scale=nw[own, 1:2])
                    last.then_inc(act_used, 1)
                else:
                    for hd in range(2):
                        own = slice((1 - hd) * KVL, (2 - hd) * KVL)
                        last = nc.scalar.activation(stack[own, odd, hd, 0, half(u - 2)], unit_ps[own, :], ACT.Copy)
                    last.then_inc(act_used, 1)

            def power(j, odd, n):
                act.wait_ge(biased, at(j, odd, NT, n + 1))
                if n >= 2:
                    act.wait_ge(turned, at(j, odd, NT, n - 1))
                nc.scalar.activation(prob[:, n % 2, :], score_ps[:, n % 2].rearrange("p h n -> p (h n)"), ACT.Exp,
                                     bias=bias[:, n:n + 1], scale=SCALE, accum_out=total[:, n:n + 1]
                                     ).then_inc(powered, 1)

            def keep(j, odd, n):
                act.wait_ge(turned, at(j, odd, NT, n + 1))
                act.wait_ge(valued, at(j, odd, NT, n + 1))
                nc.scalar.activation(probT[:, n % 2], turned_ps[:], ACT.Copy).then_inc(kept, 1)

            def store(j, odd, t):
                act.wait_ge(ctx_turned, at(j, odd, TT, t + 1))
                nc.scalar.activation(mixed[:, bass.ds(j * 2 + odd, 1), tile(t)], ctx_ps[:, TURN:TURN + P].unsqueeze(1),
                                     ACT.Copy).then_inc(ctx_stored, 1)

            def steps(j, odd, more):
                nj, nodd = (j, 1) if odd == 0 else (j + 1, 0)
                for n in range(NT):
                    if n + 1 < NT:
                        power(j, odd, n + 1)
                    if more and n < UA:
                        unit(nj, nodd, n)
                    keep(j, odd, n)
                    if n and n % 2 == 0:
                        store(j, odd, n // 2 - 1)
                if more:
                    act.wait_ge(turned, at(j, odd, NT, NT))
                    power(nj, nodd, 0)
                store(j, odd, TT - 1)

            for u in range(UA):
                unit(0, 0, u)
            power(0, 0, 0)
            pairs(act, steps)
            for c in range(KC):
                for h in range(NH2):
                    act.wait_ge(y_done, NH2 * c + h + 1)
                    nc.scalar.activation(g.yT[:, c, half(h)], score_ps[:, c, h, :], ACT.Copy)


def latent_attention_stage(nc, g, d):
    with ExitStack() as ctx:
        m = Scope(nc, ctx, "mla")
        latT, lat = m.sb("latT", [P, S]), m.sb("lat", [P, TT, P])
        stack = m.sb("stack", [P, 2, 2, 2, S])
        latent_block(nc, g, "latent", latT, lat, stack, d["lat_w"], d["lat_nw"])
        attention_block(nc, g, "attn", latT, lat, stack, d["mla_wqk"], d["mla_wvo"], d["lat_nw"], d["mla_rope"],
                        d["mla_table"])


M_HEADS, M_P, M_N, M_CHUNK, TAPS = 64, 64, 128, 32, 4
M_INNER = M_HEADS * M_P
M_BLOCKS = M_INNER // P
NC = P // M_CHUNK
NORM_EPS = 1e-5
NEG = -1e30
PAR = TAPS + 3


def conv_taps(nc, dve, done, base, ps, acc, tap):
    for k in range(1, TAPS):
        if k > 1:
            dve.wait_ge(done, base + (k - 1))
        nc.vector.scalar_tensor_tensor(out=acc[:, k:S], in0=ps[:, 0:S - k], scalar=tap(TAPS - 1 - k),
                                       in1=acc[:, k:S], op0=ALU.mult, op1=ALU.add).then_inc(done, 1)


def mamba_prepare_block(nc, g, s, w_dram, par_dram, dt_dram, spread_dram):
    with ExitStack() as ctx:
        m = Scope(nc, ctx, "mprep")
        w = m.sb("w", [P, KC, 2 * P + M_HEADS])
        par = m.sb("par", [P, 2, PAR])
        dtp = m.sb("dtp", [M_HEADS, 2])
        bc_ps = m.ps("bc_ps", [P, 2, S])
        dt_ps = m.ps("dt_ps", [M_HEADS, S])
        turned_ps = m.ps("turned_ps", [P, 2, HALF])
        acc, bcT = m.sb("acc", [P, 2, S]), m.sb("bcT", [P, 2, S])
        x, neg, soft, dt, keep, adt, cum, last_, dec = (
            m.sb(n, [M_HEADS, S]) for n in ("x", "neg", "soft", "dt", "keep", "adt", "cum", "last", "dec"))
        a = m.sb("a", [M_HEADS, 1])
        spread = m.sb("spread", [M_HEADS, 2, NC, TT, M_CHUNK])
        w_in, par_in, dtp_in, kept, products, conv0, conv, silu = (
            m.sem(n) for n in ("w_in", "par_in", "dtp_in", "kept", "products", "conv0", "conv", "silu"))
        v_step, a_step, turned, spread_ready, spread_out, gc_ready, mask0 = (
            m.sem(n) for n in ("v_step", "a_step", "turned", "spread_ready", "spread_out", "gc_ready", "mask0"))
        block = ctx.enter_context(nc.Block())

        @block.sync
        def _(sp):
            sp.dma_start(w[:], w_dram).then_inc(w_in, 16)
            sp.dma_start(par[:], par_dram).then_inc(par_in, 16)
            sp.dma_start(dtp[:], dt_dram).then_inc(dtp_in, 16)
            sp.wait_ge(spread_ready, 2)
            for k in range(2):
                for hd in range(2):
                    sp.dma_start(spread_dram[:, :, k, hd, :],
                                 spread[hd:M_HEADS:2, k].rearrange("h c t l -> h c (t l)")).then_inc(spread_out, 16)
            sp.wait_ge(spread_out, 64)

        @block.gpsimd
        def _(pool):
            nc.gpsimd.memset(s.causal[:], 0.0).then_inc(mask0, 1)
            nc.gpsimd.memset(s.w_diag[:], 0.0).then_inc(mask0, 1)
            nc.gpsimd.memset(s.square_sum[:], 0.0).then_inc(mask0, 1)
            for c in range(NC):
                pool.wait_ge(mask0, 3 + c)
                own = s.causal[c * M_CHUNK:(c + 1) * M_CHUNK, :]
                nc.gpsimd.affine_select(out=own, in_=own, compare_op=ALU.is_ge, fill=NEG, base=0,
                                        pattern=[[1, M_CHUNK]], channel_multiplier=-1).then_inc(mask0, 1)

        @block.tensor
        def _(pe):
            pe.wait_ge(w_in, 16)
            for h in range(NH2):
                for c in range(KC):
                    last = nc.tensor.matmul(dt_ps[:, half(h)], w[:, c, 2 * P:], g.xnT[:, c, half(h)],
                                            start=(c == 0), stop=(c == KC - 1))
            last.then_inc(products, 1)
            for n in range(2):
                for h in range(NH2):
                    for c in range(KC):
                        last = nc.tensor.matmul(bc_ps[:, n, half(h)], w[:, c, tile(n)], g.xnT[:, c, half(h)],
                                                start=(c == 0), stop=(c == KC - 1))
                last.then_inc(products, 1)
            small = M_HEADS
            pe.wait_ge(v_step, 4)
            for n, src in enumerate((dt, cum)):
                for t in range(TT):
                    last = nc.tensor.transpose(turned_ps[:, n, t * small:(t + 1) * small], src[:, tile(t)],
                                               g.ident[0:small, 0:small])
                last.then_inc(turned, 1)
            pe.wait_ge(a_step, 5)
            pe.wait_ge(gc_ready, 1)
            for t in range(TT):
                last = nc.tensor.transpose(turned_ps[:, 0, t * small:(t + 1) * small], dec[:, tile(t)],
                                           g.ident[0:small, 0:small])
            last.then_inc(turned, 1)
            pe.wait_ge(silu, 2)
            for t in range(TT):
                last = nc.tensor.matmul(bc_ps[:, 0, tile(t)], bcT[:, 0, tile(t)], bcT[:, 1, tile(t)],
                                        start=True, stop=True)
            last.then_inc(turned, 1)

        @block.scalar
        def _(act):
            act.wait_ge(products, 1)
            act.wait_ge(dtp_in, 16)
            nc.scalar.activation(x[:], dt_ps[:], ACT.Identity, bias=dtp[:, 0:1]).then_inc(a_step, 1)
            act.wait_ge(v_step, 1)
            nc.scalar.activation(soft[:], neg[:], ACT.Exp).then_inc(a_step, 1)
            nc.scalar.activation(a[:], dtp[:, 1:2], ACT.Exp).then_inc(a_step, 1)
            act.wait_ge(a_step, 3)
            nc.scalar.activation(soft[:], soft[:], ACT.Ln, bias=1.0).then_inc(a_step, 1)
            act.wait_ge(v_step, 4)
            cum_v = cum[:].rearrange("h (t c l) -> h c t l", t=TT, c=NC)
            for c in range(NC):
                nc.scalar.activation(spread[:, 0, c], cum_v[:, c], ACT.Copy)
                last = nc.scalar.activation(spread[:, 1, c], cum_v[:, c], ACT.Exp)
            last.then_inc(spread_ready, 2)
            act.wait_ge(v_step, 5)
            nc.scalar.activation(dec[:], last_[:], ACT.Exp).then_inc(a_step, 1)
            act.wait_ge(par_in, 16)
            for n in range(2):
                act.wait_ge(products, 2 + n)
                nc.scalar.activation(acc[:, n, :], bc_ps[:, n, :], ACT.Identity, bias=par[:, n, TAPS:TAPS + 1],
                                     scale=par[:, n, TAPS - 1:TAPS]).then_inc(conv0, 1)
            for n in range(2):
                act.wait_ge(conv, 3 * n + 3)
                nc.scalar.activation(bcT[:, n, :], acc[:, n, :], ACT.Silu).then_inc(silu, 1)

        @block.vector
        def _(dve):
            nc.vector.memset(keep[:], 1.0).then_inc(kept, 1)
            dve.wait_ge(kept, 1)
            nc.vector.memset(keep[:, 0:S:M_CHUNK], 0.0).then_inc(kept, 1)
            dve.wait_ge(a_step, 1)
            nc.vector.scalar_tensor_tensor(out=neg[:], in0=x[:], scalar=-1.0, in1=x[:], op0=ALU.mult, op1=ALU.min
                                           ).then_inc(v_step, 1)
            dve.wait_ge(a_step, 4)
            nc.vector.scalar_tensor_tensor(out=dt[:], in0=x[:], scalar=0.0, in1=soft[:], op0=ALU.max, op1=ALU.add
                                           ).then_inc(v_step, 1)
            dve.wait_ge(v_step, 2)
            nc.vector.tensor_scalar(dt[:], dt[:], 0.0, None, ALU.max).then_inc(v_step, 1)
            nc.vector.tensor_scalar(a[:], a[:], -1.0, None, ALU.mult).then_inc(kept, 1)
            dve.wait_ge(v_step, 3)
            dve.wait_ge(kept, 3)
            nc.vector.tensor_scalar(adt[:], dt[:], a[:, 0:1], None, ALU.mult).then_inc(kept, 1)
            dve.wait_ge(kept, 4)
            nc.vector.tensor_tensor_scan(cum[:], keep[:], adt[:], 0.0, ALU.mult, ALU.add).then_inc(v_step, 1)
            dve.wait_ge(v_step, 4)
            cum_v = cum[:].rearrange("h (c l) -> h c l", l=M_CHUNK)
            end = cum_v[:, :, M_CHUNK - 1:M_CHUNK].to_broadcast((M_HEADS, S // M_CHUNK, M_CHUNK))
            nc.vector.tensor_tensor(last_[:].rearrange("h (c l) -> h c l", l=M_CHUNK), end, cum_v, ALU.subtract
                                    ).then_inc(v_step, 1)
            dve.wait_ge(par_in, 16)
            for n in range(2):
                dve.wait_ge(conv0, n + 1)
                conv_taps(nc, dve, conv, 3 * n, bc_ps[:, n, :], acc[:, n, :], lambda k: par[:, n, k:k + 1])
            dve.wait_ge(turned, 1)
            nc.vector.tensor_copy(s.dt[:].rearrange("p t h -> p (t h)"), turned_ps[:, 0, :]).then_inc(gc_ready, 1)
            dve.wait_ge(turned, 2)
            nc.vector.tensor_copy(s.cum[:].rearrange("p t h -> p (t h)"), turned_ps[:, 1, :])
            dve.wait_ge(turned, 3)
            nc.vector.tensor_copy(s.decay[:].rearrange("p t h -> p (t h)"), turned_ps[:, 0, :])
            dve.wait_ge(turned, 4)
            for c in range(NC):
                own = slice(c * M_CHUNK, (c + 1) * M_CHUNK)
                nc.vector.tensor_copy(s.gram[own], bc_ps[own, 0, :].rearrange("p (t n) -> p t n", t=TT)[:, :, own])


def mamba_heads_block(nc, g, s, hidden, wg_dram, wh_dram, par_dram, spread_dram):
    with ExitStack() as ctx:
        m = Scope(nc, ctx, "mamba")
        wg, wh = m.sb("wg", [P, KC, P]), m.sb("wh", [P, KC, P])
        par = m.sb("par", [P, M_BLOCKS, PAR])
        ae = m.sb("ae", [P, 2, 2, TT, M_CHUNK])
        dif, ed = m.sb("dif", [P, 2, TT, M_CHUNK]), m.sb("ed", [P, 2, TT, M_CHUNK])
        acc, hT, sg, yd = (m.sb(n, [P, S]) for n in ("acc", "hT", "sg", "yd"))
        yf, square = g.yT[:, 0, :], g.yT[:, 1, :]
        hdt = m.sb("hdt", [P, TT, P])
        h_ps, gate_ps, y_ps = (m.ps(n, [P, S]) for n in ("h_ps", "gate_ps", "y_ps"))
        turned_ps = m.ps("turned_ps", [P, TT, P])
        wg_in, wh_in, ae_in, par_in = (m.sem(n) for n in ("wg_in", "wh_in", "ae_in", "par_in"))
        h_done, y_done, gate_done, turned = (m.sem(n) for n in ("h_done", "y_done", "gate_done", "turned"))
        conv0, h_ready, g_ready, powered, kept = (m.sem(n) for n in ("conv0", "h_ready", "g_ready", "powered", "kept"))
        conv, diffed, summed, quad_v, added, gated, hdt_ready = (
            m.sem(n) for n in ("conv", "diffed", "summed", "quad_v", "added", "gated", "hdt_ready"))
        masked, decayed, quad_p, squared = (m.sem(n) for n in ("masked", "decayed", "quad_p", "squared"))
        block = ctx.enter_context(nc.Block())

        def own_par(i, k):
            return par[:, bass.ds(i, 1), k:k + 1].rearrange("p a b -> p (a b)")

        def quad(i, c, engine):
            q = slice(c * M_CHUNK, (c + 1) * M_CHUNK)
            return engine.tensor_tensor(s.w_diag[q, :, :, q], dif[q], s.gram[q].unsqueeze(1).to_broadcast(
                (M_CHUNK, 2, TT, M_CHUNK)), ALU.mult)

        @block.sync
        def _(sp):
            def load_h(i):
                sp.dma_start(wh[:], wh_dram[bass.ds(i, 1)].rearrange("a p c n -> p (a c) n")).then_inc(wh_in, 16)

            def load_g(i):
                sp.dma_start(wg[:], wg_dram[bass.ds(i, 1)].rearrange("a p c n -> p (a c) n")).then_inc(wg_in, 16)

            def load_ae(i):
                src = spread_dram[bass.ds(i, 1)].rearrange("a c k h x -> (a c) (k h x)")
                src = src.unsqueeze(1).to_broadcast((NC, M_CHUNK, 4 * TT * M_CHUNK))
                sp.dma_start(ae[:].rearrange("p k h t l -> p (k h t l)"), src).then_inc(ae_in, 16)

            load_h(0)
            sp.dma_start(par[:], par_dram).then_inc(par_in, 16)
            load_ae(0)
            load_g(0)
            with sp.Fori(1, M_BLOCKS) as i:
                sp.wait_ge(h_done, i)
                load_h(i)
                sp.wait_ge(diffed, i)
                sp.wait_ge(decayed, i)
                load_ae(i)
                sp.wait_ge(gate_done, i)
                load_g(i)

        @block.tensor
        def _(pe):
            def project(i, w, w_in, ps, done):
                pe.wait_ge(w_in, i * 16 + 16)
                for h in range(NH2):
                    for c in range(KC):
                        last = nc.tensor.matmul(ps[:, half(h)], w[:, c, :], g.xnT[:, c, half(h)],
                                                start=(c == 0), stop=(c == KC - 1))
                last.then_inc(done, 1)

            def mix(i):
                pe.wait_ge(hdt_ready, i + 1)
                pe.wait_ge(quad_v, i * 2 + 2)
                pe.wait_ge(quad_p, i * 2 + 2)
                for hd in range(2):
                    for t in range(TT):
                        last = nc.tensor.matmul(y_ps[hd * M_P:(hd + 1) * M_P, tile(t)],
                                                hdt[:, t, hd * M_P:(hd + 1) * M_P], s.w_diag[:, hd, t, :],
                                                start=True, stop=True)
                last.then_inc(y_done, 1)

            def turn(i):
                pe.wait_ge(h_ready, i + 1)
                for t in range(TT):
                    last = nc.tensor.transpose(turned_ps[:, t, :], hT[:, tile(t)], g.ident[:])
                last.then_inc(turned, 1)

            project(0, wh, wh_in, h_ps, h_done)
            project(0, wg, wg_in, gate_ps, gate_done)
            turn(0)
            with pe.Fori(1, M_BLOCKS) as i:
                pe.wait_ge(conv, i * 3)
                project(i, wh, wh_in, h_ps, h_done)
                pe.wait_ge(added, i)
                mix(i - 1)
                pe.wait_ge(g_ready, i)
                project(i, wg, wg_in, gate_ps, gate_done)
                turn(i)
            pe.wait_ge(added, M_BLOCKS)
            mix(M_BLOCKS - 1)

        @block.scalar
        def _(act):
            def early(i, first):
                act.wait_ge(h_done, i + 1)
                if not first:
                    act.wait_ge(h_ready, i)
                nc.scalar.activation(acc[:], h_ps[:], ACT.Identity, bias=own_par(i, TAPS),
                                     scale=own_par(i, TAPS - 1)).then_inc(conv0, 1)
                act.wait_ge(masked, i + 1)
                nc.scalar.activation(dif[:], dif[:], ACT.Exp).then_inc(powered, 1)
                act.wait_ge(conv, i * 3 + 3)
                if not first:
                    act.wait_ge(added, i + 1)
                nc.scalar.activation(hT[:], acc[:], ACT.Silu).then_inc(h_ready, 1)

            def keep(i):
                act.wait_ge(gated, i + 1)
                act.wait_ge(squared, i + 1)
                nc.scalar.activation(square, yf, ACT.Square).then_inc(kept, 1)
                nc.scalar.activation(hidden[:, bass.ds(i, 1), :].rearrange("p a n -> p (a n)"), yf, ACT.Copy,
                                     scale=own_par(i, TAPS + 2)).then_inc(kept, 1)

            def late(i):
                act.wait_ge(gate_done, i + 1)
                nc.scalar.activation(sg[:], gate_ps[:], ACT.Silu).then_inc(g_ready, 1)

            act.wait_ge(par_in, 16)
            early(0, True)
            late(0)
            with act.Fori(1, M_BLOCKS) as i:
                early(i, False)
                keep(i - 1)
                late(i)
            keep(M_BLOCKS - 1)

        @block.vector
        def _(dve):
            def early(i, first):
                dve.wait_ge(ae_in, i * 16 + 16)
                if not first:
                    dve.wait_ge(quad_p, i * 2)
                    dve.wait_ge(quad_v, i * 2)
                own = s.cum[:, :, bass.ds(i * 2, 2)].rearrange("p t h -> p h t").unsqueeze(3)
                nc.vector.tensor_tensor(dif[:], ae[:, 0], own.to_broadcast((P, 2, TT, M_CHUNK)), ALU.subtract
                                        ).then_inc(diffed, 1)
                dve.wait_ge(conv0, i + 1)
                conv_taps(nc, dve, conv, i * 3, h_ps, acc, lambda k: own_par(i, k))
                dve.wait_ge(powered, i + 1)
                dve.wait_ge(decayed, i + 1)
                nc.vector.tensor_tensor(dif[:], dif[:], ed[:], ALU.add).then_inc(summed, 1)
                dve.wait_ge(summed, i + 1)
                if not first:
                    dve.wait_ge(y_done, i)
                for c in range(0, NC, 2):
                    quad(i, c, nc.vector).then_inc(quad_v, 1)

            def outputs(i):
                dve.wait_ge(y_done, i + 1)
                nc.vector.scalar_tensor_tensor(out=yd[:], in0=hT[:], scalar=own_par(i, TAPS + 1), in1=y_ps[:],
                                               op0=ALU.mult, op1=ALU.add).then_inc(added, 1)
                dve.wait_ge(added, i + 2)
                dve.wait_ge(g_ready, i + 1)
                dve.wait_ge(kept, i * 2 + 2)
                nc.vector.tensor_tensor(yf, yd[:], sg[:], ALU.mult).then_inc(gated, 1)

            def token_major(i):
                dve.wait_ge(turned, i + 1)
                own = s.dt[:, :, bass.ds(i * 2, 2)].unsqueeze(3).to_broadcast((P, TT, 2, M_P))
                nc.vector.tensor_tensor(hdt[:].rearrange("p t (h n) -> p t h n", h=2),
                                        turned_ps[:].rearrange("p t (h n) -> p t h n", h=2), own, ALU.mult
                                        ).then_inc(hdt_ready, 1)

            dve.wait_ge(par_in, 16)
            dve.sem_inc(added, 1)
            dve.sem_inc(kept, 2)
            early(0, True)
            token_major(0)
            with dve.Fori(1, M_BLOCKS) as i:
                early(i, False)
                outputs(i - 1)
                token_major(i)
            outputs(M_BLOCKS - 1)

        @block.gpsimd
        def _(pool):
            def build(i, first):
                pool.wait_ge(diffed, i + 1)
                nc.gpsimd.tensor_tensor(dif[:], dif[:], s.causal[:].unsqueeze(1).unsqueeze(1).to_broadcast(
                    (P, 2, TT, M_CHUNK)), ALU.add).then_inc(masked, 1)
                if not first:
                    pool.wait_ge(summed, i)
                own = s.decay[:, :, bass.ds(i * 2, 2)].rearrange("p t h -> p h t").unsqueeze(3)
                nc.gpsimd.tensor_tensor(ed[:], ae[:, 1], own.to_broadcast((P, 2, TT, M_CHUNK)), ALU.mult
                                        ).then_inc(decayed, 1)
                pool.wait_ge(summed, i + 1)
                if not first:
                    pool.wait_ge(y_done, i)
                pool.wait_ge(decayed, i + 1)
                quad(i, 1, nc.gpsimd).then_inc(quad_p, 1)
                pool.wait_ge(quad_p, i * 2 + 1)
                quad(i, 3, nc.gpsimd).then_inc(quad_p, 1)
                pool.wait_ge(quad_p, i * 2 + 2)

            def add_squares(i):
                pool.wait_ge(kept, i * 2 + 3)
                pool.wait_ge(squared, i + 1)
                nc.gpsimd.tensor_tensor(s.square_sum[:], s.square_sum[:], square, ALU.add).then_inc(squared, 1)

            pool.sem_inc(squared, 1)
            build(0, True)
            with pool.Fori(1, M_BLOCKS) as i:
                build(i, False)
                add_squares(i - 1)
            add_squares(M_BLOCKS - 1)


def mamba_norm_block(nc, g, s, token_scale):
    with ExitStack() as ctx:
        m = Scope(nc, ctx, "mnorm")
        sum_ps = m.ps("sum_ps", [P, TT])
        eps, sd = m.sb("eps", [P, 1]), m.sb("sd", [P, TT])
        summed, eps_set, rooted = m.sem("summed"), m.sem("eps_set"), m.sem("rooted")
        block = ctx.enter_context(nc.Block())

        @block.tensor
        def _(pe):
            for t in range(TT):
                last = nc.tensor.matmul(sum_ps[:, t:t + 1], s.square_sum[:, tile(t)], g.ones[:, 0:1],
                                        start=True, stop=True)
            last.then_inc(summed, 1)

        @block.scalar
        def _(act):
            act.wait_ge(eps_set, 1)
            act.wait_ge(summed, 1)
            nc.scalar.activation(sd[:], sum_ps[:], ACT.Sqrt, bias=eps[:, 0:1], scale=1.0 / M_INNER).then_inc(rooted, 1)

        @block.vector
        def _(dve):
            nc.vector.memset(eps[:], NORM_EPS).then_inc(eps_set, 1)
            dve.wait_ge(rooted, 1)
            nc.vector.reciprocal(token_scale[:], sd[:])


def mamba_stage(nc, g, persistent, d):
    token_scale = persistent.sb("token_scale", [P, TT])
    spread_dram = nc.dram_tensor("spread", (M_BLOCKS, NC, 2, 2, TT * M_CHUNK), F32, kind="Internal").ap()
    with ExitStack() as ctx:
        m = Scope(nc, ctx, "mam")
        s = Shared()
        s.gram = m.sb("gc", [P, TT, M_CHUNK])
        s.causal = m.sb("causal", [P, M_CHUNK])
        s.w_diag = m.sb("w_diag", [P, 2, TT, P])
        s.square_sum = m.sb("square_sum", [P, S])
        s.dt, s.cum, s.decay = (m.sb(n, [P, TT, M_HEADS]) for n in ("dt", "cum", "decay"))
        mamba_prepare_block(nc, g, s, d["mam_shared_w"], d["mam_shared_par"], d["mam_dt"], spread_dram)
        hidden = m.sb("hidden", [P, M_BLOCKS, S])
        mamba_heads_block(nc, g, s, hidden, d["mam_gate"], d["mam_hidden"], d["mam_par"], spread_dram)
        mamba_norm_block(nc, g, s, token_scale)
        project_out_block(nc, g, "mam_out", hidden, M_BLOCKS, d["mam_out"])
    return token_scale


KEY_HEADS, VALUE_HEADS, DK, DC = 16, 32, 128, 64
REP = VALUE_HEADS // KEY_HEADS
CHUNKS = S // DC
TC = P // DC
LEVELS = 6
DELTA_EPS = 1e-6
MIN_NORM = 1e-12


def delta_prepare_block(nc, g, s, w_dram, par_dram, rows_dram, exp_dram):
    with ExitStack() as ctx:
        m = Scope(nc, ctx, "dprep")
        V = VALUE_HEADS
        w = m.sb("w", [P, KC, 2 * V])
        par = m.sb("par", [V, 2])
        b_ps, a_ps = m.ps("b_ps", [V, S]), m.ps("a_ps", [V, S])
        turned_ps = m.ps("turned_ps", [P, 4, TT, V])
        beta, x, neg, soft, keep, gate, cum, eg, diff, rest, beg = (
            m.sb(n, [V, S]) for n in ("beta", "x", "neg", "soft", "keep", "gate", "cum", "eg", "diff", "rest", "beg"))
        rate = m.sb("rate", [V, 1])
        rows = m.sb("rows", [V, 2, TC, TT, DC])
        w_in, par_in, products, a_step, v_step, kept, turned, stored = (
            m.sem(n) for n in ("w_in", "par_in", "products", "a_step", "v_step", "kept", "turned", "stored"))
        block = ctx.enter_context(nc.Block())

        @block.sync
        def _(sp):
            sp.dma_start(w[:], w_dram).then_inc(w_in, 16)
            sp.dma_start(par[:], par_dram).then_inc(par_in, 16)
            sp.wait_ge(a_step, 10)
            for kind in range(2):
                for hd in range(REP):
                    sp.dma_start(rows_dram[:, :, hd, kind, :], rows[hd:V:REP, kind].rearrange("h c t l -> h c (t l)")
                                 ).then_inc(stored, 16)
            sp.dma_start(exp_dram, eg[:]).then_inc(stored, 16)
            sp.wait_ge(stored, 80)

        @block.tensor
        def _(pe):
            pe.wait_ge(w_in, 16)
            for n, ps in enumerate((a_ps, b_ps)):
                for h in range(NH2):
                    for c in range(KC):
                        last = nc.tensor.matmul(ps[:, half(h)], w[:, c, n * V:(n + 1) * V], g.xnT[:, c, half(h)],
                                                start=(c == 0), stop=(c == KC - 1))
                last.then_inc(products, 1)
            pe.wait_ge(v_step, 5)
            pe.wait_ge(a_step, 10)
            for n, src in enumerate((beta, cum, beg, rest)):
                for t in range(TT):
                    last = nc.tensor.transpose(turned_ps[:, n, t, :], src[:, tile(t)], g.ident[0:V, 0:V])
            last.then_inc(turned, 1)

        @block.scalar
        def _(act):
            act.wait_ge(par_in, 16)
            act.wait_ge(products, 1)
            nc.scalar.activation(x[:], a_ps[:], ACT.Identity, bias=par[:, 0:1]).then_inc(a_step, 1)
            act.wait_ge(v_step, 1)
            nc.scalar.activation(soft[:], neg[:], ACT.Exp).then_inc(a_step, 1)
            nc.scalar.activation(rate[:], par[:, 1:2], ACT.Exp).then_inc(a_step, 1)
            act.wait_ge(a_step, 3)
            nc.scalar.activation(soft[:], soft[:], ACT.Ln, bias=1.0).then_inc(a_step, 1)
            act.wait_ge(v_step, 3)
            nc.scalar.activation(eg[:], cum[:], ACT.Exp).then_inc(a_step, 1)
            cum_v, beta_v = (r[:].rearrange("h (t c l) -> h c t l", t=TT, c=TC) for r in (cum, beta))
            for c in range(TC):
                nc.scalar.activation(rows[:, 0, c], cum_v[:, c], ACT.Copy).then_inc(a_step, 1)
            act.wait_ge(v_step, 4)
            nc.scalar.activation(rest[:], diff[:], ACT.Exp).then_inc(a_step, 1)
            act.wait_ge(products, 2)
            nc.scalar.activation(beta[:], b_ps[:], ACT.Sigmoid).then_inc(kept, 1)
            act.wait_ge(kept, 5)
            for c in range(TC):
                nc.scalar.activation(rows[:, 1, c], beta_v[:, c], ACT.Copy).then_inc(a_step, 1)

        @block.vector
        def _(dve):
            nc.vector.memset(keep[:], 1.0).then_inc(kept, 1)
            dve.wait_ge(kept, 1)
            nc.vector.memset(keep[:, 0:S:DC], 0.0).then_inc(kept, 1)
            dve.wait_ge(a_step, 1)
            nc.vector.scalar_tensor_tensor(out=neg[:], in0=x[:], scalar=-1.0, in1=x[:], op0=ALU.mult, op1=ALU.min
                                           ).then_inc(v_step, 1)
            dve.wait_ge(a_step, 4)
            nc.vector.scalar_tensor_tensor(out=gate[:], in0=x[:], scalar=0.0, in1=soft[:], op0=ALU.max, op1=ALU.add
                                           ).then_inc(v_step, 1)
            nc.vector.tensor_scalar(rate[:], rate[:], -1.0, None, ALU.mult).then_inc(kept, 1)
            dve.wait_ge(v_step, 2)
            dve.wait_ge(kept, 3)
            nc.vector.tensor_scalar(gate[:], gate[:], rate[:, 0:1], None, ALU.mult).then_inc(kept, 1)
            dve.wait_ge(kept, 4)
            nc.vector.tensor_tensor_scan(cum[:], keep[:], gate[:], 0.0, ALU.mult, ALU.add).then_inc(v_step, 1)
            dve.wait_ge(v_step, 3)
            cum_v = cum[:].rearrange("h (c l) -> h c l", l=DC)
            end = cum_v[:, :, DC - 1:DC].to_broadcast((V, CHUNKS, DC))
            nc.vector.tensor_tensor(diff[:].rearrange("h (c l) -> h c l", l=DC), end, cum_v, ALU.subtract
                                    ).then_inc(v_step, 1)
            dve.wait_ge(kept, 5)
            dve.wait_ge(a_step, 5)
            nc.vector.tensor_tensor(beg[:], beta[:], eg[:], ALU.mult).then_inc(v_step, 1)
            dve.wait_ge(turned, 1)
            for n, dst in enumerate((s.beta, s.cum, s.beg, s.rest)):
                nc.vector.tensor_copy(dst[:], turned_ps[:, n])


def delta_heads_block(nc, g, s, w_dram, conv_dram, wo_dram, nw_dram, mask_dram, tri_dram, rows_dram, exp_dram):
    with ExitStack() as ctx:
        m = Scope(nc, ctx, "delta")
        w = m.sb("w", [P, KC, 6, P])
        taps = m.sb("taps", [P, 4, TAPS])
        wo = m.sb("wo", [P, REP, D])
        nw, eps = m.sb("nw", [P, 1]), m.sb("eps", [P, 1])
        mask = m.sb("mask", [P, LEVELS + 1, P], I32)
        tri = m.sb("tri", [P, 2, DC])
        rows = m.sb("rows", [P, REP, 2, TT, DC])
        egf = m.sb("egf", [P, REP, S])
        acc = m.sb("acc", [P, 2, S])
        feat = m.sb("feat", [P, 4, S])
        square = m.sb("square", [P, S])
        sz = m.sb("sz", [P, REP, S])
        norm, rnorm = m.sb("norm", [P, 2, TT]), m.sb("rnorm", [P, 2, TT])
        tok = m.sb("tok", [P, 4, TT, P])
        turned = m.sb("turned", [P, 2, S])
        dec = m.sb("dec", [P, REP, TT, DC])
        decb = m.sb("decb", [P, REP, TT, DC])
        attn = m.sb("attn", [P, REP, TT, DC])
        negN, negM, U, T, prod = (m.sb(n, [P, REP, TT, P]) for n in ("negN", "negM", "U", "T", "prod"))
        kbe, kd, u, kcdT = (m.sb(n, [P, REP, TT, P]) for n in ("kbe", "kd", "u", "kcdT"))
        qe = feat[:, 0:REP, :]
        vnew = m.sb("vnew", [P, REP, P])
        state = m.sb("state", [P, REP, P])
        core2, rstd, fin = negM, T, prod
        A, B, C, E = (m.ps(n, [P, S]) for n in ("A", "B", "C", "E"))
        AB, CE = (A, B), (C, E)
        names = ("w_in taps_in wo_in const_in rows_in egf_in blank projected summed turned_tok turned_feat gram "
                 "turned_m prod_done upd_done turned_u u_done kcd_done kcds_done ds_done mixed var_done y_done "
                 "conv0 feat_ready sz_ready squared rooted feat_kept powered m_kept prod_kept t_kept u_kept kcd_kept "
                 "core_squared core_rooted convolved normed tok_ready dif_ready halves attn_ready t_first u_updated "
                 "vnew_ready state_ready recip scaled added masked eye decb_ready kbe_ready qe_ready fin_ready "
                 "first_state released").split()
        q = {n: m.sem(n) for n in names}
        block = ctx.enter_context(nc.Block())

        def tiles(unit):
            return unit[:].rearrange("p (t n) -> p t n", t=TT)

        def rows_of(c):
            return slice(c * DC, (c + 1) * DC)

        def head_cols(table, i, width=1, at=0):
            return table[:, :, bass.ds(i * REP + at, width)]

        @block.sync
        def _(sp):
            def load(i):
                sp.dma_start(w[:], w_dram[bass.ds(i, 1)].rearrange("a p c k n -> p (a c) k n")).then_inc(q["w_in"], 16)

            def load_taps(i):
                sp.dma_start(taps[:], conv_dram[bass.ds(i, 1)].rearrange("a p b k -> p (a b) k")).then_inc(q["taps_in"], 16)

            def load_rows(i):
                src = rows_dram[bass.ds(i, 1)].rearrange("a c h k x -> (a c) (h k x)")
                src = src.unsqueeze(1).to_broadcast((TC, DC, REP * 2 * TT * DC))
                sp.dma_start(rows[:].rearrange("p h k t l -> p (h k t l)"), src).then_inc(q["rows_in"], 16)

            def load_exp(i):
                src = exp_dram[bass.ds(i * REP, REP), :].rearrange("(a h) s -> a (h s)", a=1).to_broadcast((P, REP * S))
                sp.dma_start(egf[:].rearrange("p h s -> p (h s)"), src).then_inc(q["egf_in"], 16)

            def load_out(i):
                sp.dma_start(wo[:], wo_dram[bass.ds(i, 1)].rearrange("a p h n -> p (a h) n")).then_inc(q["wo_in"], 16)

            load(0)
            load_taps(0)
            load_rows(0)
            for dst, src in ((nw, nw_dram), (mask, mask_dram), (tri, tri_dram)):
                sp.dma_start(dst[:], src).then_inc(q["const_in"], 16)
            load_exp(0)
            load_out(0)
            with sp.Fori(1, KEY_HEADS) as i:
                sp.wait_ge(q["projected"], i * 6)
                load(i)
                sp.wait_ge(q["convolved"], i * 12)
                load_taps(i)
                sp.wait_ge(q["decb_ready"], i * 4)
                load_rows(i)
                sp.wait_ge(q["state_ready"], i * (2 * CHUNKS))
                load_exp(i)
                sp.wait_ge(q["y_done"], i * 2)
                load_out(i)

        @block.tensor
        def _(pe):
            pe.wait_ge(q["blank"], 4)
            with pe.Fori(0, KEY_HEADS) as i:
                def project(n, unit):
                    for h in range(NH2):
                        for c in range(KC):
                            last = nc.tensor.matmul(unit[:, half(h)], w[:, c, n, :], g.xnT[:, c, half(h)],
                                                    start=(c == 0), stop=(c == KC - 1))
                    last.then_inc(q["projected"], 1)

                def turn(unit, src, done):
                    for t in range(TT):
                        last = nc.tensor.transpose(unit[:, tile(t)], src[:, t, :], g.ident[:])
                    last.then_inc(done, 1)

                def feat_v(n):
                    return feat[:, n, :].rearrange("p (t n) -> p t n", t=TT)

                pe.wait_ge(q["w_in"], i * 16 + 16)
                pe.wait_ge(q["added"], i * 2 + 2)
                for n, unit in enumerate((A, B, C, E)):
                    project(n, unit)
                for n in range(REP):
                    pe.wait_ge(q["convolved"], i * 12 + 3 * (n + 1))
                    project(4 + n, AB[n])
                for n in range(2):
                    pe.wait_ge(q["convolved"], i * 12 + 3 * (n + 3))
                    pe.wait_ge(q["feat_ready"], i * 4 + (n + 1))
                    turn(CE[n], feat_v(n), q["turned_tok"])
                pe.wait_ge(q["sz_ready"], i * 2 + 1)
                for n in range(2):
                    pe.wait_ge(q["squared"], i * 2 + (n + 1))
                    for t in range(TT):
                        last = nc.tensor.matmul(A[:, n * TT + t:n * TT + t + 1], square[:, tile(t)], g.ones[:, 0:1],
                                                start=True, stop=True)
                    last.then_inc(q["summed"], 1)
                pe.wait_ge(q["sz_ready"], i * 2 + 2)
                pe.wait_ge(q["feat_ready"], i * 4 + 4)
                turn(B, feat_v(3), q["turned_tok"])
                pe.wait_ge(q["rooted"], i + 1)
                turn(A, feat_v(2), q["turned_tok"])
                for n in range(2):
                    pe.wait_ge(q["tok_ready"], i * 4 + (n + 1))
                    turn(CE[n], tok[:, n], q["turned_feat"])
                pe.wait_ge(q["feat_kept"], i * 2 + 2)
                pe.wait_ge(q["tok_ready"], i * 4 + 4)
                for n, unit in ((1, A), (0, B)):
                    for t in range(TT):
                        last = nc.tensor.matmul(unit[:, tile(t)], turned[:, 1, tile(t)], turned[:, n, tile(t)],
                                                start=True, stop=True)
                    last.then_inc(q["gram"], 1)
                for hd in range(REP):
                    pe.wait_ge(q["halves"], i * 4 + 2 * (hd + 1))
                    turn(CE[hd], negN[:, hd], q["turned_m"])
                pe.wait_ge(q["attn_ready"], i * 4 + 4)
                for lv in range(LEVELS - 1):
                    for hd in range(REP):
                        pe.wait_ge(q["u_updated"], i * (2 * LEVELS) + (2 * lv + hd + 1))
                        if lv == 0:
                            pe.wait_ge(q["m_kept"], i * 2 + (hd + 1))
                            pe.wait_ge(q["t_first"], i * 2 + (hd + 1))
                        for t in range(TT):
                            last = nc.tensor.matmul(CE[hd][:, tile(t)], negM[:, hd, t, :], U[:, hd, t, :],
                                                    start=True, stop=True)
                        last.then_inc(q["prod_done"], 1)
                    for hd in range(REP):
                        pe.wait_ge(q["prod_kept"], i * (2 * LEVELS - 2) + (2 * lv + hd + 1))
                        if lv:
                            pe.wait_ge(q["t_kept"], i * (2 * LEVELS - 4) + (2 * lv + hd - 1))
                        for t in range(TT):
                            last = nc.tensor.matmul(CE[hd][:, tile(t)], T[:, hd, t, :], prod[:, hd, t, :],
                                                    start=True, stop=True)
                        last.then_inc(q["upd_done"], 1)
                    if lv < LEVELS - 2:
                        for hd in range(REP):
                            pe.wait_ge(q["u_updated"], i * (2 * LEVELS) + (2 * lv + hd + 3))
                            turn(AB[hd], U[:, hd], q["turned_u"])
                for hd in range(REP):
                    pe.wait_ge(q["u_updated"], i * (2 * LEVELS) + (2 * LEVELS - 1 + hd))
                    pe.wait_ge(q["kbe_ready"], i * 4 + 4)
                    for t in range(TT):
                        last = nc.tensor.matmul(CE[hd][:, tile(t)], kbe[:, hd, t, :], U[:, hd, t, :],
                                                start=True, stop=True)
                    last.then_inc(q["kcd_done"], 1)
                    for t in range(TT):
                        last = nc.tensor.matmul(AB[hd][:, tile(t)], U[:, hd, t, :], tok[:, 2 + hd, t, :],
                                                start=True, stop=True)
                    last.then_inc(q["u_done"], 1)
                pe.wait_ge(q["u_kept"], i * 2 + 2)
                pe.wait_ge(q["kcd_kept"], i * 2 + 2)
                pe.wait_ge(q["qe_ready"], i * 2 + 2)
                pe.wait_ge(q["first_state"], i + 1)
                for n in range(CHUNKS):
                    own, r, t = slice(n * DC, (n + 1) * DC), rows_of(n % TC), n // TC
                    if n:
                        pe.wait_ge(q["state_ready"], i * (2 * CHUNKS) + 2 * n)
                    for hd in range(REP):
                        last = nc.tensor.matmul(C[r, hd * P:(hd + 1) * P],
                                                kcdT[:, hd, t, (n % TC) * DC:(n % TC + 1) * DC], state[:, hd, :],
                                                start=True, stop=True)
                    last.then_inc(q["kcds_done"], 1)
                    for hd in range(REP):
                        nc.tensor.matmul(AB[hd][:, own], state[:, hd, :],
                                         qe[:, hd, own], start=True, stop=False)
                    pe.wait_ge(q["vnew_ready"], i * CHUNKS + (n + 1))
                    for hd in range(REP):
                        last = nc.tensor.matmul(E[:, hd * P:(hd + 1) * P], kd[r, hd, t, :], vnew[r, hd, :],
                                                start=True, stop=True)
                    last.then_inc(q["ds_done"], 1)
                    for hd in range(REP):
                        last = nc.tensor.matmul(AB[hd][:, own], vnew[r, hd, :], attn[r, hd, t, :],
                                                start=False, stop=True)
                last.then_inc(q["mixed"], 1)
                for hd in range(REP):
                    pe.wait_ge(q["core_squared"], i * 2 + (hd + 1))
                    if hd:
                        pe.wait_ge(q["state_ready"], i * (2 * CHUNKS) + 2 * CHUNKS)
                    for h in range(NH2):
                        last = nc.tensor.matmul(CE[hd][:, half(h)], g.ones[:],
                                                core2[:, hd].rearrange("p t n -> p (t n)")[:, half(h)],
                                                start=True, stop=True)
                    last.then_inc(q["var_done"], 1)
                pe.wait_ge(q["fin_ready"], i * 2 + 2)
                pe.wait_ge(q["wo_in"], i * 16 + 16)
                for c in range(KC):
                    for h in range(NH2):
                        for hd in range(REP):
                            last = nc.tensor.matmul(AB[c][:, half(h)], wo[:, hd, tile(c)],
                                                    fin[:, hd].rearrange("p t n -> p (t n)")[:, half(h)],
                                                    start=(hd == 0), stop=(hd == REP - 1))
                    last.then_inc(q["y_done"], 1)

        @block.scalar
        def _(act):
            act.wait_ge(q["const_in"], 48)
            act.wait_ge(q["blank"], 4)
            with act.Fori(0, KEY_HEADS) as i:
                units = (A, B, C, E)

                def first_tap(n):
                    act.wait_ge(q["projected"], i * 6 + (n + 1))
                    if n >= 2:
                        act.wait_ge(q["feat_ready"], i * 4 + (n - 1))
                    nc.scalar.activation(acc[:, n % 2, :], units[n][:], ACT.Copy, scale=taps[:, n, TAPS - 1:TAPS]
                                         ).then_inc(q["conv0"], 1)

                def silu(n):
                    act.wait_ge(q["convolved"], i * 12 + 3 * (n + 1))
                    nc.scalar.activation(feat[:, n, :], acc[:, n % 2, :], ACT.Silu).then_inc(q["feat_ready"], 1)

                def squares(n):
                    act.wait_ge(q["feat_ready"], i * 4 + (n + 1))
                    if n:
                        act.wait_ge(q["summed"], i * 2 + 1)
                    nc.scalar.activation(square[:], feat[:, n, :], ACT.Square).then_inc(q["squared"], 1)

                act.wait_ge(q["taps_in"], i * 16 + 16)
                first_tap(0)
                first_tap(1)
                silu(0)
                first_tap(2)
                squares(0)
                silu(1)
                first_tap(3)
                act.wait_ge(q["projected"], i * 6 + 5)
                nc.scalar.activation(sz[:, 0, :], A[:], ACT.Silu).then_inc(q["sz_ready"], 1)
                squares(1)
                silu(2)
                act.wait_ge(q["projected"], i * 6 + 6)
                nc.scalar.activation(sz[:, 1, :], B[:], ACT.Silu).then_inc(q["sz_ready"], 1)
                silu(3)
                act.wait_ge(q["summed"], i * 2 + 2)
                nc.scalar.activation(norm[:].rearrange("p a t -> p (a t)"), A[:, 0:2 * TT], ACT.Sqrt
                                     ).then_inc(q["rooted"], 1)
                for hd in range(REP):
                    act.wait_ge(q["masked"], i * 2 + (hd + 1))
                    nc.scalar.activation(dec[:, hd], dec[:, hd], ACT.Exp).then_inc(q["powered"], 1)
                for n in range(2):
                    act.wait_ge(q["turned_feat"], i * 2 + (n + 1))
                    nc.scalar.activation(turned[:, n, :], CE[n][:], ACT.Copy).then_inc(q["feat_kept"], 1)
                for hd in range(REP):
                    act.wait_ge(q["turned_m"], i * 2 + (hd + 1))
                    nc.scalar.activation(negM[:, hd], tiles(CE[hd]), ACT.Copy).then_inc(q["m_kept"], 1)
                for lv in range(LEVELS - 1):
                    for hd in range(REP):
                        act.wait_ge(q["prod_done"], i * (2 * LEVELS - 2) + (2 * lv + hd + 1))
                        nc.scalar.activation(prod[:, hd], tiles(CE[hd]), ACT.Copy).then_inc(q["prod_kept"], 1)
                    if lv < LEVELS - 2:
                        for hd in range(REP):
                            act.wait_ge(q["turned_u"], i * (2 * LEVELS - 4) + (2 * lv + hd + 1))
                            nc.scalar.activation(T[:, hd], tiles(AB[hd]), ACT.Copy).then_inc(q["t_kept"], 1)
                for hd in range(REP):
                    act.wait_ge(q["kcd_done"], i * 2 + (hd + 1))
                    nc.scalar.activation(kcdT[:, hd], tiles(CE[hd]), ACT.Copy).then_inc(q["kcd_kept"], 1)
                    act.wait_ge(q["u_done"], i * 2 + (hd + 1))
                    nc.scalar.activation(u[:, hd], tiles(AB[hd]), ACT.Copy).then_inc(q["u_kept"], 1)
                act.wait_ge(q["mixed"], i + 1)
                for hd in range(REP):
                    nc.scalar.activation(core2[:, hd], tiles(AB[hd]), ACT.Square).then_inc(q["core_squared"], 1)
                for hd in range(REP):
                    act.wait_ge(q["var_done"], i * 2 + (hd + 1))
                    nc.scalar.activation(rstd[:, hd], tiles(CE[hd]), ACT.Sqrt, bias=eps[:, 0:1], scale=1.0 / P
                                         ).then_inc(q["core_rooted"], 1)

        @block.vector
        def _(dve):
            nc.vector.memset(eps[:], DELTA_EPS).then_inc(q["blank"], 1)
            nc.vector.memset(negN[:, 0], 0.0).then_inc(q["blank"], 1)
            nc.vector.memset(negN[:, 1], 0.0).then_inc(q["blank"], 1)
            nc.vector.memset(g.yT[:], 0.0).then_inc(q["blank"], 1)
            dve.sem_inc(q["added"], 2)
            dve.wait_ge(q["const_in"], 48)
            dve.wait_ge(q["blank"], 4)
            with dve.Fori(0, KEY_HEADS) as i:
                units = (A, B, C, E)
                dve.wait_ge(q["rows_in"], i * 16 + 16)
                for hd in range(REP):
                    nc.vector.tensor_tensor(dec[:, hd], rows[:, hd, 0], head_cols(s.cum, i, at=hd).to_broadcast(
                        (P, TT, DC)), ALU.subtract).then_inc(q["dif_ready"], 1)
                dve.wait_ge(q["taps_in"], i * 16 + 16)
                for n in range(4):
                    dve.wait_ge(q["conv0"], i * 4 + (n + 1))
                    conv_taps(nc, dve, q["convolved"], i * 12 + 3 * n, units[n], acc[:, n % 2, :],
                              lambda k: taps[:, n, k:k + 1])
                dve.wait_ge(q["rooted"], i + 1)
                nc.vector.tensor_scalar(norm[:], norm[:], MIN_NORM, None, ALU.max).then_inc(q["normed"], 1)
                dve.wait_ge(q["normed"], i * 3 + 1)
                nc.vector.reciprocal(rnorm[:], norm[:]).then_inc(q["normed"], 1)
                dve.wait_ge(q["normed"], i * 3 + 2)
                nc.vector.tensor_scalar(rnorm[:, 0], rnorm[:, 0], float(DK) ** -0.5, None, ALU.mult
                                        ).then_inc(q["normed"], 1)
                dve.wait_ge(q["normed"], i * 3 + 3)
                for n in range(2):
                    dve.wait_ge(q["turned_tok"], i * 4 + (n + 1))
                    nc.vector.tensor_tensor(tok[:, n], tiles(CE[n]), rnorm[:, n].unsqueeze(2).to_broadcast((P, TT, P)),
                                            ALU.mult).then_inc(q["tok_ready"], 1)
                for n, done in ((1, 3), (0, 4)):
                    dve.wait_ge(q["turned_tok"], i * 4 + done)
                    nc.vector.tensor_tensor(tok[:, 2 + n], tiles(AB[n]), head_cols(s.beta, i, at=n).to_broadcast(
                        (P, TT, P)), ALU.mult).then_inc(q["tok_ready"], 1)
                dve.wait_ge(q["gram"], i * 2 + 1)
                for hd in range(REP):
                    dve.wait_ge(q["decb_ready"], i * 4 + 2 * (hd + 1))
                    for c in range(TC):
                        r = rows_of(c)
                        nc.vector.tensor_tensor(negN[r, hd, :, r], decb[r, hd], tiles(A)[r, :, r], ALU.mult
                                                ).then_inc(q["halves"], 1)
                dve.wait_ge(q["gram"], i * 2 + 2)
                for hd in range(REP):
                    for c in range(TC):
                        r = rows_of(c)
                        nc.vector.tensor_tensor(attn[r, hd], dec[r, hd], tiles(B)[r, :, r], ALU.mult
                                                ).then_inc(q["attn_ready"], 1)

                def level(n):
                    return mask[:, n:n + 1, :].to_broadcast((P, TT, P))

                for hd in range(REP):
                    dve.wait_ge(q["eye"], i * 4 + 2 * (hd + 1))
                    dve.wait_ge(q["halves"], i * 4 + 2 * (hd + 1))
                    dve.wait_ge(q["m_kept"], i * 2 + (hd + 1))
                    dve.sem_inc(q["released"], 1)
                    nc.vector.copy_predicated(T[:, hd], level(LEVELS), tiles(CE[hd])).then_inc(q["t_first"], 1)
                    nc.vector.copy_predicated(U[:, hd], level(0), negN[:, hd]).then_inc(q["u_updated"], 1)
                for lv in range(LEVELS - 1):
                    for hd in range(REP):
                        dve.wait_ge(q["upd_done"], i * (2 * LEVELS - 2) + (2 * lv + hd + 1))
                        dve.sem_inc(q["released"], 1)
                        nc.vector.copy_predicated(U[:, hd], level(lv + 1), tiles(CE[hd])).then_inc(q["u_updated"], 1)
                nc.vector.memset(state[:], 0.0).then_inc(q["first_state"], 1)
                dve.wait_ge(q["u_kept"], i * 2 + 2)
                dve.wait_ge(q["egf_in"], i * 16 + 16)
                dve.wait_ge(q["first_state"], i + 1)
                for n in range(CHUNKS):
                    r, t = rows_of(n % TC), n // TC
                    dve.wait_ge(q["kcds_done"], i * CHUNKS + (n + 1))
                    nc.vector.tensor_tensor(vnew[r], u[r, :, t, :], C[r, 0:REP * P].rearrange("p (h n) -> p h n", h=REP),
                                            ALU.subtract).then_inc(q["vnew_ready"], 1)
                    dve.wait_ge(q["ds_done"], i * CHUNKS + (n + 1))
                    for hd in range(REP):
                        end = (n + 1) * DC - 1
                        nc.vector.scalar_tensor_tensor(out=state[:, hd, :], in0=state[:, hd, :],
                                                       scalar=egf[:, hd, end:end + 1], in1=E[:, hd * P:(hd + 1) * P],
                                                       op0=ALU.mult, op1=ALU.add).then_inc(q["state_ready"], 1)
                    dve.wait_ge(q["state_ready"], i * (2 * CHUNKS) + (2 * n + 2))
                for hd in range(REP):
                    dve.wait_ge(q["core_rooted"], i * 2 + (hd + 1))
                    nc.vector.reciprocal(rstd[:, hd], rstd[:, hd]).then_inc(q["recip"], 1)
                    dve.wait_ge(q["recip"], i * 2 + (hd + 1))
                    dve.wait_ge(q["core_squared"], i * 2 + 2)
                    nc.vector.scalar_tensor_tensor(out=fin[:, hd].rearrange("p t n -> p (t n)"), in0=AB[hd][:],
                                                   scalar=nw[:, 0:1], in1=rstd[:, hd].rearrange("p t n -> p (t n)"),
                                                   op0=ALU.mult, op1=ALU.mult).then_inc(q["scaled"], 1)
                for c in range(KC):
                    dve.wait_ge(q["y_done"], i * 2 + (c + 1))
                    nc.vector.tensor_tensor(g.yT[:, c, :], g.yT[:, c, :], AB[c][:], ALU.add).then_inc(q["added"], 1)

        @block.gpsimd
        def _(pool):
            pool.wait_ge(q["const_in"], 48)
            with pool.Fori(0, KEY_HEADS) as i:
                for hd in range(REP):
                    pool.wait_ge(q["dif_ready"], i * 2 + (hd + 1))
                    nc.gpsimd.tensor_tensor(dec[:, hd], dec[:, hd], tri[:, 0:1, :].to_broadcast((P, TT, DC)), ALU.add
                                            ).then_inc(q["masked"], 1)
                for hd in range(REP):
                    nc.gpsimd.tensor_tensor(decb[:, hd], rows[:, hd, 1], tri[:, 1:2, :].to_broadcast((P, TT, DC)),
                                            ALU.mult).then_inc(q["decb_ready"], 1)
                    pool.wait_ge(q["powered"], i * 2 + (hd + 1))
                    pool.wait_ge(q["decb_ready"], i * 4 + (2 * hd + 1))
                    nc.gpsimd.tensor_tensor(decb[:, hd], decb[:, hd], dec[:, hd], ALU.mult).then_inc(q["decb_ready"], 1)
                for hd in range(REP):
                    for dst in (T, U):
                        nc.gpsimd.tensor_copy(dst[:, hd], g.ident[:].unsqueeze(1).to_broadcast((P, TT, P))
                                              ).then_inc(q["eye"], 1)
                pool.wait_ge(q["tok_ready"], i * 4 + 2)
                for hd in range(REP):
                    for dst, table in ((kbe, s.beg), (kd, s.rest)):
                        nc.gpsimd.tensor_tensor(dst[:, hd], tok[:, 1], head_cols(table, i, at=hd).to_broadcast(
                            (P, TT, P)), ALU.mult).then_inc(q["kbe_ready"], 1)
                pool.wait_ge(q["feat_kept"], i * 2 + 1)
                pool.wait_ge(q["egf_in"], i * 16 + 16)
                for hd in range(REP):
                    nc.gpsimd.tensor_tensor(qe[:, hd, :], turned[:, 0, :], egf[:, hd, :],
                                            ALU.mult).then_inc(q["qe_ready"], 1)
                for hd in range(REP):
                    pool.wait_ge(q["scaled"], i * 2 + (hd + 1))
                    flat = fin[:, hd].rearrange("p t n -> p (t n)")
                    nc.gpsimd.tensor_tensor(flat, flat, sz[:, hd, :], ALU.mult).then_inc(q["fin_ready"], 1)


def delta_stage(nc, g, d):
    rows_dram = nc.dram_tensor("delta_gate_rows", (KEY_HEADS, TC, REP, 2, TT * DC), F32, kind="Internal").ap()
    exp_dram = nc.dram_tensor("delta_gate_exp", (VALUE_HEADS, S), F32, kind="Internal").ap()
    with ExitStack() as ctx:
        m = Scope(nc, ctx, "del")
        s = Shared()
        s.beta, s.cum, s.beg, s.rest = (m.sb(n, [P, TT, VALUE_HEADS]) for n in ("beta", "cum", "beg", "rest"))
        delta_prepare_block(nc, g, s, d["del_ba"], d["del_par"], rows_dram, exp_dram)
        delta_heads_block(nc, g, s, d["del_w"], d["del_taps"], d["del_out"], d["del_nw"], d["del_mask"],
                          d["del_tri"], rows_dram, exp_dram)


STAGES = range(8)
L0_HEAD = 16
MLP, INTER_T, HID = 2048, 768, 128
NEXP = EXP + 1


def program(nc, d, out):
    with ExitStack() as ctx:
        g = Shared()
        m = Scope(nc, ctx, "g")
        g.x = m.sb("x", [P, TT, D])
        g.xnT = m.sb("xnT", [P, KC, S])
        g.yT = m.sb("yT", [P, KC, S])
        g.ident = m.sb("ident", [P, P])
        g.ones = m.sb("ones", [P, P])
        g.zero = m.sb("zero", [P, HALF], BF16)
        start_block(nc, g, d["x"])
        stages = list(STAGES)
        residual_block(nc, g, "res_in", post=False)
        for n in stages:
            scale = None
            if n == 0:
                linear_attention_block(nc, g, "lin", d["l0_w"], d["l0_b"], L0_HEAD)
            if n == 1:
                gated_ffn_block(nc, g, "fp4", FP4, MLP // P // 4, 4, d["fp4_w"], d["fp4_s"])
            if n == 2:
                scale = mamba_stage(nc, g, m, d)
            if n == 3:
                gated_ffn_block(nc, g, "ter", TERNARY, INTER_T // P // 3, 3, d["ter_w"], d["ter_s"])
            if n == 4:
                latent_attention_stage(nc, g, d)
            if n == 5:
                linear_block(nc, g, "ffn2", d["l2_w"], d["l2_s"])
            if n == 6:
                delta_stage(nc, g, d)
            if n == 7:
                score_dram = nc.dram_tensor("scores", (NEXP, S), F32, kind="Internal").ap()
                router_block(nc, g, "route", d["route_w"], score_dram)
                gated_ffn_block(nc, g, "moe", EXPERTS, NEXP // 3, 3, d["moe_w"], score_dram)
            last = n == stages[-1]
            residual_block(nc, g, f"res{n}", pre=not last, token_scale=scale, out=out if last else None)


def kmajor(w):
    return np.ascontiguousarray(np.transpose(w.reshape(w.shape[0], P, KC), (1, 2, 0)))


def kflat(w):
    return np.ascontiguousarray(np.transpose(w.reshape(w.shape[0], -1, P), (2, 1, 0)))


def columns(b):
    return np.ascontiguousarray(b.reshape(-1, P).T)


def ffn_blocks(wg, wu, wd, sg=None, su=None):
    nb = wg.shape[0] // P
    out = np.zeros((nb, P, 6 * P + 2), np.float32)
    for b in range(nb):
        rows = slice(b * P, (b + 1) * P)
        out[b, :, 0:2 * P] = kmajor(wg[rows]).reshape(P, -1)
        out[b, :, 2 * P:4 * P] = kmajor(wu[rows]).reshape(P, -1)
        out[b, :, 4 * P:6 * P] = wd[:, rows].T
        if sg is not None:
            out[b, :, 6 * P], out[b, :, 6 * P + 1] = sg[rows], su[rows]
    return out


def lay_out(v):
    d = {"x": v["L0_attn_x"]}
    d["l0_w"] = np.stack([kmajor(v["L0_attn_Wq"]), kmajor(v["L0_attn_Wk"]), kmajor(v["L0_attn_Wv"]),
                          kflat(v["L0_attn_Wo"])], axis=1)
    d["l0_b"] = np.stack([columns(v[f"L0_attn_b{n}"]) for n in "qkvo"], axis=1)
    pairs = MLP // (2 * P)
    gate, up = (v[f"L0_ffn_{n}_W_packed"].reshape(pairs, P, 2, P).transpose(0, 3, 2, 1).reshape(pairs, P, 2 * P)
                for n in ("gate", "up"))
    down = v["L0_ffn_down_W_packed"].reshape(D, pairs, P).transpose(1, 2, 0)
    d["fp4_w"] = np.concatenate([gate, up, down], axis=2)
    gs, us = (v[f"L0_ffn_{n}_scales"].reshape(pairs, P, 2, 8).transpose(0, 3, 2, 1).reshape(pairs, 8, 2 * P)
              for n in ("gate", "up"))
    ds = v["L0_ffn_down_scales"].reshape(D, pairs, 8).transpose(1, 2, 0)
    d["fp4_s"] = np.concatenate([gs, us, ds], axis=2)
    pad = INTER_T - v["L1_ffn_gate_w"].shape[0]
    rows = ((0, pad), (0, 0))
    d["ter_w"] = ffn_blocks(np.pad(v["L1_ffn_gate_w"], rows), np.pad(v["L1_ffn_up_w"], rows),
                            np.pad(v["L1_ffn_down_w"], ((0, 0), (0, pad))),
                            np.pad(v["L1_ffn_gate_s"], (0, pad)), np.pad(v["L1_ffn_up_s"], (0, pad)))
    d["ter_s"] = columns(v["L1_ffn_down_s"])
    d["l2_w"] = kmajor(v["L2_ffn_weight"])
    d["l2_s"] = np.stack([columns(v["L2_ffn_scale_weight"]), columns(v["L2_ffn_bias"])], axis=1)
    d["route_w"] = kmajor(v["L3_ffn_gate_w"])
    moe = [ffn_blocks(v["L3_ffn_w1"][e], v["L3_ffn_w3"][e], v["L3_ffn_w2"][e]) for e in range(EXP)]
    moe.append(ffn_blocks(v["L3_ffn_ws1"], v["L3_ffn_ws3"], v["L3_ffn_ws2"]))
    d["moe_w"] = np.concatenate(moe, axis=0)
    w_in, cw, cb = v["L1_attn_W_in"], v["L1_attn_conv_w"], v["L1_attn_conv_b"]
    d["mam_gate"] = np.stack([kmajor(w_in[b * P:(b + 1) * P]) for b in range(M_BLOCKS)])
    d["mam_hidden"] = np.stack([kmajor(w_in[M_INNER + b * P:M_INNER + (b + 1) * P]) for b in range(M_BLOCKS)])
    d["mam_shared_w"] = kmajor(w_in[2 * M_INNER:])
    blank = np.zeros(2 * M_N, np.float32)
    par = np.concatenate([cw, cb[:, None], np.concatenate([np.repeat(v["L1_attn_D"], M_P), blank])[:, None],
                          np.concatenate([v["L1_attn_norm_w"], blank])[:, None]], axis=1)
    par = par.reshape(-1, P, PAR).transpose(1, 0, 2)
    d["mam_par"], d["mam_shared_par"] = par[:, :M_BLOCKS], par[:, M_BLOCKS:]
    d["mam_dt"] = np.stack([v["L1_attn_dt_bias"], v["L1_attn_A_log"]], axis=1)
    d["mam_out"] = v["L1_attn_W_out"].T.reshape(M_BLOCKS, P, D)
    qkv, cw, wz = v["L3_attn_W_qkv"], v["L3_attn_conv_w"], v["L3_attn_W_z"]
    nk = KEY_HEADS
    w, taps = [], []
    for h in range(nk):
        blocks = [h, nk + h, 2 * nk + 2 * h, 2 * nk + 2 * h + 1]
        parts = [kmajor(qkv[b * P:(b + 1) * P]) for b in blocks]
        parts += [kmajor(wz[b * P:(b + 1) * P]) for b in (2 * h, 2 * h + 1)]
        w.append(np.stack(parts, axis=2))
        taps.append(np.stack([cw[b * P:(b + 1) * P] for b in blocks], axis=1))
    d["del_w"], d["del_taps"] = np.stack(w), np.stack(taps)
    d["del_ba"] = np.concatenate([kmajor(v["L3_attn_W_a"]), kmajor(v["L3_attn_W_b"])], axis=2)
    d["del_par"] = np.stack([v["L3_attn_dt_bias"], v["L3_attn_A_log"]], axis=1)
    d["del_out"] = v["L3_attn_W_out"].T.reshape(nk, REP, P, D).transpose(0, 2, 1, 3)
    d["del_nw"] = v["L3_attn_norm_w"][:, None]
    j, i = np.arange(P)[:, None], np.arange(P)[None, :]
    levels = [(j // (2 * b) == i // (2 * b)) & ((j // b) % 2 == 0) & ((i // b) % 2 == 1) for b in 2 ** np.arange(LEVELS)]
    levels.append(levels[0].T)
    d["del_mask"] = np.stack(levels, axis=1).astype(np.int32)
    j, i = (np.arange(P) % DC)[:, None], np.arange(DC)[None, :]
    d["del_tri"] = np.stack([np.where(j > i, NEG, 0.0), np.where(j < i, -1.0, 0.0)], axis=1).astype(np.float32)
    w = np.zeros((D, P), np.float32)
    w[:, 0:QL], w[:, KV0:KV0 + KVL] = v["L2_attn_Wq_down"], v["L2_attn_Wkv_down"]
    d["lat_w"] = w.reshape(P, KC, P)
    nw = np.zeros((P, 2), np.float32)
    nw[0:QL, 0], nw[KV0:P, 0] = v["L2_attn_q_norm_w"], v["L2_attn_kv_norm_w"]
    nw[0:KVL, 1], nw[KVL:P, 1] = v["L2_attn_kv_norm_w"], v["L2_attn_kv_norm_w"]
    d["lat_nw"] = nw
    q_up, k_up, v_up = (v[f"L2_attn_W{n}_up"].T.reshape(HEADS // 2, 2, HEAD, -1).transpose(0, 2, 1, 3) for n in "qkv")
    d["mla_wqk"] = np.concatenate([q_up, k_up], axis=3)
    wo = v["L2_attn_Wout"].reshape(HEADS // 2, 2, HEAD, D).transpose(0, 2, 1, 3)
    d["mla_wvo"] = np.concatenate([v_up.reshape(-1, HEAD, 2 * KVL), wo.reshape(-1, HEAD, 2 * D)], axis=2)
    plain = np.concatenate([np.arange(0, ROPE, 2), np.arange(1, ROPE, 2)])
    swapped = np.concatenate([np.arange(1, ROPE, 2), np.arange(0, ROPE, 2)])
    rope = [v[f"L2_attn_W{n}_rope"].reshape(P, KC, HEADS, ROPE)[:, :, :, order]
            for n in "qk" for order in (plain, swapped)]
    rope = np.stack(rope, axis=2).reshape(P, KC, 4, HEADS // 2, 2 * ROPE)
    d["mla_rope"] = rope.transpose(3, 0, 1, 2, 4)
    freq = (1.0 / np.float32(10000.0) ** (np.arange(0, ROPE, 2, dtype=np.float32) / np.float32(ROPE))).astype(np.float32)
    angle = np.outer(freq, np.arange(S, dtype=np.float32)).astype(np.float32)
    cos, sin = np.cos(angle), np.sin(angle)
    d["mla_table"] = np.stack([np.concatenate([cos] * 4), np.concatenate([-sin, sin] * 2)], axis=1)
    return {k: np.ascontiguousarray(a) for k, a in d.items()}


def kernel(**inputs):
    import concourse.bacc as bacc
    from concourse.bass_utils import run_bass_kernel_spmd

    arrays = lay_out({k: np.asarray(a) for k, a in inputs.items()})
    nc = bacc.Bacc("TRN2", target_bir_lowering=False, num_devices=1)
    d = {n: nc.dram_tensor(f"in_{n}", a.shape, mybir.dt.from_np(a.dtype), kind="ExternalInput").ap()
         for n, a in arrays.items()}
    out = nc.dram_tensor("out", arrays["x"].shape, F32, kind="ExternalOutput").ap()
    program(nc, d, out)
    r = run_bass_kernel_spmd(nc, [{f"in_{n}": a for n, a in arrays.items()}], core_ids=[0])
    return r.results[0]["out"]
```

```python
from contextlib import ExitStack

import numpy as np
import concourse.bass as bass
from concourse import mybir

F32 = mybir.dt.float32
BF16 = mybir.dt.bfloat16
I32 = mybir.dt.int32
ALU = mybir.AluOpType
ACT = mybir.ActivationFunctionType
AX = mybir.AxisListType

P = 128
S = 1024
D = 256
TT = S // P
KC = D // P
HALF = 512
NH2 = S // HALF
LN_EPS = 1e-5


def half(h):
    return slice(h * HALF, (h + 1) * HALF)


def tile(t):
    return slice(t * P, (t + 1) * P)


class Shared:
    pass


class Scope:

    def __init__(self, nc, ctx, tag):
        self.nc, self.ctx, self.tag, self.sems = nc, ctx, tag, []
        ctx.callback(self.clear)

    def clear(self):
        if self.sems:
            self.nc.clear_and_free_semaphores(self.sems)
            self.nc.all_engine_barrier()

    def sb(self, name, shape, dt=F32):
        return self.ctx.enter_context(self.nc.sbuf_tensor(f"{self.tag}_{name}", shape, dt))

    def ps(self, name, shape, dt=F32):
        return self.ctx.enter_context(self.nc.psum_tensor(f"{self.tag}_{name}", shape, dt))

    def sem(self, name):
        self.sems.append(self.nc.alloc_semaphore(f"{self.tag}_{name}"))
        return self.sems[-1]


def start_block(nc, g, x_dram):
    with ExitStack() as ctx:
        m = Scope(nc, ctx, "start")
        x_in, blank, made = m.sem("x_in"), m.sem("blank"), m.sem("made")
        block = ctx.enter_context(nc.Block())

        @block.sync
        def _(sp):
            sp.dma_start(g.x[:], x_dram[0].rearrange("(t p) d -> p t d", p=P)).then_inc(x_in, 16)
            sp.wait_ge(x_in, 16)

        @block.gpsimd
        def _(pool):
            nc.gpsimd.memset(g.ident[:], 0.0).then_inc(blank, 1)
            pool.wait_ge(blank, 1)
            nc.gpsimd.affine_select(out=g.ident[:], in_=g.ident[:], compare_op=ALU.not_equal, fill=1.0,
                                    base=0, pattern=[[-1, P]], channel_multiplier=1).then_inc(made, 1)

        @block.vector
        def _(dve):
            nc.vector.memset(g.zero[:], 0.0)
            nc.vector.memset(g.ones[:], 1.0)


def residual_block(nc, g, tag, post=True, pre=True, token_scale=None, out=None):
    with ExitStack() as ctx:
        m = Scope(nc, ctx, tag)
        y_ps = m.ps("y_ps", [P, TT, D])
        xn_ps = m.ps("xn_ps", [P, KC, S])
        stats = m.sb("stats", [P, 2, TT, 6])
        mv = m.sb("mv", [P, 2, TT, 2])
        var = m.sb("var", [P, 2, TT])
        sd = m.sb("sd", [P, 2, TT])
        rstd = m.sb("rstd", [P, 2, TT])
        shift = m.sb("shift", [P, 2, TT])
        eps = m.sb("eps", [P, 1])
        z = m.sb("z", [P, TT, D])
        xn = m.sb("xn", [P, TT, D])
        y_turned, z_ready, x_added = m.sem("y_turned"), m.sem("z_ready"), m.sem("x_added")
        small = [m.sem("small_post"), m.sem("small_pre")]
        got_sd, scaled = m.sem("got_sd"), m.sem("scaled")
        xn_ready, xn_turned, stored = m.sem("xn_ready"), m.sem("xn_turned"), m.sem("stored")
        eps_set = m.sem("eps_set")
        block = ctx.enter_context(nc.Block())

        @block.tensor
        def _(pe):
            if post:
                for t in range(TT):
                    for c in range(KC):
                        last = nc.tensor.transpose(y_ps[:, t, c * P:(c + 1) * P], g.yT[:, c, tile(t)], g.ident[:])
                    last.then_inc(y_turned, 1)
            if pre:
                for t in range(TT):
                    pe.wait_ge(xn_ready, t + 1)
                    for c in range(KC):
                        last = nc.tensor.transpose(xn_ps[:, c, tile(t)], xn[:, t, c:D:KC], g.ident[:])
                    last.then_inc(xn_turned, 1)

        def normalise(dve, n, source, source_ready):
            for t in range(TT):
                if source_ready is not None:
                    dve.wait_ge(source_ready, t + 2 - t % 2)
                nc.vector.bn_stats(stats[:, n, t, :], source[:, t, :]).then_inc(small[n], 1)
            dve.wait_ge(small[n], TT)
            for t in range(TT):
                nc.vector.bn_aggr(mv[:, n, t, :], stats[:, n, t, :]).then_inc(small[n], 1)
            dve.wait_ge(small[n], 2 * TT)
            base = 2 * TT
            if n == 0 and token_scale is not None:
                nc.vector.tensor_tensor(var[:, n, :], mv[:, n, :, 1], token_scale[:], ALU.mult).then_inc(small[n], 1)
                dve.wait_ge(small[n], base + 1)
                nc.vector.tensor_tensor(var[:, n, :], var[:, n, :], token_scale[:], ALU.mult).then_inc(small[n], 1)
            else:
                nc.vector.tensor_copy(var[:, n, :], mv[:, n, :, 1]).then_inc(small[n], 2)
            dve.wait_ge(got_sd, n + (1 if post or n == 0 else 0))
            nc.vector.reciprocal(rstd[:, n, :], sd[:, n, :]).then_inc(small[n], 1)
            dve.wait_ge(small[n], base + 3)
            if n == 0 and token_scale is not None:
                nc.vector.tensor_tensor(rstd[:, n, :], rstd[:, n, :], token_scale[:], ALU.mult).then_inc(small[n], 1)
                dve.wait_ge(small[n], base + 4)
            nc.vector.scalar_tensor_tensor(out=shift[:, n, :], in0=mv[:, n, :, 0], scalar=-1.0,
                                           in1=rstd[:, n, :], op0=ALU.mult, op1=ALU.mult).then_inc(scaled, 1)

        @block.vector
        def _(dve):
            nc.vector.memset(eps[:], LN_EPS).then_inc(eps_set, 1)
            if post:
                normalise(dve, 0, y_ps, y_turned)
                for t in range(TT):
                    dve.wait_ge(z_ready, t + 1)
                    nc.vector.tensor_tensor(g.x[:, t, :], g.x[:, t, :], z[:, t, :], ALU.add).then_inc(x_added, 1)
            if pre:
                normalise(dve, 1, g.x, x_added if post else None)
                dve.wait_ge(scaled, 1 + post)
                for t in range(TT):
                    nc.vector.tensor_scalar(xn[:, t, :], g.x[:, t, :], rstd[:, 1, t:t + 1], shift[:, 1, t:t + 1],
                                            ALU.mult, ALU.add).then_inc(xn_ready, 1)
                dve.wait_ge(xn_turned, TT)
                nc.vector.tensor_copy(g.xnT[:, 1, :], xn_ps[:, 1, :])

        @block.scalar
        def _(act):
            act.wait_ge(eps_set, 1)
            for n, wanted in ((0, post), (1, pre)):
                if not wanted:
                    continue
                act.wait_ge(small[n], 2 * TT + 2)
                nc.scalar.activation(sd[:, n, :], var[:, n, :], ACT.Sqrt, bias=eps[:, 0:1]).then_inc(got_sd, 1)
                if n == 0:
                    act.wait_ge(scaled, 1)
                    for t in range(TT):
                        nc.scalar.activation(z[:, t, :], y_ps[:, t, :], ACT.Identity, bias=shift[:, 0, t:t + 1],
                                             scale=rstd[:, 0, t:t + 1]).then_inc(z_ready, 1)
            if pre:
                act.wait_ge(xn_turned, TT)
                nc.scalar.activation(g.xnT[:, 0, :], xn_ps[:, 0, :], ACT.Copy)

        @block.sync
        def _(sp):
            if out is not None:
                sp.wait_ge(x_added, TT)
                sp.dma_start(out[0].rearrange("(t p) d -> p t d", p=P), g.x[:]).then_inc(stored, 16)
                sp.wait_ge(stored, 16)


def open_sums(nc, g, bank):
    return nc.tensor.matmul(bank, g.zero[:, 0:P], g.zero[:], start=True, stop=True, skip_group_check=True)


def linear_attention_block(nc, g, tag, w_dram, b_dram, head_dim):
    scale = float(head_dim) ** -0.5
    with ExitStack() as ctx:
        m = Scope(nc, ctx, tag)
        w = m.sb("w", [P, 4, KC, D])
        b = m.sb("b", [P, 4, KC])
        qkv_ps = m.ps("qkv_ps", [P, 3, S])
        y_ps = m.ps("y_ps", [P, S])
        low, ex, high, phi = (m.sb(n, [P, 2, S]) for n in ("low", "ex", "high", "phi"))
        kv, total = m.sb("kv", [P, S]), m.sb("total", [P, S])
        ones = m.sb("ones", [P, S])
        context = m.sb("context", [P, KC, S])
        w_in, b_in = m.sem("w_in"), m.sem("b_in")
        projected, low_ready, ex_ready, step = m.sem("projected"), m.sem("low_ready"), m.sem("ex_ready"), m.sem("step")
        ctx_ready, y_ready, y_used = m.sem("ctx_ready"), m.sem("y_ready"), m.sem("y_used")
        block = ctx.enter_context(nc.Block())
        STEPS = 7

        @block.sync
        def _(sp):
            sp.dma_start(b[:], b_dram).then_inc(b_in, 16)
            sp.dma_start(w[:], w_dram).then_inc(w_in, 16)

        @block.tensor
        def _(pe):
            pe.wait_ge(w_in, 16)
            for f in range(KC):
                if f:
                    pe.wait_ge(ctx_ready, f)
                for n in range(3):
                    for h in range(NH2):
                        for c in range(KC):
                            last = nc.tensor.matmul(qkv_ps[:, n, half(h)], w[:, n, c, tile(f)], g.xnT[:, c, half(h)],
                                                    start=(c == 0), stop=(c == KC - 1))
                    last.then_inc(projected, 1)
            pe.wait_ge(ctx_ready, KC)
            for o in range(KC):
                out = y_ps if o == 0 else qkv_ps[:, 0, :]
                for h in range(NH2):
                    for c in range(KC):
                        last = nc.tensor.matmul(out[:, half(h)], w[:, 3, c, tile(o)], context[:, c, half(h)],
                                                start=(c == 0), stop=(c == KC - 1))
                last.then_inc(y_ready, 1)

        @block.vector
        def _(dve):
            nc.vector.memset(ones[:], 1.0).then_inc(step, 1)
            dve.wait_ge(b_in, 16)
            for f in range(KC):
                for n in range(2):
                    dve.wait_ge(projected, 3 * f + n + 1)
                    if f:
                        dve.wait_ge(ex_ready, 2 * f)
                    nc.vector.tensor_scalar(low[:, n, :], qkv_ps[:, n, :], b[:, n, f:f + 1], 0.0,
                                            ALU.add, ALU.min).then_inc(low_ready, 1)
                    nc.vector.tensor_scalar(high[:, n, :], qkv_ps[:, n, :], b[:, n, f:f + 1], 0.0,
                                            ALU.add, ALU.max).then_inc(step, 1)
                done = 1 + STEPS * f + 2
                for n in range(2):
                    dve.wait_ge(ex_ready, 2 * f + n + 1)
                    dve.wait_ge(step, done)
                    nc.vector.tensor_tensor(phi[:, n, :], high[:, n, :], ex[:, n, :], ALU.add).then_inc(step, 1)
                dve.wait_ge(projected, 3 * f + 3)
                dve.wait_ge(step, done + 2)
                nc.vector.scalar_tensor_tensor(out=kv[:], in0=qkv_ps[:, 2, :], scalar=b[:, 2, f:f + 1],
                                               in1=phi[:, 1, :], op0=ALU.add, op1=ALU.mult).then_inc(step, 1)
                dve.wait_ge(step, done + 3)
                nc.vector.tensor_tensor_scan(total[:], ones[:], kv[:], 0.0, ALU.mult, ALU.add).then_inc(step, 1)
                dve.wait_ge(step, done + 4)
                nc.vector.scalar_tensor_tensor(out=context[:, f, :], in0=total[:], scalar=scale, in1=phi[:, 0, :],
                                               op0=ALU.mult, op1=ALU.mult).then_inc(ctx_ready, 1)
                dve.wait_ge(ctx_ready, f + 1)
                dve.sem_inc(step, 1)

        @block.scalar
        def _(act):
            for f in range(KC):
                for n in range(2):
                    act.wait_ge(low_ready, 2 * f + n + 1)
                    if f:
                        act.wait_ge(step, 1 + STEPS * (f - 1) + 4)
                    nc.scalar.activation(ex[:, n, :], low[:, n, :], ACT.Exp).then_inc(ex_ready, 1)
            act.wait_ge(b_in, 16)
            for o in range(KC):
                act.wait_ge(y_ready, o + 1)
                out = y_ps if o == 0 else qkv_ps[:, 0, :]
                nc.scalar.activation(g.yT[:, o, :], out[:, :], ACT.Identity, bias=b[:, 3, o:o + 1])


def linear_block(nc, g, tag, w_dram, sb_dram):
    with ExitStack() as ctx:
        m = Scope(nc, ctx, tag)
        w = m.sb("w", [P, KC, D])
        sb_ = m.sb("sb", [P, 2, KC])
        y_ps = m.ps("y_ps", [P, KC, S])
        w_in, s_in, y_ready = m.sem("w_in"), m.sem("s_in"), m.sem("y_ready")
        block = ctx.enter_context(nc.Block())

        @block.sync
        def _(sp):
            sp.dma_start(w[:], w_dram).then_inc(w_in, 16)
            sp.dma_start(sb_[:], sb_dram).then_inc(s_in, 16)

        @block.tensor
        def _(pe):
            pe.wait_ge(w_in, 16)
            for o in range(KC):
                for h in range(NH2):
                    for c in range(KC):
                        last = nc.tensor.matmul(y_ps[:, o, half(h)], w[:, c, tile(o)], g.xnT[:, c, half(h)],
                                                start=(c == 0), stop=(c == KC - 1))
                last.then_inc(y_ready, 1)

        @block.scalar
        def _(act):
            act.wait_ge(s_in, 16)
            for o in range(KC):
                act.wait_ge(y_ready, o + 1)
                nc.scalar.activation(g.yT[:, o, :], y_ps[:, o, :], ACT.Identity, bias=sb_[:, 1, o:o + 1],
                                     scale=sb_[:, 0, o:o + 1])


FP4, TERNARY, EXPERTS = "fp4", "ternary", "experts"


def gated_ffn_block(nc, g, tag, kind, loops, ring, w_dram, extra_dram):
    U = NH2 * ring
    NV = 6 * P
    pairs = ring // 2
    with ExitStack() as ctx:
        m = Scope(nc, ctx, tag)
        y_ps = m.ps("y_ps", [P, KC, NH2, HALF])
        gate_ps = m.ps("gate_ps", [P, NH2, HALF])
        up_ps = m.ps("up_ps", [P, NH2, HALF])
        acted = m.sb("acted", [P, 2, HALF])
        inner = m.sb("inner", [P, 2, HALF])
        w_in = [m.sem(f"w_in{s}") for s in range(pairs if kind == FP4 else ring)]
        gu_ready, acted_ready, inner_ready = m.sem("gu_ready"), m.sem("acted_ready"), m.sem("inner_ready")
        down_done = m.sem("down_done")
        if kind == FP4:
            packed = m.sb("packed", [P, pairs, NV], I32)
            scales = m.sb("scales", [P, pairs, NV])
            mag = m.sb("mag", [P, 2, NV], I32)
            sign = m.sb("sign", [P, 2, NV], I32)
            t_low, t_high, t_sign = (m.sb(n, [P, 2, NV]) for n in ("t_low", "t_high", "t_sign"))
            wf = m.sb("wf", [P, pairs, 2, NV])
            s_in = [m.sem(f"s_in{s}") for s in range(pairs)]
            unpacked, w_made, w_used = m.sem("unpacked"), m.sem("w_made"), m.sem("w_used")

            def weight(s, what, c):
                if what == 2:
                    return wf[:, s // 2, s % 2, 4 * P + c * P:4 * P + (c + 1) * P]
                return wf[:, s // 2, c, (2 * what + s % 2) * P:(2 * what + s % 2 + 1) * P]
        else:
            wf = m.sb("wf", [P, ring, NV + 2])

            def weight(s, what, c):
                return wf[:, s, (2 * what + c) * P:(2 * what + c + 1) * P]
        if kind == TERNARY:
            out_scale = m.sb("out_scale", [P, KC])
            out_in = m.sem("out_in")
        if kind == EXPERTS:
            score = m.sb("score", [P, ring, S])
            scored = m.sb("scored", [P, 2, HALF])
            up_sb = m.sb("up_sb", [P, 2, HALF])
            e_in = [m.sem(f"e_in{s}") for s in range(ring)]
            scored_ready, up_ready = m.sem("scored_ready"), m.sem("up_ready")
        ps_freed = up_ready if kind == EXPERTS else inner_ready
        block = ctx.enter_context(nc.Block())

        @block.sync
        def _(sp):
            def load(i, s):
                if kind == FP4:
                    at = i * pairs + s
                    sp.dma_start(packed[:, s, :], w_dram[bass.ds(at, 1)].rearrange("a p n -> p (a n)")
                                 ).then_inc(w_in[s], 16)
                    src = extra_dram[bass.ds(at, 1)].rearrange("a b n -> (a b) n")
                    sp.dma_start(scales[:, s, :], src.unsqueeze(1).to_broadcast((8, 16, NV))).then_inc(s_in[s], 16)
                else:
                    at = i * ring + s
                    sp.dma_start(wf[:, s, :], w_dram[bass.ds(at, 1)].rearrange("a p n -> p (a n)")
                                 ).then_inc(w_in[s], 16)
                    if kind == EXPERTS:
                        sp.dma_start(score[:, s, :], extra_dram[bass.ds(at, 1), :].to_broadcast((P, S))
                                     ).then_inc(e_in[s], 16)

            for s in range(len(w_in)):
                load(0, s)
            if kind == TERNARY:
                sp.dma_start(out_scale[:], extra_dram).then_inc(out_in, 16)
            with sp.Fori(1, loops) as i:
                for s in range(len(w_in)):
                    if kind == FP4:
                        sp.wait_ge(w_made, i * pairs + (s + 1 - pairs))
                    else:
                        sp.wait_ge(down_done, i * U + (2 * s + 4 - U))
                    load(i, s)

        @block.tensor
        def _(pe):
            pe.sem_inc(down_done, 2)
            if kind == FP4:
                pe.sem_inc(w_used, pairs)
            for c in range(KC):
                for h in range(NH2):
                    open_sums(nc, g, y_ps[:, c, h, :])

            def gate_up(i, u):
                s, h = (u // NH2) % ring, u % NH2
                if h == 0:
                    if kind == FP4:
                        if s % 2 == 0:
                            pe.wait_ge(w_made, i * pairs + (u // 4 + 1))
                    else:
                        pe.wait_ge(w_in[s], i * 16 + 16 * (1 + u // U))
                pe.wait_ge(ps_freed, i * U + (u + 1))
                for what, ps in ((0, gate_ps), (1, up_ps)):
                    for c in range(KC):
                        last = nc.tensor.matmul(ps[:, h, :], weight(s, what, c), g.xnT[:, c, half(h)],
                                                start=(c == 0), stop=(c == KC - 1))
                last.then_inc(gu_ready, 1)

            def down(i, u):
                s, h = u // NH2, u % NH2
                pe.wait_ge(inner_ready, i * U + (u + (1 if kind == EXPERTS else 3)))
                for c in range(KC):
                    last = nc.tensor.matmul(y_ps[:, c, h, :], weight(s, 2, c), inner[:, u % 2, :],
                                            start=False, stop=True, skip_group_check=True)
                last.then_inc(down_done, 1)
                if kind == FP4 and u % 4 == 3:
                    pe.wait_ge(down_done, i * U + (u + 3))
                    pe.sem_inc(w_used, 1)

            gate_up(0, 0)
            with pe.Fori(0, loops - 1) as i:
                for u in range(U):
                    gate_up(i, u + 1)
                    down(i, u)
            for u in range(U):
                if u + 1 < U:
                    gate_up(loops - 1, u + 1)
                down(loops - 1, u)

        @block.scalar
        def _(act):
            if kind == TERNARY:
                act.wait_ge(out_in, 16)
            with act.Fori(0, loops) as i:
                for u in range(U):
                    s, h = u // NH2, u % NH2
                    if kind == EXPERTS:
                        act.wait_ge(scored_ready, i * U + (u + 1))
                        nc.scalar.activation(acted[:, u % 2, :], scored[:, u % 2, :], ACT.Silu).then_inc(acted_ready, 1)
                        continue
                    act.wait_ge(gu_ready, i * U + (u + 1))
                    if kind == FP4:
                        nc.scalar.activation(acted[:, u % 2, :], gate_ps[:, h, :], ACT.Gelu_apprx_tanh
                                             ).then_inc(acted_ready, 1)
                    else:
                        nc.scalar.activation(acted[:, u % 2, :], gate_ps[:, h, :], ACT.Silu,
                                             scale=wf[:, s, NV:NV + 1]).then_inc(acted_ready, 1)
            act.wait_ge(down_done, loops * U + 2)
            for c in range(KC):
                y = y_ps[:, c].rearrange("p h n -> p (h n)")
                if kind == TERNARY:
                    nc.scalar.activation(g.yT[:, c, :], y, ACT.Identity, scale=out_scale[:, c:c + 1])
                else:
                    nc.scalar.activation(g.yT[:, c, :], y, ACT.Copy)

        @block.vector
        def _(dve):
            dve.sem_inc(ps_freed, 2)

            def unpack(i, s, part):
                at = i * (pairs * 9) + s * 9
                if part == 0:
                    dve.wait_ge(w_in[s], i * 16 + 16)
                    for nib in range(2):
                        nc.vector.tensor_scalar(mag[:, nib, :], packed[:, s, :], 4 * nib, 7,
                                                ALU.logical_shift_right, ALU.bitwise_and).then_inc(unpacked, 1)
                        nc.vector.tensor_scalar(sign[:, nib, :], packed[:, s, :], 4 * nib, 8,
                                                ALU.logical_shift_right, ALU.bitwise_and).then_inc(unpacked, 1)
                if part == 1:
                    dve.wait_ge(unpacked, at + 4)
                    nc.vector.scalar_tensor_tensor(out=t_low[:], in0=mag[:], scalar=4.0, in1=mag[:],
                                                   op0=ALU.max, op1=ALU.add).then_inc(unpacked, 1)
                    nc.vector.tensor_scalar(t_high[:], mag[:], 6.0, 2.0, ALU.max, ALU.mult).then_inc(unpacked, 1)
                    nc.vector.tensor_scalar(t_sign[:], sign[:], -0.125, 0.5, ALU.mult, ALU.add).then_inc(unpacked, 1)
                if part == 2:
                    dve.wait_ge(unpacked, at + 7)
                    nc.vector.scalar_tensor_tensor(out=t_low[:], in0=t_low[:], scalar=-16.0, in1=t_high[:],
                                                   op0=ALU.add, op1=ALU.add).then_inc(unpacked, 1)
                    dve.wait_ge(unpacked, at + 8)
                    nc.vector.tensor_tensor(t_sign[:], t_sign[:], t_low[:], ALU.mult).then_inc(unpacked, 1)
                if part == 3:
                    dve.wait_ge(unpacked, at + 9)
                    dve.wait_ge(s_in[s], i * 16 + 16)
                    dve.wait_ge(w_used, i * pairs + (s + 1))
                    nc.vector.tensor_tensor(wf[:, s], t_sign[:], scales[:, s, :].unsqueeze(1).to_broadcast((P, 2, NV)),
                                            ALU.mult).then_inc(w_made, 1)

            def multiply(i, u):
                s, h = u // NH2, u % NH2
                at = i * U + (u + 1)
                if kind == EXPERTS:
                    dve.wait_ge(gu_ready, at)
                    if h == 0:
                        dve.wait_ge(e_in[s], i * 16 + 16)
                    nc.vector.tensor_tensor(scored[:, u % 2, :], gate_ps[:, h, :], score[:, s, half(h)],
                                            ALU.mult).then_inc(scored_ready, 1)
                    nc.vector.tensor_tensor(up_sb[:, u % 2, :], up_ps[:, h, :], score[:, s, half(h)],
                                            ALU.mult).then_inc(up_ready, 1)
                    dve.wait_ge(up_ready, i * U + (u + 3))
                dve.wait_ge(acted_ready, at)
                dve.wait_ge(down_done, at)
                if kind == TERNARY:
                    nc.vector.scalar_tensor_tensor(out=inner[:, u % 2, :], in0=up_ps[:, h, :],
                                                   scalar=wf[:, s, NV + 1:NV + 2], in1=acted[:, u % 2, :],
                                                   op0=ALU.mult, op1=ALU.mult).then_inc(inner_ready, 1)
                else:
                    up = up_sb[:, u % 2, :] if kind == EXPERTS else up_ps[:, h, :]
                    nc.vector.tensor_tensor(inner[:, u % 2, :], acted[:, u % 2, :], up, ALU.mult
                                            ).then_inc(inner_ready, 1)

            if kind == FP4:
                for part in range(4):
                    unpack(0, 0, part)
                with dve.Fori(0, loops - 1) as i:
                    for u in range(U):
                        multiply(i, u)
                        nxt = u // 4 + 1
                        unpack(i + nxt // pairs, nxt % pairs, u % 4)
                for u in range(U):
                    multiply(loops - 1, u)
                    if u // 4 + 1 < pairs:
                        unpack(loops - 1, u // 4 + 1, u % 4)
            else:
                with dve.Fori(0, loops) as i:
                    for u in range(U):
                        multiply(i, u)


EXP = 8
TOP = 2


def router_block(nc, g, tag, w_dram, score_dram):
    NE = EXP + 1
    with ExitStack() as ctx:
        m = Scope(nc, ctx, tag)
        w = m.sb("w", [P, KC, EXP])
        logit_ps = m.ps("logit_ps", [P, TT, EXP])
        turned_ps = m.ps("turned_ps", [NE, TT, P])
        score = m.sb("score", [P, TT, EXP])
        above = m.sb("above", [P, TT, EXP, EXP])
        tie = m.sb("tie", [P, TT, EXP, EXP])
        lower = m.sb("lower", [P, EXP, EXP])
        rank = m.sb("rank", [P, TT, EXP])
        chosen = m.sb("chosen", [P, TT, NE])
        rows = m.sb("rows", [NE, S])
        w_in, products, sig, low0, low1, step, turned, copied, stored = (
            m.sem(n) for n in ("w_in", "products", "sig", "low0", "low1", "step", "turned", "copied", "stored"))
        block = ctx.enter_context(nc.Block())

        @block.sync
        def _(sp):
            sp.dma_start(w[:], w_dram).then_inc(w_in, 16)
            sp.wait_ge(copied, 1)
            sp.dma_start(score_dram, rows[:]).then_inc(stored, 16)
            sp.wait_ge(stored, 16)

        @block.gpsimd
        def _(pool):
            nc.gpsimd.memset(lower[:], 1.0).then_inc(low0, 1)
            pool.wait_ge(low0, 1)
            nc.gpsimd.affine_select(out=lower[:], in_=lower[:], compare_op=ALU.is_gt, fill=0.0, base=0,
                                    pattern=[[1, EXP], [-1, EXP]], channel_multiplier=0).then_inc(low1, 1)

        @block.tensor
        def _(pe):
            pe.wait_ge(w_in, 16)
            for t in range(TT):
                for c in range(KC):
                    last = nc.tensor.matmul(logit_ps[:, t, :], g.xnT[:, c, tile(t)], w[:, c, :],
                                            start=(c == 0), stop=(c == KC - 1))
            last.then_inc(products, 1)
            pe.wait_ge(step, 7)
            for t in range(TT):
                last = nc.tensor.transpose(turned_ps[:, t, :], chosen[:, t, :], g.ident[:])
            last.then_inc(turned, 1)

        @block.scalar
        def _(act):
            act.wait_ge(products, 1)
            nc.scalar.activation(score[:], logit_ps[:], ACT.Sigmoid).then_inc(sig, 1)

        @block.vector
        def _(dve):
            nc.vector.memset(chosen[:], 1.0).then_inc(step, 1)
            dve.wait_ge(sig, 1)
            other = score[:].unsqueeze(2).to_broadcast((P, TT, EXP, EXP))
            own = score[:].unsqueeze(3).to_broadcast((P, TT, EXP, EXP))
            nc.vector.tensor_tensor(above[:], other, own, ALU.is_gt).then_inc(step, 1)
            nc.vector.tensor_tensor(tie[:], other, own, ALU.is_equal).then_inc(step, 1)
            dve.wait_ge(low1, 1)
            dve.wait_ge(step, 3)
            nc.vector.tensor_tensor(tie[:], tie[:], lower[:].unsqueeze(1).to_broadcast((P, TT, EXP, EXP)),
                                    ALU.mult).then_inc(step, 1)
            dve.wait_ge(step, 4)
            nc.vector.tensor_tensor(above[:], above[:], tie[:], ALU.add).then_inc(step, 1)
            dve.wait_ge(step, 5)
            nc.vector.tensor_reduce(rank[:], above[:], AX.X, ALU.add).then_inc(step, 1)
            dve.wait_ge(step, 6)
            nc.vector.scalar_tensor_tensor(out=chosen[:, :, 0:EXP], in0=rank[:], scalar=TOP - 0.5, in1=score[:],
                                           op0=ALU.is_lt, op1=ALU.mult).then_inc(step, 1)
            dve.wait_ge(turned, 1)
            nc.vector.tensor_copy(rows[:], turned_ps[:].rearrange("e t p -> e (t p)")).then_inc(copied, 1)


def project_out_block(nc, g, tag, hidden, blocks, w_dram):
    RING = 4
    with ExitStack() as ctx:
        m = Scope(nc, ctx, tag)
        w = m.sb("w", [P, RING, D])
        y_ps = m.ps("y_ps", [P, KC, NH2, HALF])
        w_in = [m.sem(f"w_in{s}") for s in range(RING)]
        block_done = m.sem("block_done")
        block = ctx.enter_context(nc.Block())

        @block.sync
        def _(sp):
            def load(i, s):
                sp.dma_start(w[:, s, :], w_dram[bass.ds(i * RING + s, 1)].rearrange("a p n -> p (a n)")
                             ).then_inc(w_in[s], 16)

            for s in range(RING):
                load(0, s)
            with sp.Fori(1, blocks // RING) as i:
                for s in range(RING):
                    sp.wait_ge(block_done, i * RING + (s + 1 - RING))
                    load(i, s)

        @block.tensor
        def _(pe):
            for c in range(KC):
                for h in range(NH2):
                    open_sums(nc, g, y_ps[:, c, h, :])
            with pe.Fori(0, blocks // RING) as i:
                for s in range(RING):
                    pe.wait_ge(w_in[s], i * 16 + 16)
                    for c in range(KC):
                        for h in range(NH2):
                            src = hidden[:, bass.ds(i * RING + s, 1), half(h)].rearrange("p a n -> p (a n)")
                            last = nc.tensor.matmul(y_ps[:, c, h, :], w[:, s, tile(c)], src, start=False, stop=True,
                                                    skip_group_check=True)
                    last.then_inc(block_done, 1)

        @block.scalar
        def _(act):
            act.wait_ge(block_done, blocks)
            nc.scalar.activation(g.yT[:], y_ps[:].rearrange("p c h n -> p c (h n)"), ACT.Copy)


HEADS, HEAD, ROPE = 16, 128, 64
QL, KVL = 48, 64
LAT_EPS = 1e-6
KV0 = 64


def latent_block(nc, g, tag, latT, lat, stack, w_dram, nw_dram):
    parts = ((0, QL), (KV0, KVL))
    with ExitStack() as ctx:
        m = Scope(nc, ctx, tag)
        w = m.sb("w", [P, KC, P])
        nw = m.sb("nw", [P, 2])
        lat_ps = m.ps("lat_ps", [P, TT, P])
        turned_ps = m.ps("turned_ps", [P, S])
        low_ps = m.ps("low_ps", [KVL, S])
        squares = m.sb("squares", [P, P])
        ssq, sd, rstd = (m.sb(n, [P, 2, TT]) for n in ("ssq", "sd", "rstd"))
        eps = m.sb("eps", [P, 1])
        w_in, nw_in, products, summed, rooted, step, scaled, turned = (
            m.sem(n) for n in ("w_in", "nw_in", "products", "summed", "rooted", "step", "scaled", "turned"))
        block = ctx.enter_context(nc.Block())

        @block.sync
        def _(sp):
            sp.dma_start(w[:], w_dram).then_inc(w_in, 16)
            sp.dma_start(nw[:], nw_dram).then_inc(nw_in, 16)

        @block.tensor
        def _(pe):
            pe.wait_ge(w_in, 16)
            for t in range(TT):
                for c in range(KC):
                    last = nc.tensor.matmul(lat_ps[:, t, :], g.xnT[:, c, tile(t)], w[:, c, :],
                                            start=(c == 0), stop=(c == KC - 1))
            last.then_inc(products, 1)
            for t in range(TT):
                pe.wait_ge(scaled, 2 * t + 2)
                last = nc.tensor.transpose(turned_ps[:, tile(t)], lat[:, t, :], g.ident[:])
            last.then_inc(turned, 1)
            for t in range(TT):
                last = nc.tensor.transpose(low_ps[:, tile(t)], lat[:, t, KV0:P], g.ident[:])
            last.then_inc(turned, 1)

        @block.scalar
        def _(act):
            act.wait_ge(products, 1)
            act.wait_ge(step, 1)
            n = 0
            for t in range(TT):
                for k, (at, width) in enumerate(parts):
                    if n:
                        act.wait_ge(summed, n)
                    nc.scalar.activation(squares[:, 0:width], lat_ps[:, t, at:at + width], ACT.Square,
                                         accum_out=ssq[:, k, t:t + 1]).then_inc(summed, 1)
                    n += 1
            act.wait_ge(summed, n)
            for k, (at, width) in enumerate(parts):
                nc.scalar.activation(sd[:, k, :], ssq[:, k, :], ACT.Sqrt, bias=eps[:, 0:1], scale=1.0 / width
                                     ).then_inc(rooted, 1)
            act.wait_ge(turned, 1)
            act.wait_ge(nw_in, 16)
            nc.scalar.activation(latT[:], turned_ps[:], ACT.Copy, scale=nw[:, 0:1])
            for odd in range(2):
                nc.scalar.activation(stack[KV0:P, odd, 0, 1, :], turned_ps[KV0:P, :], ACT.Copy, scale=nw[KV0:P, 1:2])
            act.wait_ge(turned, 2)
            for odd in range(2):
                nc.scalar.activation(stack[0:KVL, odd, 1, 1, :], low_ps[:], ACT.Copy, scale=nw[0:KVL, 1:2])

        @block.vector
        def _(dve):
            nc.vector.memset(eps[:], LAT_EPS).then_inc(step, 1)
            dve.wait_ge(rooted, 2)
            nc.vector.reciprocal(rstd[:], sd[:]).then_inc(step, 1)
            nc.vector.memset(lat[:], 0.0).then_inc(step, 1)
            dve.wait_ge(step, 3)
            for t in range(TT):
                for k, (at, width) in enumerate(parts):
                    nc.vector.tensor_scalar(lat[:, t, at:at + width], lat_ps[:, t, at:at + width],
                                            rstd[:, k, t:t + 1], None, ALU.mult).then_inc(scaled, 1)


def attention_block(nc, g, tag, latT, lat, stack, wqk_dram, wvo_dram, nw_dram, rope_dram, table_dram):
    SCALE = float(HEAD + ROPE) ** -0.5
    PAIRS = HEADS // 2
    NT = 2 * TT
    UA, UR = 4, 4
    UNITS = UA + UR
    UNIT_AT = {n: n for n in range(UA)} | {UA + 1 + 2 * r: UA + r for r in range(UR)}
    with ExitStack() as ctx:
        m = Scope(nc, ctx, tag)
        wqk = m.sb("wqk", [P, 2, QL + KVL])
        wvo = m.sb("wvo", [P, 2 * KVL + 2 * D])
        wr = m.sb("wr", [P, KC, 2, P])
        nw = m.sb("nw", [P, 2])
        table = m.sb("table", [P, 2, S])
        absorb = m.sb("absorb", [QL, 2 * KVL])
        wout = m.sb("wout", [P, PAIRS, D])
        part = m.sb("part", [P, 2, 2, HALF])
        prob = m.sb("prob", [P, 2, S])
        probT = m.sb("probT", [P, 4, TT, P])
        total, inv, top, bias = (m.sb(n, [P, NT]) for n in ("total", "inv", "top", "bias"))
        mixed = m.sb("mixed", [P, PAIRS, S])
        score_ps = m.ps("score_ps", [P, 2, NH2, HALF])
        turned_ps = m.ps("turned_ps", [P, TT, P])
        unit_ps = m.ps("unit_ps", [P, HALF])
        ctx_ps = m.ps("ctx_ps", [P, P])
        wqk_in, wvo_in, wr_in, table_in, nw_in = (m.sem(n) for n in ("wqk_in", "wvo_in", "wr_in", "table_in", "nw_in"))
        projected, act_used, rope_used, rotated = (m.sem(n) for n in ("projected", "act_used", "rope_used", "rotated"))
        scored, maxed, biased, powered, turned, kept = (
            m.sem(n) for n in ("scored", "maxed", "biased", "powered", "turned", "kept"))
        inverted, normed, valued, ctx_stored, y_done = (
            m.sem(n) for n in ("inverted", "normed", "valued", "ctx_stored", "y_done"))
        block = ctx.enter_context(nc.Block())

        def at(j, odd, per_pair, n):
            return j * (2 * per_pair) + (odd * per_pair + n)

        def pairs(eng, steps):
            with eng.Fori(0, PAIRS // 2 - 1) as j:
                for odd in range(2):
                    steps(j, odd, True)
            steps(PAIRS // 2 - 1, 0, True)
            steps(PAIRS // 2 - 1, 1, False)

        @block.sync
        def _(sp):
            def load(i):
                sp.dma_start(wqk[:], wqk_dram[bass.ds(i, 1)].rearrange("a p h n -> p (a h) n")).then_inc(wqk_in, 16)
                sp.dma_start(wvo[:], wvo_dram[bass.ds(i, 1)].rearrange("a p n -> p (a n)")).then_inc(wvo_in, 16)

            def load_rope(i):
                sp.dma_start(wr[:], rope_dram[bass.ds(i, 1)].rearrange("a p c k n -> p (a c) k n")).then_inc(wr_in, 16)

            load(0)
            sp.dma_start(nw[:], nw_dram).then_inc(nw_in, 16)
            load_rope(0)
            sp.dma_start(table[:], table_dram).then_inc(table_in, 16)
            with sp.Fori(1, PAIRS) as i:
                sp.wait_ge(projected, i * UNITS + (2 - UNITS))
                load(i)
                sp.wait_ge(projected, i * UNITS)
                load_rope(i)

        @block.tensor
        def _(pe):
            pe.sem_inc(rope_used, UR)
            pe.sem_inc(valued, 2)
            pe.sem_inc(kept, 1)
            pe.sem_inc(ctx_stored, 1)

            def unit(j, odd, u):
                if u == 0:
                    pe.wait_ge(rope_used, at(j, odd, UR, UR))
                    pe.wait_ge(wqk_in, at(j, odd, 16, 16))
                    for hd in (1, 0):
                        cols = slice((1 - hd) * KVL, (2 - hd) * KVL)
                        last = nc.tensor.matmul(unit_ps[0:QL, cols], wqk[:, hd, 0:QL], wqk[:, hd, QL:], start=True,
                                                stop=True)
                elif u == 1:
                    pe.wait_ge(act_used, at(j, odd, UA, u))
                    pe.wait_ge(wvo_in, at(j, odd, 16, 16))
                    last = nc.tensor.matmul(unit_ps[:], wvo[:, 0:2 * KVL], wvo[:, 2 * KVL:], start=True, stop=True)
                elif u < UA:
                    pe.wait_ge(act_used, at(j, odd, UA, u))
                    last = nc.tensor.matmul(unit_ps[:], absorb[:], latT[0:QL, half(u - 2)], start=True, stop=True)
                else:
                    r = u - UA
                    if r == 0:
                        pe.wait_ge(act_used, at(j, odd, UA, UA))
                        pe.wait_ge(wr_in, at(j, odd, 16, 16))
                    else:
                        pe.wait_ge(rope_used, at(j, odd, UR, UR + r))
                    qk, h = r // 2, r % 2
                    for c in range(KC):
                        last = nc.tensor.matmul(unit_ps[:], wr[:, c, qk, :], g.xnT[:, c, half(h)],
                                                start=(c == 0), stop=(c == KC - 1))
                last.then_inc(projected, 1)

            def scores(j, odd, n):
                if n == 0:
                    pe.wait_ge(rotated, at(j, odd, 8, 14))
                    pe.wait_ge(act_used, at(j, odd, UA, UA))
                hd, t = n % 2, n // 2
                for h in range(NH2):
                    last = nc.tensor.matmul(score_ps[:, n % 2, h, :], stack[:, odd, hd, 0, tile(t)],
                                            stack[:, odd, hd, 1, half(h)], start=True, stop=True)
                last.then_inc(scored, 1)

            def turn(j, odd, n):
                pe.wait_ge(normed, at(j, odd, NT, n + 1))
                pe.wait_ge(kept, at(j, odd, NT, n + 1))
                for k in range(TT):
                    last = nc.tensor.transpose(turned_ps[:, k, :], prob[:, n % 2, tile(k)], g.ident[:])
                last.then_inc(turned, 1)

            def values(j, odd, t):
                pe.wait_ge(kept, at(j, odd, NT, 2 * t + 3))
                pe.wait_ge(ctx_stored, at(j, odd, TT, t + 1))
                for k in range(TT):
                    for hd in range(2):
                        last = nc.tensor.matmul(ctx_ps[hd * KVL:(hd + 1) * KVL, :], lat[:, k, KV0:P],
                                                probT[:, 2 * (t % 2) + hd, k, :], start=(k == 0), stop=(k == TT - 1))
                last.then_inc(valued, 1)

            def steps(j, odd, more):
                nj, nodd = (j, 1) if odd == 0 else (j + 1, 0)
                for n in range(NT):
                    if n + 1 < NT:
                        scores(j, odd, n + 1)
                    if n and n % 2 == 0:
                        values(j, odd, n // 2 - 1)
                    if more and n in UNIT_AT:
                        unit(nj, nodd, UNIT_AT[n])
                    turn(j, odd, n)
                if more:
                    scores(nj, nodd, 0)
                values(j, odd, TT - 1)

            for u in range(UNITS):
                unit(0, 0, u)
            scores(0, 0, 0)
            pairs(pe, steps)
            pe.wait_ge(ctx_stored, PAIRS * TT + 1)
            for c in range(KC):
                for h in range(NH2):
                    for p in range(PAIRS):
                        last = nc.tensor.matmul(score_ps[:, c, h, :], wout[:, p, tile(c)], mixed[:, p, half(h)],
                                                start=(p == 0), stop=(p == PAIRS - 1))
                    last.then_inc(y_done, 1)

        @block.vector
        def _(dve):
            dve.wait_ge(table_in, 16)

            def unit(j, odd, u):
                r = u - UA
                h, quarter = r % 2, ROPE // 2
                dve.wait_ge(projected, at(j, odd, UNITS, u + 1))
                dve.wait_ge(rotated, at(j, odd, 8, 4 * (r // 2) + 2 * h + 4))
                nc.vector.tensor_tensor(part[:, h, 0, :], unit_ps[:], table[:, 0, half(h)], ALU.mult)
                for k in range(P // quarter):
                    src, dst = (slice(x * quarter, (x + 1) * quarter) for x in (k, k ^ 1))
                    last = nc.vector.tensor_tensor(part[dst, h, 1, :], unit_ps[src, :], table[src, 1, half(h)], ALU.mult)
                last.then_inc(rope_used, 1)

            def largest(j, odd, n):
                dve.wait_ge(scored, at(j, odd, NT, n + 1))
                nc.vector.tensor_reduce(top[:, n:n + 1], score_ps[:, n % 2].rearrange("p h n -> p (h n)"), AX.X, ALU.max
                                        ).then_inc(maxed, 1)
                dve.wait_ge(maxed, at(j, odd, NT, n + 1))
                nc.vector.tensor_scalar(bias[:, n:n + 1], top[:, n:n + 1], -SCALE, None, ALU.mult
                                        ).then_inc(biased, 1)

            def normalise(j, odd, n):
                dve.wait_ge(powered, at(j, odd, NT, n + 1))
                nc.vector.reciprocal(inv[:, n:n + 1], total[:, n:n + 1]).then_inc(inverted, 1)
                dve.wait_ge(inverted, at(j, odd, NT, n + 1))
                nc.vector.tensor_scalar(prob[:, n % 2, :], prob[:, n % 2, :], inv[:, n:n + 1], None, ALU.mult
                                        ).then_inc(normed, 1)

            def steps(j, odd, more):
                nj, nodd = (j, 1) if odd == 0 else (j + 1, 0)
                for n in range(NT):
                    normalise(j, odd, n)
                    if n + 1 < NT:
                        largest(j, odd, n + 1)
                    if more and UNIT_AT.get(n, 0) >= UA:
                        unit(nj, nodd, UNIT_AT[n])
                if more:
                    largest(nj, nodd, 0)

            for u in range(UA, UNITS):
                unit(0, 0, u)
            largest(0, 0, 0)
            pairs(dve, steps)

        @block.gpsimd
        def _(pool):
            pool.sem_inc(rotated, 6)
            with pool.Fori(0, PAIRS // 2) as j:
                for odd in range(2):
                    for r in range(4):
                        qk, h = r // 2, r % 2
                        pool.wait_ge(rope_used, at(j, odd, UR, UR + r + 1))
                        for hd in range(2):
                            own = slice(ROPE * hd, ROPE * hd + ROPE)
                            nc.gpsimd.tensor_tensor(stack[own, odd, hd, qk, half(h)], part[own, h, 0, :],
                                                    part[own, h, 1, :], ALU.add).then_inc(rotated, 1)

        @block.scalar
        def _(act):
            act.wait_ge(nw_in, 16)

            def unit(j, odd, u):
                act.wait_ge(projected, at(j, odd, UNITS, u + 1))
                if u == 0:
                    nc.scalar.activation(absorb[:], unit_ps[0:QL, 0:2 * KVL], ACT.Copy).then_inc(act_used, 1)
                elif u == 1:
                    for hd in range(2):
                        own = slice(hd * KVL, (hd + 1) * KVL)
                        last = nc.scalar.activation(wout[own, bass.ds(j * 2 + odd, 1), :],
                                                    unit_ps[own, hd * D:(hd + 1) * D].unsqueeze(1), ACT.Copy,
                                                    scale=nw[own, 1:2])
                    last.then_inc(act_used, 1)
                else:
                    for hd in range(2):
                        own = slice((1 - hd) * KVL, (2 - hd) * KVL)
                        last = nc.scalar.activation(stack[own, odd, hd, 0, half(u - 2)], unit_ps[own, :], ACT.Copy)
                    last.then_inc(act_used, 1)

            def power(j, odd, n):
                act.wait_ge(biased, at(j, odd, NT, n + 1))
                if n >= 2:
                    act.wait_ge(turned, at(j, odd, NT, n - 1))
                nc.scalar.activation(prob[:, n % 2, :], score_ps[:, n % 2].rearrange("p h n -> p (h n)"), ACT.Exp,
                                     bias=bias[:, n:n + 1], scale=SCALE, accum_out=total[:, n:n + 1]
                                     ).then_inc(powered, 1)

            def keep(j, odd, n):
                act.wait_ge(turned, at(j, odd, NT, n + 1))
                act.wait_ge(valued, at(j, odd, TT, n // 2 + 1))
                nc.scalar.activation(probT[:, n % 4], turned_ps[:], ACT.Copy).then_inc(kept, 1)

            def store(j, odd, t):
                act.wait_ge(valued, at(j, odd, TT, t + 3))
                nc.scalar.activation(mixed[:, bass.ds(j * 2 + odd, 1), tile(t)], ctx_ps[:].unsqueeze(1),
                                     ACT.Copy).then_inc(ctx_stored, 1)

            def steps(j, odd, more):
                nj, nodd = (j, 1) if odd == 0 else (j + 1, 0)
                for n in range(NT):
                    if n + 1 < NT:
                        power(j, odd, n + 1)
                    if more and n < UA:
                        unit(nj, nodd, n)
                    keep(j, odd, n)
                    if n and n % 2 == 0:
                        store(j, odd, n // 2 - 1)
                if more:
                    act.wait_ge(turned, at(j, odd, NT, NT))
                    power(nj, nodd, 0)
                store(j, odd, TT - 1)

            for u in range(UA):
                unit(0, 0, u)
            power(0, 0, 0)
            pairs(act, steps)
            for c in range(KC):
                for h in range(NH2):
                    act.wait_ge(y_done, NH2 * c + h + 1)
                    nc.scalar.activation(g.yT[:, c, half(h)], score_ps[:, c, h, :], ACT.Copy)


def latent_attention_stage(nc, g, d):
    with ExitStack() as ctx:
        m = Scope(nc, ctx, "mla")
        latT, lat = m.sb("latT", [P, S]), m.sb("lat", [P, TT, P])
        stack = m.sb("stack", [P, 2, 2, 2, S])
        latent_block(nc, g, "latent", latT, lat, stack, d["lat_w"], d["lat_nw"])
        attention_block(nc, g, "attn", latT, lat, stack, d["mla_wqk"], d["mla_wvo"], d["lat_nw"], d["mla_rope"],
                        d["mla_table"])


M_HEADS, M_P, M_N, M_CHUNK, TAPS = 64, 64, 128, 32, 4
M_INNER = M_HEADS * M_P
M_BLOCKS = M_INNER // P
NC = P // M_CHUNK
NORM_EPS = 1e-5
NEG = -1e30
PAR = TAPS + 3


def conv_taps(nc, dve, done, base, ps, acc, tap):
    for k in range(1, TAPS):
        if k > 1:
            dve.wait_ge(done, base + (k - 1))
        nc.vector.scalar_tensor_tensor(out=acc[:, k:S], in0=ps[:, 0:S - k], scalar=tap(TAPS - 1 - k),
                                       in1=acc[:, k:S], op0=ALU.mult, op1=ALU.add).then_inc(done, 1)


def mamba_prepare_block(nc, g, s, w_dram, par_dram, dt_dram, spread_dram):
    with ExitStack() as ctx:
        m = Scope(nc, ctx, "mprep")
        w = m.sb("w", [P, KC, 2 * P + M_HEADS])
        par = m.sb("par", [P, 2, PAR])
        dtp = m.sb("dtp", [M_HEADS, 2])
        bc_ps = m.ps("bc_ps", [P, 2, S])
        dt_ps = m.ps("dt_ps", [M_HEADS, S])
        turned_ps = m.ps("turned_ps", [P, 2, HALF])
        acc, bcT = m.sb("acc", [P, 2, S]), m.sb("bcT", [P, 2, S])
        x, neg, soft, dt, keep, adt, cum, last_, dec = (
            m.sb(n, [M_HEADS, S]) for n in ("x", "neg", "soft", "dt", "keep", "adt", "cum", "last", "dec"))
        a = m.sb("a", [M_HEADS, 1])
        spread = m.sb("spread", [M_HEADS, 2, NC, TT, M_CHUNK])
        w_in, par_in, dtp_in, kept, products, conv0, conv, silu = (
            m.sem(n) for n in ("w_in", "par_in", "dtp_in", "kept", "products", "conv0", "conv", "silu"))
        v_step, a_step, turned, spread_ready, spread_out, gc_ready, mask0 = (
            m.sem(n) for n in ("v_step", "a_step", "turned", "spread_ready", "spread_out", "gc_ready", "mask0"))
        block = ctx.enter_context(nc.Block())

        @block.sync
        def _(sp):
            sp.dma_start(w[:], w_dram).then_inc(w_in, 16)
            sp.dma_start(par[:], par_dram).then_inc(par_in, 16)
            sp.dma_start(dtp[:], dt_dram).then_inc(dtp_in, 16)
            sp.wait_ge(spread_ready, 2)
            for k in range(2):
                for hd in range(2):
                    sp.dma_start(spread_dram[:, :, k, hd, :],
                                 spread[hd:M_HEADS:2, k].rearrange("h c t l -> h c (t l)")).then_inc(spread_out, 16)
            sp.wait_ge(spread_out, 64)

        @block.gpsimd
        def _(pool):
            nc.gpsimd.memset(s.causal[:], 0.0).then_inc(mask0, 1)
            nc.gpsimd.memset(s.w_diag[:], 0.0).then_inc(mask0, 1)
            nc.gpsimd.memset(s.square_sum[:], 0.0).then_inc(mask0, 1)
            for c in range(NC):
                pool.wait_ge(mask0, 3 + c)
                own = s.causal[c * M_CHUNK:(c + 1) * M_CHUNK, :]
                nc.gpsimd.affine_select(out=own, in_=own, compare_op=ALU.is_ge, fill=NEG, base=0,
                                        pattern=[[1, M_CHUNK]], channel_multiplier=-1).then_inc(mask0, 1)

        @block.tensor
        def _(pe):
            pe.wait_ge(w_in, 16)
            for h in range(NH2):
                for c in range(KC):
                    last = nc.tensor.matmul(dt_ps[:, half(h)], w[:, c, 2 * P:], g.xnT[:, c, half(h)],
                                            start=(c == 0), stop=(c == KC - 1))
            last.then_inc(products, 1)
            for n in range(2):
                for h in range(NH2):
                    for c in range(KC):
                        last = nc.tensor.matmul(bc_ps[:, n, half(h)], w[:, c, tile(n)], g.xnT[:, c, half(h)],
                                                start=(c == 0), stop=(c == KC - 1))
                last.then_inc(products, 1)
            small = M_HEADS
            pe.wait_ge(v_step, 4)
            for n, src in enumerate((dt, cum)):
                for t in range(TT):
                    last = nc.tensor.transpose(turned_ps[:, n, t * small:(t + 1) * small], src[:, tile(t)],
                                               g.ident[0:small, 0:small])
                last.then_inc(turned, 1)
            pe.wait_ge(a_step, 5)
            pe.wait_ge(gc_ready, 1)
            for t in range(TT):
                last = nc.tensor.transpose(turned_ps[:, 0, t * small:(t + 1) * small], dec[:, tile(t)],
                                           g.ident[0:small, 0:small])
            last.then_inc(turned, 1)
            pe.wait_ge(silu, 2)
            for t in range(TT):
                last = nc.tensor.matmul(bc_ps[:, 0, tile(t)], bcT[:, 0, tile(t)], bcT[:, 1, tile(t)],
                                        start=True, stop=True)
            last.then_inc(turned, 1)

        @block.scalar
        def _(act):
            act.wait_ge(products, 1)
            act.wait_ge(dtp_in, 16)
            nc.scalar.activation(x[:], dt_ps[:], ACT.Identity, bias=dtp[:, 0:1]).then_inc(a_step, 1)
            act.wait_ge(v_step, 1)
            nc.scalar.activation(soft[:], neg[:], ACT.Exp).then_inc(a_step, 1)
            nc.scalar.activation(a[:], dtp[:, 1:2], ACT.Exp).then_inc(a_step, 1)
            act.wait_ge(a_step, 3)
            nc.scalar.activation(soft[:], soft[:], ACT.Ln, bias=1.0).then_inc(a_step, 1)
            act.wait_ge(v_step, 4)
            cum_v = cum[:].rearrange("h (t c l) -> h c t l", t=TT, c=NC)
            for c in range(NC):
                nc.scalar.activation(spread[:, 0, c], cum_v[:, c], ACT.Copy)
                last = nc.scalar.activation(spread[:, 1, c], cum_v[:, c], ACT.Exp)
            last.then_inc(spread_ready, 2)
            act.wait_ge(v_step, 5)
            nc.scalar.activation(dec[:], last_[:], ACT.Exp).then_inc(a_step, 1)
            act.wait_ge(par_in, 16)
            for n in range(2):
                act.wait_ge(products, 2 + n)
                nc.scalar.activation(acc[:, n, :], bc_ps[:, n, :], ACT.Identity, bias=par[:, n, TAPS:TAPS + 1],
                                     scale=par[:, n, TAPS - 1:TAPS]).then_inc(conv0, 1)
            for n in range(2):
                act.wait_ge(conv, 3 * n + 3)
                nc.scalar.activation(bcT[:, n, :], acc[:, n, :], ACT.Silu).then_inc(silu, 1)

        @block.vector
        def _(dve):
            nc.vector.memset(keep[:], 1.0).then_inc(kept, 1)
            dve.wait_ge(kept, 1)
            nc.vector.memset(keep[:, 0:S:M_CHUNK], 0.0).then_inc(kept, 1)
            dve.wait_ge(a_step, 1)
            nc.vector.scalar_tensor_tensor(out=neg[:], in0=x[:], scalar=-1.0, in1=x[:], op0=ALU.mult, op1=ALU.min
                                           ).then_inc(v_step, 1)
            dve.wait_ge(a_step, 4)
            nc.vector.scalar_tensor_tensor(out=dt[:], in0=x[:], scalar=0.0, in1=soft[:], op0=ALU.max, op1=ALU.add
                                           ).then_inc(v_step, 1)
            dve.wait_ge(v_step, 2)
            nc.vector.tensor_scalar(dt[:], dt[:], 0.0, None, ALU.max).then_inc(v_step, 1)
            nc.vector.tensor_scalar(a[:], a[:], -1.0, None, ALU.mult).then_inc(kept, 1)
            dve.wait_ge(v_step, 3)
            dve.wait_ge(kept, 3)
            nc.vector.tensor_scalar(adt[:], dt[:], a[:, 0:1], None, ALU.mult).then_inc(kept, 1)
            dve.wait_ge(kept, 4)
            nc.vector.tensor_tensor_scan(cum[:], keep[:], adt[:], 0.0, ALU.mult, ALU.add).then_inc(v_step, 1)
            dve.wait_ge(v_step, 4)
            cum_v = cum[:].rearrange("h (c l) -> h c l", l=M_CHUNK)
            end = cum_v[:, :, M_CHUNK - 1:M_CHUNK].to_broadcast((M_HEADS, S // M_CHUNK, M_CHUNK))
            nc.vector.tensor_tensor(last_[:].rearrange("h (c l) -> h c l", l=M_CHUNK), end, cum_v, ALU.subtract
                                    ).then_inc(v_step, 1)
            dve.wait_ge(par_in, 16)
            for n in range(2):
                dve.wait_ge(conv0, n + 1)
                conv_taps(nc, dve, conv, 3 * n, bc_ps[:, n, :], acc[:, n, :], lambda k: par[:, n, k:k + 1])
            dve.wait_ge(turned, 1)
            nc.vector.tensor_copy(s.dt[:].rearrange("p t h -> p (t h)"), turned_ps[:, 0, :]).then_inc(gc_ready, 1)
            dve.wait_ge(turned, 2)
            nc.vector.tensor_copy(s.cum[:].rearrange("p t h -> p (t h)"), turned_ps[:, 1, :])
            dve.wait_ge(turned, 3)
            nc.vector.tensor_copy(s.decay[:].rearrange("p t h -> p (t h)"), turned_ps[:, 0, :])
            dve.wait_ge(turned, 4)
            for c in range(NC):
                own = slice(c * M_CHUNK, (c + 1) * M_CHUNK)
                nc.vector.tensor_copy(s.gram[own], bc_ps[own, 0, :].rearrange("p (t n) -> p t n", t=TT)[:, :, own])


def mamba_heads_block(nc, g, s, hidden, wg_dram, wh_dram, par_dram, spread_dram):
    with ExitStack() as ctx:
        m = Scope(nc, ctx, "mamba")
        wg, wh = m.sb("wg", [P, KC, P]), m.sb("wh", [P, KC, P])
        par = m.sb("par", [P, M_BLOCKS, PAR])
        ae = m.sb("ae", [P, 2, 2, TT, M_CHUNK])
        dif, ed = m.sb("dif", [P, 2, TT, M_CHUNK]), m.sb("ed", [P, 2, TT, M_CHUNK])
        acc, sg = (m.sb(n, [P, S]) for n in ("acc", "sg"))
        hT = m.sb("hT", [P, 2, S])
        yf, square = g.yT[:, 0, :], g.yT[:, 1, :]
        hdt = m.sb("hdt", [P, TT, P])
        h_ps, gate_ps, y_ps = (m.ps(n, [P, S]) for n in ("h_ps", "gate_ps", "y_ps"))
        turned_ps = m.ps("turned_ps", [P, TT, P])
        wg_in, wh_in, ae_in, par_in = (m.sem(n) for n in ("wg_in", "wh_in", "ae_in", "par_in"))
        h_done, y_done, gate_done, turned = (m.sem(n) for n in ("h_done", "y_done", "gate_done", "turned"))
        conv0, h_ready, g_ready, powered, kept = (m.sem(n) for n in ("conv0", "h_ready", "g_ready", "powered", "kept"))
        conv, diffed, summed, quad_v, added, gated, hdt_ready = (
            m.sem(n) for n in ("conv", "diffed", "summed", "quad_v", "added", "gated", "hdt_ready"))
        masked, decayed, quad_p, squared = (m.sem(n) for n in ("masked", "decayed", "quad_p", "squared"))
        block = ctx.enter_context(nc.Block())

        def own_par(i, k):
            return par[:, bass.ds(i, 1), k:k + 1].rearrange("p a b -> p (a b)")

        def quad(i, c, engine):
            q = slice(c * M_CHUNK, (c + 1) * M_CHUNK)
            return engine.tensor_tensor(s.w_diag[q, :, :, q], dif[q], s.gram[q].unsqueeze(1).to_broadcast(
                (M_CHUNK, 2, TT, M_CHUNK)), ALU.mult)

        def steps(eng, step):
            step(0, 0, 0, False)
            step(1, 1, 1, False)
            with eng.Fori(1, M_BLOCKS // 2 - 1) as j:
                for n in range(2):
                    step(j * 2 + n, n, 2, False)
            step(M_BLOCKS - 2, 0, 2, False)
            step(M_BLOCKS - 1, 1, 2, True)

        @block.sync
        def _(sp):
            def load_h(i):
                sp.dma_start(wh[:], wh_dram[bass.ds(i, 1)].rearrange("a p c n -> p (a c) n")).then_inc(wh_in, 16)

            def load_g(i):
                sp.dma_start(wg[:], wg_dram[bass.ds(i, 1)].rearrange("a p c n -> p (a c) n")).then_inc(wg_in, 16)

            def load_ae(i):
                src = spread_dram[bass.ds(i, 1)].rearrange("a c k h x -> (a c) (k h x)")
                src = src.unsqueeze(1).to_broadcast((NC, M_CHUNK, 4 * TT * M_CHUNK))
                sp.dma_start(ae[:].rearrange("p k h t l -> p (k h t l)"), src).then_inc(ae_in, 16)

            load_h(0)
            sp.dma_start(par[:], par_dram).then_inc(par_in, 16)
            load_ae(0)
            load_g(0)
            with sp.Fori(1, M_BLOCKS) as i:
                sp.wait_ge(h_done, i)
                load_h(i)
                sp.wait_ge(diffed, i)
                sp.wait_ge(decayed, i)
                load_ae(i)
                sp.wait_ge(gate_done, i)
                load_g(i)

        @block.tensor
        def _(pe):
            def project(i, w, w_in, ps, done):
                pe.wait_ge(w_in, i * 16 + 16)
                for h in range(NH2):
                    for c in range(KC):
                        last = nc.tensor.matmul(ps[:, half(h)], w[:, c, :], g.xnT[:, c, half(h)],
                                                start=(c == 0), stop=(c == KC - 1))
                last.then_inc(done, 1)

            def mix(i):
                pe.wait_ge(hdt_ready, i + 1)
                pe.wait_ge(quad_v, i * 2 + 2)
                pe.wait_ge(quad_p, i * 2 + 2)
                for hd in range(2):
                    for t in range(TT):
                        last = nc.tensor.matmul(y_ps[hd * M_P:(hd + 1) * M_P, tile(t)],
                                                hdt[:, t, hd * M_P:(hd + 1) * M_P], s.w_diag[:, hd, t, :],
                                                start=True, stop=True)
                last.then_inc(y_done, 1)

            def turn(i, parity):
                pe.wait_ge(h_ready, i + 1)
                for t in range(TT):
                    last = nc.tensor.transpose(turned_ps[:, t, :], hT[:, parity, tile(t)], g.ident[:])
                last.then_inc(turned, 1)

            def step(i, parity, behind, last):
                first = behind == 0
                if not last:
                    pe.wait_ge(conv, i * 3 + 3)
                    project(i + 1, wh, wh_in, h_ps, h_done)
                if not first:
                    pe.wait_ge(added, i)
                    mix(i - 1)
                    pe.wait_ge(g_ready, i)
                project(i, wg, wg_in, gate_ps, gate_done)
                turn(i, parity)

            project(0, wh, wh_in, h_ps, h_done)
            steps(pe, step)
            pe.wait_ge(added, M_BLOCKS)
            mix(M_BLOCKS - 1)

        @block.scalar
        def _(act):
            def first_tap(i):
                act.wait_ge(h_done, i + 1)
                nc.scalar.activation(acc[:], h_ps[:], ACT.Identity, bias=own_par(i, TAPS),
                                     scale=own_par(i, TAPS - 1)).then_inc(conv0, 1)

            def keep(i):
                act.wait_ge(gated, i + 1)
                act.wait_ge(squared, i + 1)
                nc.scalar.activation(square, yf, ACT.Square).then_inc(kept, 1)
                nc.scalar.activation(hidden[:, bass.ds(i, 1), :].rearrange("p a n -> p (a n)"), yf, ACT.Copy,
                                     scale=own_par(i, TAPS + 2)).then_inc(kept, 1)

            def step(i, parity, behind, last):
                first = behind == 0
                act.wait_ge(conv, i * 3 + 3)
                if not first:
                    act.wait_ge(added, i)
                nc.scalar.activation(hT[:, parity, :], acc[:], ACT.Silu).then_inc(h_ready, 1)
                if not last:
                    act.wait_ge(h_ready, i + 1)
                    first_tap(i + 1)
                if behind == 2:
                    keep(i - 2)
                act.wait_ge(masked, i + 1)
                nc.scalar.activation(dif[:], dif[:], ACT.Exp).then_inc(powered, 1)
                if not first:
                    act.wait_ge(gated, i)
                act.wait_ge(gate_done, i + 1)
                nc.scalar.activation(sg[:], gate_ps[:], ACT.Silu).then_inc(g_ready, 1)

            act.wait_ge(par_in, 16)
            first_tap(0)
            steps(act, step)
            keep(M_BLOCKS - 2)
            keep(M_BLOCKS - 1)

        @block.vector
        def _(dve):
            def convolve(i):
                dve.wait_ge(conv0, i + 1)
                conv_taps(nc, dve, conv, i * 3, h_ps, acc, lambda k: own_par(i, k))

            def add_skip(i, parity):
                dve.wait_ge(y_done, i + 1)
                dve.wait_ge(kept, i * 2 + 2)
                nc.vector.scalar_tensor_tensor(out=yf, in0=hT[:, parity, :], scalar=own_par(i, TAPS + 1),
                                               in1=y_ps[:], op0=ALU.mult, op1=ALU.add).then_inc(added, 1)

            def gate(i):
                dve.wait_ge(added, i + 2)
                dve.wait_ge(g_ready, i + 1)
                nc.vector.tensor_tensor(yf, yf, sg[:], ALU.mult).then_inc(gated, 1)

            def token_major(i):
                dve.wait_ge(turned, i + 1)
                own = s.dt[:, :, bass.ds(i * 2, 2)].unsqueeze(3).to_broadcast((P, TT, 2, M_P))
                nc.vector.tensor_tensor(hdt[:].rearrange("p t (h n) -> p t h n", h=2),
                                        turned_ps[:].rearrange("p t (h n) -> p t h n", h=2), own, ALU.mult
                                        ).then_inc(hdt_ready, 1)

            def step(i, parity, behind, last):
                first = behind == 0
                dve.wait_ge(ae_in, i * 16 + 16)
                if not first:
                    dve.wait_ge(quad_p, i * 2)
                    dve.wait_ge(quad_v, i * 2)
                own = s.cum[:, :, bass.ds(i * 2, 2)].rearrange("p t h -> p h t").unsqueeze(3)
                nc.vector.tensor_tensor(dif[:], ae[:, 0], own.to_broadcast((P, 2, TT, M_CHUNK)), ALU.subtract
                                        ).then_inc(diffed, 1)
                if not last:
                    convolve(i + 1)
                if not first:
                    add_skip(i - 1, 1 - parity)
                dve.wait_ge(powered, i + 1)
                dve.wait_ge(decayed, i + 1)
                nc.vector.tensor_tensor(dif[:], dif[:], ed[:], ALU.add).then_inc(summed, 1)
                dve.wait_ge(summed, i + 1)
                if not first:
                    dve.wait_ge(y_done, i)
                for c in range(0, NC, 2):
                    quad(i, c, nc.vector).then_inc(quad_v, 1)
                if not first:
                    gate(i - 1)
                token_major(i)

            dve.wait_ge(par_in, 16)
            dve.sem_inc(added, 1)
            dve.sem_inc(kept, 2)
            convolve(0)
            steps(dve, step)
            add_skip(M_BLOCKS - 1, 1)
            gate(M_BLOCKS - 1)

        @block.gpsimd
        def _(pool):
            def build(i, first):
                pool.wait_ge(diffed, i + 1)
                nc.gpsimd.tensor_tensor(dif[:], dif[:], s.causal[:].unsqueeze(1).unsqueeze(1).to_broadcast(
                    (P, 2, TT, M_CHUNK)), ALU.add).then_inc(masked, 1)
                if not first:
                    pool.wait_ge(summed, i)
                own = s.decay[:, :, bass.ds(i * 2, 2)].rearrange("p t h -> p h t").unsqueeze(3)
                nc.gpsimd.tensor_tensor(ed[:], ae[:, 1], own.to_broadcast((P, 2, TT, M_CHUNK)), ALU.mult
                                        ).then_inc(decayed, 1)
                pool.wait_ge(summed, i + 1)
                if not first:
                    pool.wait_ge(y_done, i)
                pool.wait_ge(decayed, i + 1)
                quad(i, 1, nc.gpsimd).then_inc(quad_p, 1)
                pool.wait_ge(quad_p, i * 2 + 1)
                quad(i, 3, nc.gpsimd).then_inc(quad_p, 1)
                pool.wait_ge(quad_p, i * 2 + 2)

            def add_squares(i):
                pool.wait_ge(kept, i * 2 + 3)
                pool.wait_ge(squared, i + 1)
                nc.gpsimd.tensor_tensor(s.square_sum[:], s.square_sum[:], square, ALU.add).then_inc(squared, 1)

            pool.sem_inc(squared, 1)
            build(0, True)
            build(1, False)
            with pool.Fori(2, M_BLOCKS) as i:
                build(i, False)
                add_squares(i - 2)
            add_squares(M_BLOCKS - 2)
            add_squares(M_BLOCKS - 1)


def mamba_norm_block(nc, g, s, token_scale):
    with ExitStack() as ctx:
        m = Scope(nc, ctx, "mnorm")
        sum_ps = m.ps("sum_ps", [P, TT])
        eps, sd = m.sb("eps", [P, 1]), m.sb("sd", [P, TT])
        summed, eps_set, rooted = m.sem("summed"), m.sem("eps_set"), m.sem("rooted")
        block = ctx.enter_context(nc.Block())

        @block.tensor
        def _(pe):
            for t in range(TT):
                last = nc.tensor.matmul(sum_ps[:, t:t + 1], s.square_sum[:, tile(t)], g.ones[:, 0:1],
                                        start=True, stop=True)
            last.then_inc(summed, 1)

        @block.scalar
        def _(act):
            act.wait_ge(eps_set, 1)
            act.wait_ge(summed, 1)
            nc.scalar.activation(sd[:], sum_ps[:], ACT.Sqrt, bias=eps[:, 0:1], scale=1.0 / M_INNER).then_inc(rooted, 1)

        @block.vector
        def _(dve):
            nc.vector.memset(eps[:], NORM_EPS).then_inc(eps_set, 1)
            dve.wait_ge(rooted, 1)
            nc.vector.reciprocal(token_scale[:], sd[:])


def mamba_stage(nc, g, persistent, d):
    token_scale = persistent.sb("token_scale", [P, TT])
    spread_dram = nc.dram_tensor("spread", (M_BLOCKS, NC, 2, 2, TT * M_CHUNK), F32, kind="Internal").ap()
    with ExitStack() as ctx:
        m = Scope(nc, ctx, "mam")
        s = Shared()
        s.gram = m.sb("gc", [P, TT, M_CHUNK])
        s.causal = m.sb("causal", [P, M_CHUNK])
        s.w_diag = m.sb("w_diag", [P, 2, TT, P])
        s.square_sum = m.sb("square_sum", [P, S])
        s.dt, s.cum, s.decay = (m.sb(n, [P, TT, M_HEADS]) for n in ("dt", "cum", "decay"))
        mamba_prepare_block(nc, g, s, d["mam_shared_w"], d["mam_shared_par"], d["mam_dt"], spread_dram)
        hidden = m.sb("hidden", [P, M_BLOCKS, S])
        mamba_heads_block(nc, g, s, hidden, d["mam_gate"], d["mam_hidden"], d["mam_par"], spread_dram)
        mamba_norm_block(nc, g, s, token_scale)
        project_out_block(nc, g, "mam_out", hidden, M_BLOCKS, d["mam_out"])
    return token_scale


KEY_HEADS, VALUE_HEADS, DK, DC = 16, 32, 128, 64
REP = VALUE_HEADS // KEY_HEADS
CHUNKS = S // DC
TC = P // DC
LEVELS = 6
DELTA_EPS = 1e-6
MIN_NORM = 1e-12


def delta_prepare_block(nc, g, s, w_dram, par_dram, rows_dram, exp_dram):
    with ExitStack() as ctx:
        m = Scope(nc, ctx, "dprep")
        V = VALUE_HEADS
        w = m.sb("w", [P, KC, 2 * V])
        par = m.sb("par", [V, 2])
        b_ps, a_ps = m.ps("b_ps", [V, S]), m.ps("a_ps", [V, S])
        turned_ps = m.ps("turned_ps", [P, 4, TT, V])
        beta, x, neg, soft, keep, gate, cum, eg, diff, rest, beg = (
            m.sb(n, [V, S]) for n in ("beta", "x", "neg", "soft", "keep", "gate", "cum", "eg", "diff", "rest", "beg"))
        rate = m.sb("rate", [V, 1])
        rows = m.sb("rows", [V, 2, TC, TT, DC])
        w_in, par_in, products, a_step, v_step, kept, turned, stored = (
            m.sem(n) for n in ("w_in", "par_in", "products", "a_step", "v_step", "kept", "turned", "stored"))
        block = ctx.enter_context(nc.Block())

        @block.sync
        def _(sp):
            sp.dma_start(w[:], w_dram).then_inc(w_in, 16)
            sp.dma_start(par[:], par_dram).then_inc(par_in, 16)
            sp.wait_ge(a_step, 10)
            for kind in range(2):
                for hd in range(REP):
                    sp.dma_start(rows_dram[:, :, hd, kind, :], rows[hd:V:REP, kind].rearrange("h c t l -> h c (t l)")
                                 ).then_inc(stored, 16)
            sp.dma_start(exp_dram, eg[:]).then_inc(stored, 16)
            sp.wait_ge(stored, 80)

        @block.tensor
        def _(pe):
            pe.wait_ge(w_in, 16)
            for n, ps in enumerate((a_ps, b_ps)):
                for h in range(NH2):
                    for c in range(KC):
                        last = nc.tensor.matmul(ps[:, half(h)], w[:, c, n * V:(n + 1) * V], g.xnT[:, c, half(h)],
                                                start=(c == 0), stop=(c == KC - 1))
                last.then_inc(products, 1)
            pe.wait_ge(v_step, 5)
            pe.wait_ge(a_step, 10)
            for n, src in enumerate((beta, cum, beg, rest)):
                for t in range(TT):
                    last = nc.tensor.transpose(turned_ps[:, n, t, :], src[:, tile(t)], g.ident[0:V, 0:V])
            last.then_inc(turned, 1)

        @block.scalar
        def _(act):
            act.wait_ge(par_in, 16)
            act.wait_ge(products, 1)
            nc.scalar.activation(x[:], a_ps[:], ACT.Identity, bias=par[:, 0:1]).then_inc(a_step, 1)
            act.wait_ge(v_step, 1)
            nc.scalar.activation(soft[:], neg[:], ACT.Exp).then_inc(a_step, 1)
            nc.scalar.activation(rate[:], par[:, 1:2], ACT.Exp).then_inc(a_step, 1)
            act.wait_ge(a_step, 3)
            nc.scalar.activation(soft[:], soft[:], ACT.Ln, bias=1.0).then_inc(a_step, 1)
            act.wait_ge(v_step, 3)
            nc.scalar.activation(eg[:], cum[:], ACT.Exp).then_inc(a_step, 1)
            cum_v, beta_v = (r[:].rearrange("h (t c l) -> h c t l", t=TT, c=TC) for r in (cum, beta))
            for c in range(TC):
                nc.scalar.activation(rows[:, 0, c], cum_v[:, c], ACT.Copy).then_inc(a_step, 1)
            act.wait_ge(v_step, 4)
            nc.scalar.activation(rest[:], diff[:], ACT.Exp).then_inc(a_step, 1)
            act.wait_ge(products, 2)
            nc.scalar.activation(beta[:], b_ps[:], ACT.Sigmoid).then_inc(kept, 1)
            act.wait_ge(kept, 5)
            for c in range(TC):
                nc.scalar.activation(rows[:, 1, c], beta_v[:, c], ACT.Copy).then_inc(a_step, 1)

        @block.vector
        def _(dve):
            nc.vector.memset(keep[:], 1.0).then_inc(kept, 1)
            dve.wait_ge(kept, 1)
            nc.vector.memset(keep[:, 0:S:DC], 0.0).then_inc(kept, 1)
            dve.wait_ge(a_step, 1)
            nc.vector.scalar_tensor_tensor(out=neg[:], in0=x[:], scalar=-1.0, in1=x[:], op0=ALU.mult, op1=ALU.min
                                           ).then_inc(v_step, 1)
            dve.wait_ge(a_step, 4)
            nc.vector.scalar_tensor_tensor(out=gate[:], in0=x[:], scalar=0.0, in1=soft[:], op0=ALU.max, op1=ALU.add
                                           ).then_inc(v_step, 1)
            nc.vector.tensor_scalar(rate[:], rate[:], -1.0, None, ALU.mult).then_inc(kept, 1)
            dve.wait_ge(v_step, 2)
            dve.wait_ge(kept, 3)
            nc.vector.tensor_scalar(gate[:], gate[:], rate[:, 0:1], None, ALU.mult).then_inc(kept, 1)
            dve.wait_ge(kept, 4)
            nc.vector.tensor_tensor_scan(cum[:], keep[:], gate[:], 0.0, ALU.mult, ALU.add).then_inc(v_step, 1)
            dve.wait_ge(v_step, 3)
            cum_v = cum[:].rearrange("h (c l) -> h c l", l=DC)
            end = cum_v[:, :, DC - 1:DC].to_broadcast((V, CHUNKS, DC))
            nc.vector.tensor_tensor(diff[:].rearrange("h (c l) -> h c l", l=DC), end, cum_v, ALU.subtract
                                    ).then_inc(v_step, 1)
            dve.wait_ge(kept, 5)
            dve.wait_ge(a_step, 5)
            nc.vector.tensor_tensor(beg[:], beta[:], eg[:], ALU.mult).then_inc(v_step, 1)
            dve.wait_ge(turned, 1)
            for n, dst in enumerate((s.beta, s.cum, s.beg, s.rest)):
                nc.vector.tensor_copy(dst[:], turned_ps[:, n])


def delta_heads_block(nc, g, s, w_dram, conv_dram, wo_dram, nw_dram, mask_dram, tri_dram, rows_dram, exp_dram):
    HT = TT // NH2
    CONV = NH2 * (TAPS - 1)
    PIECES = 6 * NH2 * KC
    with ExitStack() as ctx:
        m = Scope(nc, ctx, "delta")
        w = m.sb("w", [P, KC, 6, P])
        taps = m.sb("taps", [P, 4, TAPS])
        wo = m.sb("wo", [P, REP, D])
        nw, eps = m.sb("nw", [P, 1]), m.sb("eps", [P, 1])
        mask = m.sb("mask", [P, LEVELS + 1, P], I32)
        tri = m.sb("tri", [P, 2, DC])
        rows = m.sb("rows", [P, REP, 2, TT, DC])
        egf = m.sb("egf", [P, REP, S])
        feat = m.sb("feat", [P, 4, S])
        sz_new, sz = m.sb("sz_new", [P, REP, S]), m.sb("sz", [P, REP, S])
        norm, rnorm = m.sb("norm", [P, 2, TT]), m.sb("rnorm", [P, 2, TT])
        tok = m.sb("tok", [P, 4, TT, P])
        turned = m.sb("turned", [P, 2, S])
        acc = turned
        dec = m.sb("dec", [P, REP, TT, DC])
        decb = m.sb("decb", [P, REP, TT, DC])
        attn = m.sb("attn", [P, REP, TT, DC])
        negN, negM, U, T, prod = (m.sb(n, [P, REP, TT, P]) for n in ("negN", "negM", "U", "T", "prod"))
        kbe, kd, u = (m.sb(n, [P, REP, TT, P]) for n in ("kbe", "kd", "u"))
        square = kbe
        comb = (m.sb("comb", [P, TT, TC * P]), tok[:, 0:2].rearrange("p a t n -> p (a t n)").rearrange(
            "p (t x) -> p t x", t=TT))
        vnew = m.sb("vnew", [P, REP, P])
        state = m.sb("state", [P, REP, P])
        core = negM[:].rearrange("p h t n -> p (h t n)").rearrange("p (t h n) -> p t h n", t=TT, h=REP)
        fin = prod
        junk = m.sb("junk", [P, REP, P])
        ssq, rstd = m.sb("ssq", [P, TT, REP]), m.sb("rstd", [P, TT, REP])
        A, B, C, E = (m.ps(n, [P, S]) for n in ("A", "B", "C", "E"))
        AB, CE = (A, B), (C, E)
        names = ("w_in taps_in wo_in const_in rows_in egf_in blank projected turned_tok turned_feat gram "
                 "turned_m prod_done upd_done turned_u u_done kcd_done kcds_done ds_done mixed core_turned y_done "
                 "conv0 feat_ready sz_ready squared rooted feat_kept powered m_kept prod_kept t_kept u_kept kcd_kept "
                 "core_kept core_squared core_rooted convolved normed tok_ready dif_ready halves attn_ready t_first "
                 "u_updated vnew_ready state_ready recip core_scaled fin_ready added masked eye decb_ready kbe_ready "
                 "qe_ready sz_moved first_state released pool_released").split()
        q = {n: m.sem(n) for n in names}
        block = ctx.enter_context(nc.Block())

        def tiles(unit):
            return unit[:].rearrange("p (t n) -> p t n", t=TT)

        def compact(unit, h=0):
            return unit[:, half(h)].rearrange("p (t n) -> p t n", t=TT)

        def rows_of(c):
            return slice(c * DC, (c + 1) * DC)

        def head_cols(table, i, width=1, at=0):
            return table[:, :, bass.ds(i * REP + at, width)]

        def quarters(head):
            return comb[head][:].rearrange("p t (k n) -> p t k n", n=DC)

        @block.sync
        def _(sp):
            def load(i):
                sp.dma_start(w[:], w_dram[bass.ds(i, 1)].rearrange("a p c k n -> p (a c) k n")).then_inc(q["w_in"], 16)

            def load_taps(i):
                sp.dma_start(taps[:], conv_dram[bass.ds(i, 1)].rearrange("a p b k -> p (a b) k")).then_inc(q["taps_in"], 16)

            def load_rows(i):
                src = rows_dram[bass.ds(i, 1)].rearrange("a c h k x -> (a c) (h k x)")
                src = src.unsqueeze(1).to_broadcast((TC, DC, REP * 2 * TT * DC))
                sp.dma_start(rows[:].rearrange("p h k t l -> p (h k t l)"), src).then_inc(q["rows_in"], 16)

            def load_exp(i):
                src = exp_dram[bass.ds(i * REP, REP), :].rearrange("(a h) s -> a (h s)", a=1).to_broadcast((P, REP * S))
                sp.dma_start(egf[:].rearrange("p h s -> p (h s)"), src).then_inc(q["egf_in"], 16)

            def load_out(i):
                sp.dma_start(wo[:], wo_dram[bass.ds(i, 1)].rearrange("a p h n -> p (a h) n")).then_inc(q["wo_in"], 16)

            load(0)
            load_taps(0)
            load_rows(0)
            for dst, src in ((nw, nw_dram), (mask, mask_dram), (tri, tri_dram)):
                sp.dma_start(dst[:], src).then_inc(q["const_in"], 16)
            load_exp(0)
            load_out(0)
            with sp.Fori(1, KEY_HEADS) as i:
                sp.wait_ge(q["projected"], i * 6)
                load(i)
                sp.wait_ge(q["convolved"], i * (4 * CONV))
                load_taps(i)
                sp.wait_ge(q["decb_ready"], i * 4)
                load_rows(i)
                sp.wait_ge(q["state_ready"], i * (2 * CHUNKS))
                load_exp(i)
                sp.wait_ge(q["y_done"], i * 2)
                load_out(i)

        @block.tensor
        def _(pe):
            pe.wait_ge(q["blank"], 5)
            pe.sem_inc(q["fin_ready"], 4)

            def project(i, k):
                n, h, c = k // (NH2 * KC), k // KC % NH2, k % KC
                if k == 0:
                    pe.wait_ge(q["w_in"], i * 16 + 16)
                elif n >= 2 and k % (NH2 * KC) == 0:
                    pe.wait_ge(q["convolved"], i * (4 * CONV) + CONV * (n - 1))
                last = nc.tensor.matmul(AB[n % 2][:, half(h)], w[:, c, n, :], g.xnT[:, c, half(h)],
                                        start=(c == 0), stop=(c == KC - 1))
                if k % (NH2 * KC) == NH2 * KC - 1:
                    last.then_inc(q["projected"], 1)

            def turn(unit, src, done):
                for t in range(TT):
                    last = nc.tensor.transpose(unit[:, tile(t)], src[:, t, :], g.ident[:])
                last.then_inc(done, 1)

            def chunkwise(out, weights, moving, done):
                for t in range(TT):
                    for c in range(TC):
                        r = rows_of(c)
                        last = nc.tensor.matmul(out[r, t, :], weights[:, t, r], moving[:, t, r], start=True, stop=True)
                last.then_inc(done, 1)

            def feat_v(n):
                return feat[:, n, :].rearrange("p (t n) -> p t n", t=TT)

            def turn_qk(i, n):
                pe.wait_ge(q["feat_ready"], i * 4 + (n + 1))
                turn(CE[n], feat_v(n), q["turned_tok"])

            def turn_output(i, h, hd):
                unit = E[:, half(1)] if h == 0 else B[:, half(hd)]
                pe.wait_ge(q["core_scaled"], i * 2 + (h + 1))
                if h == 0 and hd:
                    pe.wait_ge(q["fin_ready"], i * 4 + 5)
                for t in range(HT):
                    last = nc.tensor.transpose(unit[:, tile(t)], core[:, h * HT + t, hd, :], g.ident[:])
                last.then_inc(q["core_turned"], 1)

            def output(i, h):
                pe.wait_ge(q["fin_ready"], i * 4 + (2 * h + 6))
                pe.wait_ge(q["wo_in"], i * 16 + 16)
                for c in range(KC):
                    for hd in range(REP):
                        last = nc.tensor.matmul(AB[h][:, half(c)], wo[:, hd, tile(c)],
                                                fin[:, hd].rearrange("p t n -> p (t n)")[:, half(h)],
                                                start=(hd == 0), stop=(hd == REP - 1))
                last.then_inc(q["y_done"], 1)

            def head(i, more):
                pe.wait_ge(q["feat_ready"], i * 4 + 4)
                pe.wait_ge(q["sz_ready"], i * 2 + 2)
                pe.wait_ge(q["added"], i * 2 + 1)
                turn(A, feat_v(2), q["turned_tok"])
                for n in range(2):
                    pe.wait_ge(q["tok_ready"], i * 4 + (n + 1))
                    turn(CE[n], tok[:, n], q["turned_feat"])
                pe.wait_ge(q["added"], i * 2 + 2)
                turn(B, feat_v(3), q["turned_tok"])
                pe.wait_ge(q["feat_kept"], i * 2 + 2)
                pe.wait_ge(q["tok_ready"], i * 4 + 3)
                for t in range(TT):
                    last = nc.tensor.matmul(A[:, tile(t)], turned[:, 1, tile(t)], turned[:, 1, tile(t)],
                                            start=True, stop=True)
                last.then_inc(q["gram"], 1)
                pe.wait_ge(q["tok_ready"], i * 4 + 4)
                for ch in range(CHUNKS):
                    own = slice(ch * DC, (ch + 1) * DC)
                    last = nc.tensor.matmul(compact(B)[rows_of(ch % TC), ch // TC, :], turned[:, 1, own],
                                            turned[:, 0, own], start=True, stop=True)
                last.then_inc(q["gram"], 1)
                for hd in range(REP):
                    pe.wait_ge(q["halves"], i * 4 + 2 * (hd + 1))
                    turn(CE[hd], negN[:, hd], q["turned_m"])
                for lv in range(LEVELS - 1):
                    for hd in range(REP):
                        if lv:
                            if lv == 1 and hd == 0:
                                pe.wait_ge(q["attn_ready"], i * 2 + 2)
                            pe.wait_ge(q["u_updated"], i * (2 * LEVELS) + (2 * lv + hd + 1))
                            turn(AB[hd], U[:, hd], q["turned_u"])
                        pe.wait_ge(q["u_updated"], i * (2 * LEVELS) + (2 * lv + hd + 1))
                        if lv == 0:
                            pe.wait_ge(q["m_kept"], i * 2 + (hd + 1))
                        chunkwise(compact(CE[hd]), negM[:, hd], U[:, hd], q["prod_done"])
                    for hd in range(REP):
                        pe.wait_ge(q["prod_kept"], i * (2 * LEVELS - 2) + (2 * lv + hd + 1))
                        if lv == 0:
                            pe.wait_ge(q["t_first"], i * 2 + (hd + 1))
                        if lv:
                            pe.wait_ge(q["t_kept"], i * (2 * LEVELS - 4) + (2 * lv + hd - 1))
                        chunkwise(compact(CE[hd], 1), T[:, hd], prod[:, hd], q["upd_done"])
                for hd in range(REP):
                    pe.wait_ge(q["u_updated"], i * (2 * LEVELS) + (2 * LEVELS - 1 + hd))
                    pe.wait_ge(q["kbe_ready"], i * 4 + 4)
                    for t in range(TT):
                        last = nc.tensor.matmul(CE[hd][:, tile(t)], kbe[:, hd, t, :], U[:, hd, t, :],
                                                start=True, stop=True)
                    last.then_inc(q["kcd_done"], 1)
                    for t in range(TT):
                        last = nc.tensor.matmul(AB[hd][:, tile(t)], U[:, hd, t, :], tok[:, 2 + hd, t, :],
                                                start=True, stop=True)
                    last.then_inc(q["u_done"], 1)
                if more:
                    pe.wait_ge(q["u_kept"], i * 2 + 1)
                    project(i + 1, 0)
                pe.wait_ge(q["u_kept"], i * 2 + 2)
                pe.wait_ge(q["kcd_kept"], i * 2 + 2)
                pe.wait_ge(q["qe_ready"], i * 2 + 2)
                pe.wait_ge(q["first_state"], i + 1)
                for n in range(CHUNKS):
                    c, t = n % TC, n // TC
                    r, other = rows_of(c), rows_of(1 - c)
                    if n:
                        pe.wait_ge(q["state_ready"], i * (2 * CHUNKS) + 2 * n)
                    if n >= TC:
                        pe.wait_ge(q["core_kept"], i * CHUNKS + (n - 1))
                    for hd in range(REP):
                        last = nc.tensor.matmul(C[:, c * HALF + hd * P:c * HALF + (hd + 1) * P],
                                                comb[hd][:, t, c * P:(c + 1) * P], state[:, hd, :],
                                                start=(hd == 0), stop=True, skip_group_check=True)
                    last.then_inc(q["kcds_done"], 1)
                    if more and n:
                        project(i + 1, 2 * n if n < CHUNKS // 2 else n + CHUNKS // 2)
                    pe.wait_ge(q["vnew_ready"], i * CHUNKS + (n + 1))
                    for hd in range(REP):
                        last = nc.tensor.matmul(E[:, hd * P:(hd + 1) * P], kd[r, hd, t, :], vnew[r, hd, :],
                                                start=True, stop=True)
                    last.then_inc(q["ds_done"], 1)
                    for hd in range(REP):
                        last = nc.tensor.matmul(C[other, c * HALF + hd * P:c * HALF + (hd + 1) * P],
                                                attn[r, hd, t, :], vnew[r, hd, :], start=False, stop=True,
                                                skip_group_check=True)
                    last.then_inc(q["mixed"], 1)
                    if more and n < CHUNKS // 2:
                        project(i + 1, 2 * n + 1)
                    if n == 14:
                        turn_output(i, 0, 0)
                turn_output(i, 0, 1)
                if more:
                    pe.wait_ge(q["core_kept"], i * CHUNKS + CHUNKS)
                    turn_qk(i + 1, 0)
                    pe.wait_ge(q["sz_ready"], i * 2 + 3)
                output(i, 0)
                if more:
                    pe.wait_ge(q["sz_ready"], i * 2 + 4)
                for hd in range(REP):
                    turn_output(i, 1, hd)
                if more:
                    pe.wait_ge(q["state_ready"], i * (2 * CHUNKS) + 2 * CHUNKS)
                    turn_qk(i + 1, 1)
                output(i, 1)

            for k in range(PIECES):
                project(0, k)
            for n in range(2):
                turn_qk(0, n)
            with pe.Fori(0, KEY_HEADS - 1) as i:
                head(i, True)
            head(KEY_HEADS - 1, False)

        @block.scalar
        def _(act):
            act.wait_ge(q["const_in"], 48)
            act.wait_ge(q["blank"], 5)

            def first_tap(i, n):
                act.wait_ge(q["projected"], i * 6 + (n + 1))
                if n == 0:
                    act.wait_ge(q["taps_in"], i * 16 + 16)
                if n >= 2:
                    act.wait_ge(q["feat_ready"], i * 4 + (n - 1))
                nc.scalar.activation(acc[:, n % 2, :], AB[n % 2][:], ACT.Copy, scale=taps[:, n, TAPS - 1:TAPS]
                                     ).then_inc(q["conv0"], 1)

            def silu(i, n):
                act.wait_ge(q["convolved"], i * (4 * CONV) + CONV * (n + 1))
                nc.scalar.activation(feat[:, n, :], acc[:, n % 2, :], ACT.Silu).then_inc(q["feat_ready"], 1)

            def gate(i, n):
                act.wait_ge(q["projected"], i * 6 + (5 + n))
                nc.scalar.activation(sz_new[:, n, :], AB[n][:], ACT.Silu).then_inc(q["sz_ready"], 1)

            def squares(i, n):
                act.wait_ge(q["turned_tok"], i * 4 + (n + 1))
                for t in range(TT):
                    nc.scalar.activation(square[:, n, t, :], tiles(CE[n])[:, t, :], ACT.Square,
                                         accum_out=norm[:, n, t:t + 1]).then_inc(q["squared"], 1)

            def norms(i):
                act.wait_ge(q["squared"], i * (2 * TT) + 2 * TT)
                nc.scalar.activation(norm[:], norm[:], ACT.Sqrt).then_inc(q["rooted"], 1)

            def decays(i):
                for hd in range(REP):
                    act.wait_ge(q["masked"], i * 2 + (hd + 1))
                    nc.scalar.activation(dec[:, hd], dec[:, hd], ACT.Exp).then_inc(q["powered"], 1)

            def root_output(i, h):
                own = slice(h * HT, (h + 1) * HT)
                act.wait_ge(q["core_squared"], i * (REP * TT) + REP * HT * (h + 1))
                nc.scalar.activation(rstd[:, own], ssq[:, own], ACT.Sqrt, bias=eps[:, 0:1], scale=1.0 / P
                                     ).then_inc(q["core_rooted"], 1)

            def head(i, more):
                for n in range(2):
                    act.wait_ge(q["turned_feat"], i * 2 + (n + 1))
                    nc.scalar.activation(turned[:, n, :], CE[n][:], ACT.Copy).then_inc(q["feat_kept"], 1)
                for hd in range(REP):
                    act.wait_ge(q["turned_m"], i * 2 + (hd + 1))
                    nc.scalar.activation(negM[:, hd], tiles(CE[hd]), ACT.Copy).then_inc(q["m_kept"], 1)
                for lv in range(LEVELS - 1):
                    for hd in range(REP):
                        if lv:
                            act.wait_ge(q["turned_u"], i * (2 * LEVELS - 4) + (2 * lv + hd - 1))
                            nc.scalar.activation(T[:, hd], tiles(AB[hd]), ACT.Copy).then_inc(q["t_kept"], 1)
                        act.wait_ge(q["prod_done"], i * (2 * LEVELS - 2) + (2 * lv + hd + 1))
                        for c in range(TC):
                            r = rows_of(c)
                            last = nc.scalar.activation(prod[r, hd, :, r], compact(CE[hd])[r], ACT.Copy)
                        last.then_inc(q["prod_kept"], 1)
                for hd in range(REP):
                    act.wait_ge(q["kcd_done"], i * 2 + (hd + 1))
                    nc.scalar.activation(quarters(hd)[:, :, 0:4:3, :], CE[hd][:].rearrange(
                        "p (t c n) -> p t c n", t=TT, c=TC), ACT.Copy).then_inc(q["kcd_kept"], 1)
                    act.wait_ge(q["u_done"], i * 2 + (hd + 1))
                    nc.scalar.activation(u[:, hd], tiles(AB[hd]), ACT.Copy).then_inc(q["u_kept"], 1)
                for n in range(CHUNKS):
                    c, t = n % TC, n // TC
                    if more:
                        if n in (2, 4, 6, 8):
                            first_tap(i + 1, (n - 2) // 2)
                        if n in (4, 6, 8, 10):
                            silu(i + 1, (n - 4) // 2)
                        if n == 12:
                            act.wait_ge(q["sz_moved"], i + 1)
                            gate(i + 1, 0)
                        if n == 14:
                            decays(i + 1)
                    act.wait_ge(q["mixed"], i * CHUNKS + (n + 1))
                    nc.scalar.activation(core[rows_of(c), t].rearrange("p h n -> p (h n)"),
                                         C[rows_of(1 - c), c * HALF:c * HALF + REP * P], ACT.Copy
                                         ).then_inc(q["core_kept"], 1)
                    if c == TC - 1:
                        act.wait_ge(q["core_kept"], i * CHUNKS + (n + 1))
                        for hd in range(REP):
                            if t:
                                act.wait_ge(q["core_squared"], i * (REP * TT) + (REP * (t - 1) + hd + 1))
                            nc.scalar.activation(junk[:, hd, :], core[:, t, hd, :], ACT.Square,
                                                 accum_out=ssq[:, t, hd:hd + 1]).then_inc(q["core_squared"], 1)
                    if n == 12:
                        root_output(i, 0)
                root_output(i, 1)
                if more:
                    gate(i + 1, 1)
                    for n in range(2):
                        squares(i + 1, n)
                    norms(i + 1)

            first_tap(0, 0)
            for n in range(4):
                if n < 3:
                    first_tap(0, n + 1)
                silu(0, n)
            for n in range(2):
                gate(0, n)
            for n in range(2):
                squares(0, n)
            norms(0)
            decays(0)
            with act.Fori(0, KEY_HEADS - 1) as i:
                head(i, True)
            head(KEY_HEADS - 1, False)

        @block.vector
        def _(dve):
            nc.vector.memset(eps[:], DELTA_EPS).then_inc(q["blank"], 1)
            nc.vector.memset(negN[:, 0], 0.0).then_inc(q["blank"], 1)
            nc.vector.memset(negN[:, 1], 0.0).then_inc(q["blank"], 1)
            nc.vector.memset(g.yT[:], 0.0).then_inc(q["blank"], 1)
            nc.vector.memset(prod[:], 0.0).then_inc(q["blank"], 1)
            dve.sem_inc(q["added"], 2)
            dve.wait_ge(q["const_in"], 48)
            dve.wait_ge(q["blank"], 5)

            def convolve(i, n, j):
                k, h = j // NH2 + 1, j % NH2
                at, to = max(k, h * HALF), (h + 1) * HALF
                if j == 0:
                    dve.wait_ge(q["conv0"], i * 4 + (n + 1))
                if j >= NH2:
                    dve.wait_ge(q["convolved"], i * (4 * CONV) + (CONV * n + j + 1 - NH2))
                nc.vector.scalar_tensor_tensor(out=acc[:, n % 2, at:to], in0=AB[n % 2][:, at - k:to - k],
                                               scalar=taps[:, n, TAPS - 1 - k:TAPS - k], in1=acc[:, n % 2, at:to],
                                               op0=ALU.mult, op1=ALU.add).then_inc(q["convolved"], 1)

            def differences(i, hd):
                dve.wait_ge(q["rows_in"], i * 16 + 16)
                nc.vector.tensor_tensor(dec[:, hd], rows[:, hd, 0], head_cols(s.cum, i, at=hd).to_broadcast(
                    (P, TT, DC)), ALU.subtract).then_inc(q["dif_ready"], 1)

            def norms(i):
                dve.wait_ge(q["rooted"], i + 1)
                nc.vector.tensor_scalar(norm[:], norm[:], MIN_NORM, None, ALU.max).then_inc(q["normed"], 1)
                dve.wait_ge(q["normed"], i * 3 + 1)
                nc.vector.reciprocal(rnorm[:], norm[:]).then_inc(q["normed"], 1)
                dve.wait_ge(q["normed"], i * 3 + 2)
                nc.vector.tensor_scalar(rnorm[:, 0], rnorm[:, 0], float(DK) ** -0.5, None, ALU.mult
                                        ).then_inc(q["normed"], 1)

            def scale_output(i, h):
                own = slice(h * HT, (h + 1) * HT)
                dve.wait_ge(q["core_rooted"], i * 2 + (h + 1))
                nc.vector.reciprocal(rstd[:, own], rstd[:, own]).then_inc(q["recip"], 1)
                dve.wait_ge(q["recip"], i * 2 + (h + 1))
                part = core[:, own].rearrange("p t h n -> p (t h) n")
                factor = rstd[:, own].rearrange("p t h -> p (t h)").unsqueeze(2).to_broadcast((P, REP * HT, P))
                nc.vector.tensor_tensor(part, part, factor, ALU.mult).then_inc(q["core_scaled"], 1)

            def gate_output(i, h, hd):
                dve.wait_ge(q["core_turned"], i * 4 + (2 * h + hd + 1))
                if h == 0 and hd == 0:
                    dve.wait_ge(q["sz_moved"], i + 1)
                unit = E[:, half(1)] if h == 0 else B[:, half(hd)]
                nc.vector.scalar_tensor_tensor(out=fin[:, hd].rearrange("p t n -> p (t n)")[:, half(h)], in0=unit,
                                               scalar=nw[:, 0:1], in1=sz[:, hd, half(h)], op0=ALU.mult,
                                               op1=ALU.mult).then_inc(q["fin_ready"], 1)

            def add_output(i, h):
                dve.wait_ge(q["y_done"], i * 2 + (h + 1))
                nc.vector.tensor_tensor(g.yT[:, :, half(h)], g.yT[:, :, half(h)],
                                        AB[h][:].rearrange("p (c n) -> p c n", c=KC), ALU.add).then_inc(q["added"], 1)

            def normalise(i):
                dve.wait_ge(q["normed"], i * 3 + 3)
                for n in range(2):
                    dve.wait_ge(q["turned_tok"], i * 4 + (n + 1))
                    nc.vector.tensor_tensor(tok[:, n], tiles(CE[n]), rnorm[:, n].unsqueeze(2).to_broadcast((P, TT, P)),
                                            ALU.mult).then_inc(q["tok_ready"], 1)

            def head(i, more):
                for n in range(REP):
                    dve.wait_ge(q["turned_tok"], i * 4 + (n + 3))
                    nc.vector.tensor_tensor(tok[:, 2 + n], tiles(AB[n]), head_cols(s.beta, i, at=n).to_broadcast(
                        (P, TT, P)), ALU.mult).then_inc(q["tok_ready"], 1)
                dve.wait_ge(q["gram"], i * 2 + 1)
                for hd in range(REP):
                    dve.wait_ge(q["decb_ready"], i * 4 + 2 * (hd + 1))
                    for c in range(TC):
                        r = rows_of(c)
                        nc.vector.tensor_tensor(negN[r, hd, :, r], decb[r, hd], tiles(A)[r, :, r], ALU.mult
                                                ).then_inc(q["halves"], 1)

                def level(n):
                    return mask[:, n:n + 1, :].to_broadcast((P, TT, P))

                for hd in range(REP):
                    dve.wait_ge(q["eye"], i * 4 + 2 * (hd + 1))
                    dve.wait_ge(q["halves"], i * 4 + 2 * (hd + 1))
                    dve.sem_inc(q["released"], 1)
                    nc.vector.copy_predicated(U[:, hd], level(0), negN[:, hd]).then_inc(q["u_updated"], 1)
                for hd in range(REP):
                    dve.wait_ge(q["m_kept"], i * 2 + (hd + 1))
                    dve.sem_inc(q["released"], 1)
                    nc.vector.copy_predicated(T[:, hd], level(LEVELS), negM[:, hd]).then_inc(q["t_first"], 1)
                dve.wait_ge(q["gram"], i * 2 + 2)
                for hd in range(REP):
                    nc.vector.tensor_tensor(attn[:, hd], dec[:, hd], compact(B), ALU.mult).then_inc(q["attn_ready"], 1)
                for lv in range(LEVELS - 1):
                    for hd in range(REP):
                        dve.wait_ge(q["upd_done"], i * (2 * LEVELS - 2) + (2 * lv + hd + 1))
                        dve.sem_inc(q["released"], 1)
                        for c in range(TC):
                            r = rows_of(c)
                            last = nc.vector.copy_predicated(U[r, hd, :, r], mask[r, lv + 1:lv + 2, r].to_broadcast(
                                (DC, TT, DC)), compact(CE[hd], 1)[r])
                        last.then_inc(q["u_updated"], 1)
                nc.vector.memset(state[:], 0.0).then_inc(q["first_state"], 1)
                dve.wait_ge(q["u_kept"], i * 2 + 2)
                dve.wait_ge(q["egf_in"], i * 16 + 16)
                dve.wait_ge(q["first_state"], i + 1)
                for n in range(CHUNKS):
                    c, t = n % TC, n // TC
                    r = rows_of(c)
                    unit, step = (n - 2) // 2, (n % 2) * (CONV // 2)
                    dve.wait_ge(q["kcds_done"], i * CHUNKS + (n + 1))
                    nc.vector.tensor_tensor(vnew[r], u[r, :, t, :], C[r, c * HALF:c * HALF + REP * P].rearrange(
                        "p (h n) -> p h n", h=REP), ALU.subtract).then_inc(q["vnew_ready"], 1)
                    if more and 2 <= n < 10:
                        convolve(i + 1, unit, step)
                    if n == 15:
                        gate_output(i, 0, 0)
                    dve.wait_ge(q["ds_done"], i * CHUNKS + (n + 1))
                    for hd in range(REP):
                        end = (n + 1) * DC - 1
                        nc.vector.scalar_tensor_tensor(out=state[:, hd, :], in0=state[:, hd, :],
                                                       scalar=egf[:, hd, end:end + 1], in1=E[:, hd * P:(hd + 1) * P],
                                                       op0=ALU.mult, op1=ALU.add).then_inc(q["state_ready"], 1)
                    if more and 2 <= n < 10:
                        convolve(i + 1, unit, step + 1)
                        convolve(i + 1, unit, step + 2)
                    if more and n in (10, 11):
                        differences(i + 1, n - 10)
                    if n == 13:
                        scale_output(i, 0)
                    dve.wait_ge(q["state_ready"], i * (2 * CHUNKS) + (2 * n + 2))
                gate_output(i, 0, 1)
                scale_output(i, 1)
                for hd in range(REP):
                    gate_output(i, 1, hd)
                add_output(i, 0)
                if more:
                    norms(i + 1)
                    normalise(i + 1)
                add_output(i, 1)

            dve.wait_ge(q["taps_in"], 16)
            for n in range(4):
                for j in range(CONV):
                    convolve(0, n, j)
            for hd in range(REP):
                differences(0, hd)
            norms(0)
            normalise(0)
            with dve.Fori(0, KEY_HEADS - 1) as i:
                head(i, True)
            head(KEY_HEADS - 1, False)

        @block.gpsimd
        def _(pool):
            pool.wait_ge(q["const_in"], 48)

            def eyes():
                for hd in range(REP):
                    for dst in (T, U):
                        nc.gpsimd.tensor_copy(dst[:, hd], g.ident[:].unsqueeze(1).to_broadcast((P, TT, P))
                                              ).then_inc(q["eye"], 1)

            def decays(i):
                for hd in range(REP):
                    pool.wait_ge(q["dif_ready"], i * 2 + (hd + 1))
                    nc.gpsimd.tensor_tensor(dec[:, hd], dec[:, hd], tri[:, 0:1, :].to_broadcast((P, TT, DC)), ALU.add
                                            ).then_inc(q["masked"], 1)
                for hd in range(REP):
                    nc.gpsimd.tensor_tensor(decb[:, hd], rows[:, hd, 1], tri[:, 1:2, :].to_broadcast((P, TT, DC)),
                                            ALU.mult).then_inc(q["decb_ready"], 1)
                    pool.wait_ge(q["powered"], i * 2 + (hd + 1))
                    pool.wait_ge(q["decb_ready"], i * 4 + (2 * hd + 1))
                    nc.gpsimd.tensor_tensor(decb[:, hd], decb[:, hd], dec[:, hd], ALU.mult).then_inc(q["decb_ready"], 1)

            def head(i, more):
                pool.wait_ge(q["sz_ready"], i * 2 + 2)
                pool.wait_ge(q["fin_ready"], i * 4 + 4)
                pool.sem_inc(q["pool_released"], 1)
                nc.gpsimd.tensor_copy(sz[:], sz_new[:]).then_inc(q["sz_moved"], 1)
                pool.wait_ge(q["tok_ready"], i * 4 + 2)
                for hd in range(REP):
                    for dst, table in ((kbe, s.beg), (kd, s.rest)):
                        nc.gpsimd.tensor_tensor(dst[:, hd], tok[:, 1], head_cols(table, i, at=hd).to_broadcast(
                            (P, TT, P)), ALU.mult).then_inc(q["kbe_ready"], 1)
                pool.wait_ge(q["feat_kept"], i * 2 + 2)
                pool.wait_ge(q["kbe_ready"], i * 4 + 4)
                pool.wait_ge(q["egf_in"], i * 16 + 16)
                for hd in range(REP):
                    nc.gpsimd.tensor_tensor(quarters(hd)[:, :, 1:3, :], *(x.rearrange("p (t c n) -> p t c n", t=TT, c=TC)
                                            for x in (turned[:, 0, :], egf[:, hd, :])), ALU.mult
                                            ).then_inc(q["qe_ready"], 1)
                if more:
                    pool.wait_ge(q["kcd_done"], i * 2 + 2)
                    pool.wait_ge(q["u_done"], i * 2 + 2)
                    pool.sem_inc(q["pool_released"], 1)
                    eyes()
                    decays(i + 1)

            eyes()
            decays(0)
            with pool.Fori(0, KEY_HEADS - 1) as i:
                head(i, True)
            head(KEY_HEADS - 1, False)


def delta_stage(nc, g, d):
    rows_dram = nc.dram_tensor("delta_gate_rows", (KEY_HEADS, TC, REP, 2, TT * DC), F32, kind="Internal").ap()
    exp_dram = nc.dram_tensor("delta_gate_exp", (VALUE_HEADS, S), F32, kind="Internal").ap()
    with ExitStack() as ctx:
        m = Scope(nc, ctx, "del")
        s = Shared()
        s.beta, s.cum, s.beg, s.rest = (m.sb(n, [P, TT, VALUE_HEADS]) for n in ("beta", "cum", "beg", "rest"))
        delta_prepare_block(nc, g, s, d["del_ba"], d["del_par"], rows_dram, exp_dram)
        delta_heads_block(nc, g, s, d["del_w"], d["del_taps"], d["del_out"], d["del_nw"], d["del_mask"],
                          d["del_tri"], rows_dram, exp_dram)


STAGES = range(8)
L0_HEAD = 16
MLP, INTER_T, HID = 2048, 768, 128
NEXP = EXP + 1


def program(nc, d, out):
    with ExitStack() as ctx:
        g = Shared()
        m = Scope(nc, ctx, "g")
        g.x = m.sb("x", [P, TT, D])
        g.xnT = m.sb("xnT", [P, KC, S])
        g.yT = m.sb("yT", [P, KC, S])
        g.ident = m.sb("ident", [P, P])
        g.ones = m.sb("ones", [P, P])
        g.zero = m.sb("zero", [P, HALF], BF16)
        start_block(nc, g, d["x"])
        stages = list(STAGES)
        residual_block(nc, g, "res_in", post=False)
        for n in stages:
            scale = None
            if n == 0:
                linear_attention_block(nc, g, "lin", d["l0_w"], d["l0_b"], L0_HEAD)
            if n == 1:
                gated_ffn_block(nc, g, "fp4", FP4, MLP // P // 4, 4, d["fp4_w"], d["fp4_s"])
            if n == 2:
                scale = mamba_stage(nc, g, m, d)
            if n == 3:
                gated_ffn_block(nc, g, "ter", TERNARY, INTER_T // P // 3, 3, d["ter_w"], d["ter_s"])
            if n == 4:
                latent_attention_stage(nc, g, d)
            if n == 5:
                linear_block(nc, g, "ffn2", d["l2_w"], d["l2_s"])
            if n == 6:
                delta_stage(nc, g, d)
            if n == 7:
                score_dram = nc.dram_tensor("scores", (NEXP, S), F32, kind="Internal").ap()
                router_block(nc, g, "route", d["route_w"], score_dram)
                gated_ffn_block(nc, g, "moe", EXPERTS, NEXP // 3, 3, d["moe_w"], score_dram)
            last = n == stages[-1]
            residual_block(nc, g, f"res{n}", pre=not last, token_scale=scale, out=out if last else None)


def kmajor(w):
    return np.ascontiguousarray(np.transpose(w.reshape(w.shape[0], P, KC), (1, 2, 0)))


def kflat(w):
    return np.ascontiguousarray(np.transpose(w.reshape(w.shape[0], -1, P), (2, 1, 0)))


def columns(b):
    return np.ascontiguousarray(b.reshape(-1, P).T)


def ffn_blocks(wg, wu, wd, sg=None, su=None):
    nb = wg.shape[0] // P
    out = np.zeros((nb, P, 6 * P + 2), np.float32)
    for b in range(nb):
        rows = slice(b * P, (b + 1) * P)
        out[b, :, 0:2 * P] = kmajor(wg[rows]).reshape(P, -1)
        out[b, :, 2 * P:4 * P] = kmajor(wu[rows]).reshape(P, -1)
        out[b, :, 4 * P:6 * P] = wd[:, rows].T
        if sg is not None:
            out[b, :, 6 * P], out[b, :, 6 * P + 1] = sg[rows], su[rows]
    return out


def lay_out(v):
    d = {"x": v["L0_attn_x"]}
    d["l0_w"] = np.stack([kmajor(v["L0_attn_Wq"]), kmajor(v["L0_attn_Wk"]), kmajor(v["L0_attn_Wv"]),
                          kflat(v["L0_attn_Wo"])], axis=1)
    d["l0_b"] = np.stack([columns(v[f"L0_attn_b{n}"]) for n in "qkvo"], axis=1)
    pairs = MLP // (2 * P)
    gate, up = (v[f"L0_ffn_{n}_W_packed"].reshape(pairs, P, 2, P).transpose(0, 3, 2, 1).reshape(pairs, P, 2 * P)
                for n in ("gate", "up"))
    down = v["L0_ffn_down_W_packed"].reshape(D, pairs, P).transpose(1, 2, 0)
    d["fp4_w"] = np.concatenate([gate, up, down], axis=2)
    gs, us = (v[f"L0_ffn_{n}_scales"].reshape(pairs, P, 2, 8).transpose(0, 3, 2, 1).reshape(pairs, 8, 2 * P)
              for n in ("gate", "up"))
    ds = v["L0_ffn_down_scales"].reshape(D, pairs, 8).transpose(1, 2, 0)
    d["fp4_s"] = np.concatenate([gs, us, ds], axis=2)
    pad = INTER_T - v["L1_ffn_gate_w"].shape[0]
    rows = ((0, pad), (0, 0))
    d["ter_w"] = ffn_blocks(np.pad(v["L1_ffn_gate_w"], rows), np.pad(v["L1_ffn_up_w"], rows),
                            np.pad(v["L1_ffn_down_w"], ((0, 0), (0, pad))),
                            np.pad(v["L1_ffn_gate_s"], (0, pad)), np.pad(v["L1_ffn_up_s"], (0, pad)))
    d["ter_s"] = columns(v["L1_ffn_down_s"])
    d["l2_w"] = kmajor(v["L2_ffn_weight"])
    d["l2_s"] = np.stack([columns(v["L2_ffn_scale_weight"]), columns(v["L2_ffn_bias"])], axis=1)
    d["route_w"] = kmajor(v["L3_ffn_gate_w"])
    moe = [ffn_blocks(v["L3_ffn_w1"][e], v["L3_ffn_w3"][e], v["L3_ffn_w2"][e]) for e in range(EXP)]
    moe.append(ffn_blocks(v["L3_ffn_ws1"], v["L3_ffn_ws3"], v["L3_ffn_ws2"]))
    d["moe_w"] = np.concatenate(moe, axis=0)
    w_in, cw, cb = v["L1_attn_W_in"], v["L1_attn_conv_w"], v["L1_attn_conv_b"]
    d["mam_gate"] = np.stack([kmajor(w_in[b * P:(b + 1) * P]) for b in range(M_BLOCKS)])
    d["mam_hidden"] = np.stack([kmajor(w_in[M_INNER + b * P:M_INNER + (b + 1) * P]) for b in range(M_BLOCKS)])
    d["mam_shared_w"] = kmajor(w_in[2 * M_INNER:])
    blank = np.zeros(2 * M_N, np.float32)
    par = np.concatenate([cw, cb[:, None], np.concatenate([np.repeat(v["L1_attn_D"], M_P), blank])[:, None],
                          np.concatenate([v["L1_attn_norm_w"], blank])[:, None]], axis=1)
    par = par.reshape(-1, P, PAR).transpose(1, 0, 2)
    d["mam_par"], d["mam_shared_par"] = par[:, :M_BLOCKS], par[:, M_BLOCKS:]
    d["mam_dt"] = np.stack([v["L1_attn_dt_bias"], v["L1_attn_A_log"]], axis=1)
    d["mam_out"] = v["L1_attn_W_out"].T.reshape(M_BLOCKS, P, D)
    qkv, cw, wz = v["L3_attn_W_qkv"], v["L3_attn_conv_w"], v["L3_attn_W_z"]
    nk = KEY_HEADS
    w, taps = [], []
    for h in range(nk):
        blocks = [h, nk + h, 2 * nk + 2 * h, 2 * nk + 2 * h + 1]
        parts = [kmajor(qkv[b * P:(b + 1) * P]) for b in blocks]
        parts += [kmajor(wz[b * P:(b + 1) * P]) for b in (2 * h, 2 * h + 1)]
        w.append(np.stack(parts, axis=2))
        taps.append(np.stack([cw[b * P:(b + 1) * P] for b in blocks], axis=1))
    d["del_w"], d["del_taps"] = np.stack(w), np.stack(taps)
    d["del_ba"] = np.concatenate([kmajor(v["L3_attn_W_a"]), kmajor(v["L3_attn_W_b"])], axis=2)
    d["del_par"] = np.stack([v["L3_attn_dt_bias"], v["L3_attn_A_log"]], axis=1)
    d["del_out"] = v["L3_attn_W_out"].T.reshape(nk, REP, P, D).transpose(0, 2, 1, 3)
    d["del_nw"] = v["L3_attn_norm_w"][:, None]
    j, i = np.arange(P)[:, None], np.arange(P)[None, :]
    levels = [(j // (2 * b) == i // (2 * b)) & ((j // b) % 2 == 0) & ((i // b) % 2 == 1) for b in 2 ** np.arange(LEVELS)]
    levels.append(levels[0].T)
    d["del_mask"] = np.stack(levels, axis=1).astype(np.int32)
    j, i = (np.arange(P) % DC)[:, None], np.arange(DC)[None, :]
    d["del_tri"] = np.stack([np.where(j > i, NEG, 0.0), np.where(j < i, -1.0, 0.0)], axis=1).astype(np.float32)
    w = np.zeros((D, P), np.float32)
    w[:, 0:QL], w[:, KV0:KV0 + KVL] = v["L2_attn_Wq_down"], v["L2_attn_Wkv_down"]
    d["lat_w"] = w.reshape(P, KC, P)
    nw = np.zeros((P, 2), np.float32)
    nw[0:QL, 0], nw[KV0:P, 0] = v["L2_attn_q_norm_w"], v["L2_attn_kv_norm_w"]
    nw[0:KVL, 1], nw[KVL:P, 1] = v["L2_attn_kv_norm_w"], v["L2_attn_kv_norm_w"]
    d["lat_nw"] = nw
    q_up, k_up, v_up = (v[f"L2_attn_W{n}_up"].T.reshape(HEADS // 2, 2, HEAD, -1).transpose(0, 2, 1, 3) for n in "qkv")
    d["mla_wqk"] = np.concatenate([q_up, k_up], axis=3)
    wo = v["L2_attn_Wout"].reshape(HEADS // 2, 2, HEAD, D).transpose(0, 2, 1, 3)
    d["mla_wvo"] = np.concatenate([v_up.reshape(-1, HEAD, 2 * KVL), wo.reshape(-1, HEAD, 2 * D)], axis=2)
    order = np.concatenate([np.arange(0, ROPE, 2), np.arange(1, ROPE, 2)])
    rope = [v[f"L2_attn_W{n}_rope"].reshape(P, KC, HEADS, ROPE)[:, :, :, order] for n in "qk"]
    rope = np.stack(rope, axis=2).reshape(P, KC, 2, HEADS // 2, 2 * ROPE)
    d["mla_rope"] = rope.transpose(3, 0, 1, 2, 4)
    freq = (1.0 / np.float32(10000.0) ** (np.arange(0, ROPE, 2, dtype=np.float32) / np.float32(ROPE))).astype(np.float32)
    angle = np.outer(freq, np.arange(S, dtype=np.float32)).astype(np.float32)
    cos, sin = np.cos(angle), np.sin(angle)
    d["mla_table"] = np.stack([np.concatenate([cos] * 4), np.concatenate([sin, -sin] * 2)], axis=1)
    return {k: np.ascontiguousarray(a) for k, a in d.items()}


def kernel(**inputs):
    import concourse.bacc as bacc
    from concourse.bass_utils import run_bass_kernel_spmd

    arrays = lay_out({k: np.asarray(a) for k, a in inputs.items()})
    nc = bacc.Bacc("TRN2", target_bir_lowering=False, num_devices=1)
    d = {n: nc.dram_tensor(f"in_{n}", a.shape, mybir.dt.from_np(a.dtype), kind="ExternalInput").ap()
         for n, a in arrays.items()}
    out = nc.dram_tensor("out", arrays["x"].shape, F32, kind="ExternalOutput").ap()
    program(nc, d, out)
    r = run_bass_kernel_spmd(nc, [{f"in_{n}": a for n, a in arrays.items()}], core_ids=[0])
    return r.results[0]["out"]
```
